# Optimizing a Trainium2 kernel written in Bass

```python
import numpy as np
import jax
import jax.numpy as jnp

def _softmax(x, axis=-1):
    return jax.nn.softmax(x, axis=axis)

def _gelu(x):
    return jax.nn.gelu(x, approximate=True)

def _silu(x):
    return jax.nn.silu(x)

def _sigmoid(x):
    return jax.nn.sigmoid(x)

def _layernorm(x, axis=-1, eps=1e-05):
    m = jnp.mean(x, axis=axis, keepdims=True)
    v = jnp.var(x, axis=axis, keepdims=True)
    return (x - m) / jnp.sqrt(v + eps)

def _scatter_add(tgt, idx, src, axis=0):
    return tgt.at[idx].add(src)

def _segment_sum(src, seg, n):
    return jax.ops.segment_sum(src, seg, n)
kernel_name = 'mk_seq_postln_d2_jaxref_r4_bdb4ed'

def setup_inputs(seed: int=0):
    np.random.seed(seed)
    _w = jnp.asarray

    def _L0_attn_setup():
        import jax, jax.numpy as jnp
        import numpy as np
        HEADS = 16
        KV_HEADS = 4
        DIM_HEAD = 64
        SCALE = DIM_HEAD ** (-0.5)

        def _rotate_half(x):
            x1, x2 = jnp.split(x, 2, axis=-1)
            return jnp.concatenate((-x2, x1), axis=-1)

        def _rope_freqs(n, d):
            inv_freq = 1.0 / 10000.0 ** (jnp.arange(0, d, 2, dtype=jnp.float32) / d)
            freqs = jnp.einsum('i,j->ij', jnp.arange(n, dtype=jnp.float32), inv_freq)
            return jnp.concatenate((freqs, freqs), axis=-1)
        key = jax.random.key(seed)
        ks = jax.random.split(key, 4)
        b, n, dim = (2, 512, 256)
        inner = HEADS * DIM_HEAD
        s = dim ** (-0.5)
        return {'x': jax.random.normal(ks[0], (b, n, dim), jnp.float32), 'Wq': jax.random.normal(ks[1], (dim, inner), jnp.float32) * s, 'Wkv': jax.random.normal(ks[2], (dim, DIM_HEAD * KV_HEADS * 2), jnp.float32) * s, 'Wo': jax.random.normal(ks[3], (inner, dim), jnp.float32) * s, 'bo': jnp.zeros((dim,), jnp.float32)}
    _L0_attn_in = _L0_attn_setup()

    def _L0_ffn_setup():
        import jax, jax.numpy as jnp
        import numpy as np
        B, S, H, F, G = (8, 512, 256, 1024, 128)
        EPS = 1e-05

        def _dequant(q, scales, g):
            K, N = q.shape
            w = (q.astype(jnp.float32) - 128.0).reshape(K // g, g, N) * scales[:, None, :]
            return w.reshape(K, N)
        key = jax.random.key(seed)
        ks = jax.random.split(key, 8)
        x = jax.random.normal(ks[0], (B, S, H), dtype=jnp.float32)
        ln_gamma = jnp.ones((H,), jnp.float32)
        ln_beta = jnp.zeros((H,), jnp.float32)
        fc1_q = jax.random.randint(ks[1], (H, F), 0, 64, dtype=jnp.int32)
        fc2_q = jax.random.randint(ks[2], (F, H), 0, 64, dtype=jnp.int32)
        fc1_scales = jax.random.uniform(ks[3], (H // G, F), jnp.float32) * 0.02 + 0.001
        fc2_scales = jax.random.uniform(ks[4], (F // G, H), jnp.float32) * 0.02 + 0.001
        fc1_bias = jax.random.normal(ks[5], (F,), jnp.float32) * 0.02
        fc2_bias = jax.random.normal(ks[6], (H,), jnp.float32) * 0.02
        return {'x': x, 'ln_gamma': ln_gamma, 'ln_beta': ln_beta, 'fc1_q': fc1_q, 'fc1_scales': fc1_scales, 'fc1_bias': fc1_bias, 'fc2_q': fc2_q, 'fc2_scales': fc2_scales, 'fc2_bias': fc2_bias}
    _L0_ffn_in = _L0_ffn_setup()

    def _L1_attn_setup():
        import jax, jax.numpy as jnp
        import numpy as np
        B, S, DIM = (2, 2048, 256)
        NH, NKV, HD = (16, 4, 64)
        GROUPS = NH // NKV
        CHUNK = 128
        THETA = 10000.0

        def _slopes(h):
            return jnp.asarray([2.0 ** (-8.0 / h * (i + 1)) for i in range(h)], dtype=jnp.float32)

        def _rope_tables(s, d):
            inv = 1.0 / THETA ** (np.arange(0, d, 2, dtype=np.float64) / d)
            freqs = np.outer(np.arange(s, dtype=np.float64), inv)
            emb = np.concatenate([freqs, freqs], axis=-1)
            return (jnp.asarray(np.cos(emb), jnp.float32), jnp.asarray(np.sin(emb), jnp.float32))

        def _apply_rope(x, cos, sin):
            x1, x2 = jnp.split(x, 2, axis=-1)
            rot = jnp.concatenate([-x2, x1], axis=-1)
            return x * cos + rot * sin

        def _lightning_attn(q, k, v, slopes, chunk):
            b, h, s, d = q.shape
            nc = s // chunk
            t = jnp.arange(chunk, dtype=jnp.float32)
            sl = slopes[:, None, None]
            mask = jnp.where(t[:, None] >= t[None, :], jnp.exp(-sl * (t[:, None] - t[None, :])), 0.0)
            q_dec = jnp.exp(-slopes[:, None] * (t + 1.0))[..., None]
            k_dec = jnp.exp(-slopes[:, None] * (chunk - 1.0 - t))[..., None]
            blk_dec = jnp.exp(-slopes * chunk)[None, :, None, None]

            def to_chunks(x):
                return x.reshape(b, h, nc, chunk, d).transpose(2, 0, 1, 3, 4)
            qc, kc, vc = (to_chunks(q), to_chunks(k), to_chunks(v))

            def step(kv, inp):
                qi, ki, vi = inp
                scores = jnp.einsum('bhtd,bhsd->bhts', qi, ki) * mask
                o = jnp.einsum('bhts,bhsd->bhtd', scores, vi) + jnp.einsum('bhtd,bhde->bhte', qi * q_dec, kv)
                kv = blk_dec * kv + jnp.einsum('bhtd,bhte->bhde', ki * k_dec, vi)
                return (kv, o)
            kv0 = jnp.zeros((b, h, d, d), q.dtype)
            _, outs = jax.lax.scan(step, kv0, (qc, kc, vc))
            return outs.transpose(1, 2, 0, 3, 4).reshape(b, h, s, d)
        key = jax.random.key(seed)
        k0, k1, k2, k3, k4 = jax.random.split(key, 5)
        x = jax.random.normal(k0, (B, S, DIM), jnp.float32)
        Wq = jax.random.normal(k1, (NH * HD, DIM), jnp.float32) * 0.02
        Wk = jax.random.normal(k2, (NKV * HD, DIM), jnp.float32) * 0.02
        Wv = jax.random.normal(k3, (NKV * HD, DIM), jnp.float32) * 0.02
        Wo = jax.random.normal(k4, (DIM, NH * HD), jnp.float32) * 0.02
        return {'x': x, 'Wq': Wq, 'Wk': Wk, 'Wv': Wv, 'Wo': Wo}
    _L1_attn_in = _L1_attn_setup()

    def _L1_ffn_setup():
        import jax, jax.numpy as jnp
        import numpy as np
        import math
        D = 256
        H = 16
        E = 8
        TOPK = 2
        LAT = D // 2
        KPH = LAT // H
        HD = D // H

        def _forward(hs, q_w, q_b, k_w, k_b, v_w, v_b, o_w, o_b, router_w, router_b, w1, b1, w2, b2):
            B, S, _ = hs.shape
            Q = (hs @ q_w + q_b).reshape(B, S, H, HD).transpose(0, 2, 1, 3)
            K = (hs @ k_w + k_b).reshape(B, S, H, KPH).transpose(0, 2, 1, 3)
            V = (hs @ v_w + v_b).reshape(B, S, H, KPH).transpose(0, 2, 1, 3)
            scores = jnp.einsum('bhsk,bhtk->bhst', Q[..., :KPH], K) / math.sqrt(KPH)
            attn = jax.nn.softmax(scores, axis=-1)
            ao = jnp.einsum('bhst,bhtv->bhsv', attn, V)
            ao = ao.transpose(0, 2, 1, 3).reshape(B, S, H * KPH)
            ao = jnp.concatenate([ao, jnp.zeros((B, S, D - LAT), ao.dtype)], axis=-1)
            mla_out = ao @ o_w + o_b
            probs = jax.nn.softmax(mla_out @ router_w + router_b, axis=-1)
            topw, topi = jax.lax.top_k(probs, TOPK)
            topw = topw / (topw.sum(-1, keepdims=True) + 1e-08)
            combine = jnp.sum(jax.nn.one_hot(topi, E, dtype=probs.dtype) * topw[..., None], axis=-2)
            h1 = jnp.einsum('bsd,edf->ebsf', mla_out, w1) + b1[:, None, None, :]
            h1 = jax.nn.gelu(h1, approximate=False)
            h2 = jnp.einsum('ebsf,efd->ebsd', h1, w2) + b2[:, None, None, :]
            moe_out = jnp.einsum('bse,ebsd->bsd', combine, h2)
            return hs + 0.3 * moe_out
        key = jax.random.key(seed)
        ks = jax.random.split(key, 16)
        s = 0.02
        inp = {'hidden_states': jax.random.normal(ks[0], (2, 512, D), jnp.float32), 'q_w': jax.random.normal(ks[1], (D, D), jnp.float32) * s, 'q_b': jnp.zeros((D,), jnp.float32), 'k_w': jax.random.normal(ks[2], (D, LAT), jnp.float32) * s, 'k_b': jnp.zeros((LAT,), jnp.float32), 'v_w': jax.random.normal(ks[3], (D, LAT), jnp.float32) * s, 'v_b': jnp.zeros((LAT,), jnp.float32), 'o_w': jax.random.normal(ks[4], (D, D), jnp.float32) * s, 'o_b': jnp.zeros((D,), jnp.float32), 'router_w': jax.random.normal(ks[5], (D, E), jnp.float32) * s, 'router_b': jnp.zeros((E,), jnp.float32), 'w1': jax.random.normal(ks[6], (E, D, 2 * D), jnp.float32) * s, 'b1': jnp.zeros((E, 2 * D), jnp.float32), 'w2': jax.random.normal(ks[7], (E, 2 * D, D), jnp.float32) * s, 'b2': jnp.zeros((E, D), jnp.float32)}
        return inp
    _L1_ffn_in = _L1_ffn_setup()
    _d = {'L0_attn_x': _L0_attn_in['x'], 'L0_attn_Wq': _L0_attn_in['Wq'], 'L0_attn_Wkv': _L0_attn_in['Wkv'], 'L0_attn_Wo': _L0_attn_in['Wo'], 'L0_attn_bo': _L0_attn_in['bo'], 'L0_ffn_ln_gamma': _L0_ffn_in['ln_gamma'], 'L0_ffn_ln_beta': _L0_ffn_in['ln_beta'], 'L0_ffn_fc1_q': _L0_ffn_in['fc1_q'], 'L0_ffn_fc1_scales': _L0_ffn_in['fc1_scales'], 'L0_ffn_fc1_bias': _L0_ffn_in['fc1_bias'], 'L0_ffn_fc2_q': _L0_ffn_in['fc2_q'], 'L0_ffn_fc2_scales': _L0_ffn_in['fc2_scales'], 'L0_ffn_fc2_bias': _L0_ffn_in['fc2_bias'], 'L1_attn_Wq': _L1_attn_in['Wq'], 'L1_attn_Wk': _L1_attn_in['Wk'], 'L1_attn_Wv': _L1_attn_in['Wv'], 'L1_attn_Wo': _L1_attn_in['Wo'], 'L1_ffn_q_w': _L1_ffn_in['q_w'], 'L1_ffn_q_b': _L1_ffn_in['q_b'], 'L1_ffn_k_w': _L1_ffn_in['k_w'], 'L1_ffn_k_b': _L1_ffn_in['k_b'], 'L1_ffn_v_w': _L1_ffn_in['v_w'], 'L1_ffn_v_b': _L1_ffn_in['v_b'], 'L1_ffn_o_w': _L1_ffn_in['o_w'], 'L1_ffn_o_b': _L1_ffn_in['o_b'], 'L1_ffn_router_w': _L1_ffn_in['router_w'], 'L1_ffn_router_b': _L1_ffn_in['router_b'], 'L1_ffn_w1': _L1_ffn_in['w1'], 'L1_ffn_b1': _L1_ffn_in['b1'], 'L1_ffn_w2': _L1_ffn_in['w2'], 'L1_ffn_b2': _L1_ffn_in['b2']}
    _x0 = _d['L0_attn_x']
    _d['L0_attn_x'] = jax.random.normal(jax.random.fold_in(jax.random.key(seed), 1), (8, 512, 256), dtype=_x0.dtype)
    del _x0
    return _d

def reference(L0_attn_x, L0_attn_Wq, L0_attn_Wkv, L0_attn_Wo, L0_attn_bo, L0_ffn_ln_gamma, L0_ffn_ln_beta, L0_ffn_fc1_q, L0_ffn_fc1_scales, L0_ffn_fc1_bias, L0_ffn_fc2_q, L0_ffn_fc2_scales, L0_ffn_fc2_bias, L1_attn_Wq, L1_attn_Wk, L1_attn_Wv, L1_attn_Wo, L1_ffn_q_w, L1_ffn_q_b, L1_ffn_k_w, L1_ffn_k_b, L1_ffn_v_w, L1_ffn_v_b, L1_ffn_o_w, L1_ffn_o_b, L1_ffn_router_w, L1_ffn_router_b, L1_ffn_w1, L1_ffn_b1, L1_ffn_w2, L1_ffn_b2):

    def _L0_attn_ref(x, Wq, Wkv, Wo, bo):
        import jax, jax.numpy as jnp
        import numpy as np
        HEADS = 16
        KV_HEADS = 4
        DIM_HEAD = 64
        SCALE = DIM_HEAD ** (-0.5)

        def _rotate_half(x):
            x1, x2 = jnp.split(x, 2, axis=-1)
            return jnp.concatenate((-x2, x1), axis=-1)

        def _rope_freqs(n, d):
            inv_freq = 1.0 / 10000.0 ** (jnp.arange(0, d, 2, dtype=jnp.float32) / d)
            freqs = jnp.einsum('i,j->ij', jnp.arange(n, dtype=jnp.float32), inv_freq)
            return jnp.concatenate((freqs, freqs), axis=-1)
        b, n, dim = x.shape
        g = HEADS // KV_HEADS
        q = (x @ Wq).reshape(b, n, HEADS, DIM_HEAD).transpose(0, 2, 1, 3)
        kv = (x @ Wkv).reshape(b, n, 2 * KV_HEADS, DIM_HEAD)
        k = kv[:, :, :KV_HEADS].transpose(0, 2, 1, 3)
        v = kv[:, :, KV_HEADS:].transpose(0, 2, 1, 3)
        freqs = _rope_freqs(n, DIM_HEAD)
        cos, sin = (jnp.cos(freqs), jnp.sin(freqs))
        q = q * cos + _rotate_half(q) * sin
        k = k * cos + _rotate_half(k) * sin
        k = jnp.repeat(k, g, axis=1)
        v = jnp.repeat(v, g, axis=1)
        dots = jnp.einsum('bhid,bhjd->bhij', q, k) * SCALE
        attn = jax.nn.softmax(dots, axis=-1)
        out = jnp.einsum('bhij,bhjd->bhid', attn, v)
        out = out.transpose(0, 2, 1, 3).reshape(b, n, HEADS * DIM_HEAD)
        return out @ Wo + bo

    def _L0_ffn_ref(x, ln_gamma, ln_beta, fc1_q, fc1_scales, fc1_bias, fc2_q, fc2_scales, fc2_bias):
        import jax, jax.numpy as jnp
        import numpy as np
        B, S, H, F, G = (8, 512, 256, 1024, 128)
        EPS = 1e-05

        def _dequant(q, scales, g):
            K, N = q.shape
            w = (q.astype(jnp.float32) - 128.0).reshape(K // g, g, N) * scales[:, None, :]
            return w.reshape(K, N)
        residual = x
        mu = jnp.mean(x, axis=-1, keepdims=True)
        var = jnp.mean(jnp.square(x - mu), axis=-1, keepdims=True)
        h = (x - mu) * jax.lax.rsqrt(var + EPS) * ln_gamma + ln_beta
        hf = h.reshape(-1, H)
        w1 = _dequant(fc1_q, fc1_scales, G)
        y = hf @ w1 + fc1_bias
        y = jax.nn.silu(y)
        w2 = _dequant(fc2_q, fc2_scales, G)
        z = y @ w2 + fc2_bias
        return residual + 0.5 * z.reshape(residual.shape)

    def _L1_attn_ref(x, Wq, Wk, Wv, Wo):
        import jax, jax.numpy as jnp
        import numpy as np
        B, S, DIM = (2, 2048, 256)
        NH, NKV, HD = (16, 4, 64)
        GROUPS = NH // NKV
        CHUNK = 128
        THETA = 10000.0

        def _slopes(h):
            return jnp.asarray([2.0 ** (-8.0 / h * (i + 1)) for i in range(h)], dtype=jnp.float32)

        def _rope_tables(s, d):
            inv = 1.0 / THETA ** (np.arange(0, d, 2, dtype=np.float64) / d)
            freqs = np.outer(np.arange(s, dtype=np.float64), inv)
            emb = np.concatenate([freqs, freqs], axis=-1)
            return (jnp.asarray(np.cos(emb), jnp.float32), jnp.asarray(np.sin(emb), jnp.float32))

        def _apply_rope(x, cos, sin):
            x1, x2 = jnp.split(x, 2, axis=-1)
            rot = jnp.concatenate([-x2, x1], axis=-1)
            return x * cos + rot * sin

        def _lightning_attn(q, k, v, slopes, chunk):
            b, h, s, d = q.shape
            nc = s // chunk
            t = jnp.arange(chunk, dtype=jnp.float32)
            sl = slopes[:, None, None]
            mask = jnp.where(t[:, None] >= t[None, :], jnp.exp(-sl * (t[:, None] - t[None, :])), 0.0)
            q_dec = jnp.exp(-slopes[:, None] * (t + 1.0))[..., None]
            k_dec = jnp.exp(-slopes[:, None] * (chunk - 1.0 - t))[..., None]
            blk_dec = jnp.exp(-slopes * chunk)[None, :, None, None]

            def to_chunks(x):
                return x.reshape(b, h, nc, chunk, d).transpose(2, 0, 1, 3, 4)
            qc, kc, vc = (to_chunks(q), to_chunks(k), to_chunks(v))

            def step(kv, inp):
                qi, ki, vi = inp
                scores = jnp.einsum('bhtd,bhsd->bhts', qi, ki) * mask
                o = jnp.einsum('bhts,bhsd->bhtd', scores, vi) + jnp.einsum('bhtd,bhde->bhte', qi * q_dec, kv)
                kv = blk_dec * kv + jnp.einsum('bhtd,bhte->bhde', ki * k_dec, vi)
                return (kv, o)
            kv0 = jnp.zeros((b, h, d, d), q.dtype)
            _, outs = jax.lax.scan(step, kv0, (qc, kc, vc))
            return outs.transpose(1, 2, 0, 3, 4).reshape(b, h, s, d)
        b, s, _ = x.shape
        q = (x @ Wq.T).reshape(b, s, NH, HD).transpose(0, 2, 1, 3)
        k = (x @ Wk.T).reshape(b, s, NKV, HD).transpose(0, 2, 1, 3)
        v = (x @ Wv.T).reshape(b, s, NKV, HD).transpose(0, 2, 1, 3)
        cos, sin = _rope_tables(s, HD)
        q = _apply_rope(q, cos, sin)
        k = _apply_rope(k, cos, sin)
        k = jnp.repeat(k, GROUPS, axis=1)
        v = jnp.repeat(v, GROUPS, axis=1)
        out = _lightning_attn(q, k, v, _slopes(NH), CHUNK)
        out = out.transpose(0, 2, 1, 3).reshape(b, s, NH * HD)
        return out @ Wo.T

    def _L1_ffn_ref(hidden_states, q_w, q_b, k_w, k_b, v_w, v_b, o_w, o_b, router_w, router_b, w1, b1, w2, b2):
        import jax, jax.numpy as jnp
        import numpy as np
        import math
        D = 256
        H = 16
        E = 8
        TOPK = 2
        LAT = D // 2
        KPH = LAT // H
        HD = D // H

        def _forward(hs, q_w, q_b, k_w, k_b, v_w, v_b, o_w, o_b, router_w, router_b, w1, b1, w2, b2):
            B, S, _ = hs.shape
            Q = (hs @ q_w + q_b).reshape(B, S, H, HD).transpose(0, 2, 1, 3)
            K = (hs @ k_w + k_b).reshape(B, S, H, KPH).transpose(0, 2, 1, 3)
            V = (hs @ v_w + v_b).reshape(B, S, H, KPH).transpose(0, 2, 1, 3)
            scores = jnp.einsum('bhsk,bhtk->bhst', Q[..., :KPH], K) / math.sqrt(KPH)
            attn = jax.nn.softmax(scores, axis=-1)
            ao = jnp.einsum('bhst,bhtv->bhsv', attn, V)
            ao = ao.transpose(0, 2, 1, 3).reshape(B, S, H * KPH)
            ao = jnp.concatenate([ao, jnp.zeros((B, S, D - LAT), ao.dtype)], axis=-1)
            mla_out = ao @ o_w + o_b
            probs = jax.nn.softmax(mla_out @ router_w + router_b, axis=-1)
            topw, topi = jax.lax.top_k(probs, TOPK)
            topw = topw / (topw.sum(-1, keepdims=True) + 1e-08)
            combine = jnp.sum(jax.nn.one_hot(topi, E, dtype=probs.dtype) * topw[..., None], axis=-2)
            h1 = jnp.einsum('bsd,edf->ebsf', mla_out, w1) + b1[:, None, None, :]
            h1 = jax.nn.gelu(h1, approximate=False)
            h2 = jnp.einsum('ebsf,efd->ebsd', h1, w2) + b2[:, None, None, :]
            moe_out = jnp.einsum('bse,ebsd->bsd', combine, h2)
            return hs + 0.3 * moe_out
        return _forward(hidden_states, q_w, q_b, k_w, k_b, v_w, v_b, o_w, o_b, router_w, router_b, w1, b1, w2, b2)
    x = L0_attn_x
    x = _layernorm(x + _L0_attn_ref(x, L0_attn_Wq, L0_attn_Wkv, L0_attn_Wo, L0_attn_bo), axis=-1)
    x = _layernorm(x + _L0_ffn_ref(x, L0_ffn_ln_gamma, L0_ffn_ln_beta, L0_ffn_fc1_q, L0_ffn_fc1_scales, L0_ffn_fc1_bias, L0_ffn_fc2_q, L0_ffn_fc2_scales, L0_ffn_fc2_bias), axis=-1)
    x = _layernorm(x + _L1_attn_ref(x, L1_attn_Wq, L1_attn_Wk, L1_attn_Wv, L1_attn_Wo), axis=-1)
    x = _layernorm(x + _L1_ffn_ref(x, L1_ffn_q_w, L1_ffn_q_b, L1_ffn_k_w, L1_ffn_k_b, L1_ffn_v_w, L1_ffn_v_b, L1_ffn_o_w, L1_ffn_o_b, L1_ffn_router_w, L1_ffn_router_b, L1_ffn_w1, L1_ffn_b1, L1_ffn_w2, L1_ffn_b2), axis=-1)
    return x

_drawn_inputs = setup_inputs


def setup_inputs(seed=0):
    import zlib

    import numpy as np

    out = dict(_drawn_inputs(seed))
    spreads = {'L0_attn_bo': (0.0, 0.1),
     'L0_ffn_ln_gamma': (1.0, 0.2),
     'L0_ffn_ln_beta': (0.0, 0.1),
     'L1_ffn_q_b': (0.0, 0.8),
     'L1_ffn_k_b': (0.0, 2.0),
     'L1_ffn_v_b': (0.0, 0.8),
     'L1_ffn_o_b': (0.0, 0.8),
     'L1_ffn_router_b': (0.0, 0.515),
     'L1_ffn_b1': (0.0, 0.8),
     'L1_ffn_b2': (0.0, 2.0)}
    factors = {'L0_ffn_fc1_bias': 8.0,
     'L0_ffn_fc2_bias': 8.0,
     'L1_ffn_q_w': 8.0,
     'L1_ffn_k_w': 8.0,
     'L1_ffn_v_w': 8.0,
     'L1_ffn_o_w': 8.0,
     'L1_ffn_router_w': 8.0,
     'L1_ffn_w1': 8.0,
     'L1_ffn_w2': 8.0}
    for name, (base, spread) in spreads.items():
        noise = np.random.default_rng([zlib.crc32(name.encode()), seed]).standard_normal(out[name].shape)
        drawn = base * np.exp(spread * noise) if base else spread * noise
        out[name] = jnp.asarray(drawn.astype(out[name].dtype))
    for name, factor in factors.items():
        out[name] = (out[name] * factor).astype(out[name].dtype)
    return out
```

```python
from contextlib import ExitStack

import numpy as np

import concourse.bass as bass
from concourse import mybir

F32 = mybir.dt.float32
F32R = mybir.dt.float32r
I32 = mybir.dt.int32
ACT = mybir.ActivationFunctionType
ALU = mybir.AluOpType
AX = mybir.AxisListType

P = 128
BATCH, SEQ, D = 8, 512, 256
TT = SEQ // P
KD = D // P
HEADS, KVH, HD = 16, 4, 64
GRP = HEADS // KVH
PAIRS = HEADS // 2
INNER = HEADS * HD
HALF = HD // 2
EPS = 1e-5


class Steps:

    def __init__(self, sem, order):
        self.sem, self.order, self.per = sem, order, len(order)
        self.pos = {k: n for n, k in enumerate(order)}
        assert len(self.pos) == self.per

    def at(self, i, *key):
        return i * self.per + (self.pos[key] + 1 + self.per)

    def before(self, i, *key):
        return i * self.per + (self.pos[key] + 1)


def attention(nc, const, x_in, x_out, w_q, w_kv, w_o, out_bias, rope_tab, decay_tab, softmax, name):
    ctx = ExitStack()
    with ctx:
        sb = lambda n, s, dt=F32: ctx.enter_context(nc.sbuf_tensor(f"{name}_{n}", s, dt))
        sem = lambda n: ctx.enter_context(nc.semaphore(f"{name}_{n}"))
        ident = const["ident"]
        wqh, wql = (sb(n, [P, KD, INNER], F32R) for n in ("wqh", "wql"))
        wkh, wkl = (sb(n, [P, KD, 2 * KVH * HD], F32R) for n in ("wkh", "wkl"))
        woh, wol = (sb(n, [P, PAIRS, D], F32R) for n in ("woh", "wol"))
        if out_bias is not None:
            bias = sb("bias", [P, D])
        rope = sb("rope", [P, 3, SEQ])
        xc = sb("xc", [P, TT, D])
        xb = sb("xb", [P, TT, D])
        xth, xtl = (sb(n, [P, KD, SEQ], F32R) for n in ("xth", "xtl"))
        rt = sb("rt", [P, 2, 2, SEQ])
        y = sb("y", [P, 2, SEQ])
        yh = sb("yh", [P, 2, SEQ], F32R)
        qs = sb("qs", [P, 2, GRP, SEQ], F32R)
        ksh = sb("ksh", [P, KVH, SEQ], F32R)
        ksl = sb("ksl", [P, KVH, SEQ], F32R)
        v = sb("v", [P, TT, KVH * HD])
        if softmax:
            pe_ = sb("probs", [P, 2, TT, SEQ])
            rs = sb("rs", [P, HEADS, TT])
            ri = sb("ri", [P, TT, HEADS])
            mx = sb("mx", [P, HEADS, TT])
            rrep = sb("rrep", [P, SEQ])
        else:
            dec = sb("dec", [P, HEADS, SEQ])
        first_q = [0 if softmax else P * j for j in range(TT)]
        head_cols = sum(SEQ - c for c in first_q)
        pt = sb("pt", [P, 4 * head_cols])

        def weights_of(h, j):
            at = (h % 4) * head_cols + sum(SEQ - c for c in first_q[:j])
            return pt[:, at:at + SEQ - first_q[j]]

        ot = sb("ot", [P, SEQ])
        ath, atl = (sb(n, [P, PAIRS, SEQ], F32R) for n in ("ath", "atl"))
        r = sb("r", [P, 2, D])
        st6 = sb("st6", [P, 2, 6])
        mv = sb("mv", [P, 2, 2])
        vare = sb("vare", [P, 2, 1])
        rstd = sb("rstd", [P, 2, 1])
        outt = sb("outt", [P, 2, D])
        ps_s = ctx.enter_context(nc.psum_tensor(f"{name}_ps_s", [P, 4, SEQ], F32))
        ps_p = ctx.enter_context(nc.psum_tensor(f"{name}_ps_p", [P, 2, SEQ], F32))
        ps_m = ctx.enter_context(nc.psum_tensor(f"{name}_ps_m", [P, 2, SEQ], F32))

        weights_in, hi_split, weights_split = sem("weights_in"), sem("hi_split"), sem("weights_split")
        keys_scaled = sem("keys_scaled")
        held = sem("held")

        def hold(eng, semaphore, value):
            eng.wait_ge(semaphore, value)
            eng.sem_inc(held, 1)

        QN = 16 * 4 * GRP
        x_loaded = sem("x_loaded")
        q_stacked = [sem(f"q_stacked{s}") for s in range(2)]
        k_stacked = sem("k_stacked")
        stored = [sem(f"stored{s}") for s in range(2)]

        LAST = HEADS + 1
        pe_o, dve_o, act_o, pool_o = [], [], [], []
        pe_o += [("T", k) for k in range(KD)] + [("K", c) for c in range(2)]
        pe_o += [("V", t) for t in range(TT)] + [("Q", 0, c) for c in range(2)]
        dve_o += [("XH", 0), ("XL", 0), ("XH", 1), ("XL", 1), ("XB",), ("KR", 0), ("KR", 1), ("QR", 0, 0), ("QR", 0, 1)]
        act_o += [("V", t) for t in range(TT)]
        pool_o += [("KY",), ("KH",), ("KL",), ("QY", 0), ("QH", 0), ("QL", 0)]
        for h in range(LAST + 1):
            now, old = h < HEADS, 0 <= h - 1 < HEADS
            p = (h - 3) // 2 if h % 2 and h >= 3 else None
            for t in range(3):
                if now:
                    pe_o.append(("S", h, t)); dve_o.append(("M", h, t))
                    if softmax: act_o.append(("X", h, t))
            if softmax and old: dve_o.append(("I", h - 1))
            if p is not None:
                if softmax:
                    pe_o.append(("R", p)); act_o.append(("RC", p))
                pe_o.append(("A", p))
                if not softmax: act_o.append(("RC", p))
            if softmax and old:
                pe_o += [("P", h - 1, 0), ("P", h - 1, 1)]
                dve_o.append(("E", h - 1, 0)); act_o.append(("E", h - 1, 1))
            if now:
                pe_o.append(("S", h, 3)); dve_o.append(("M", h, 3))
                if softmax: act_o.append(("X", h, 3))
            if softmax and old:
                pe_o += [("P", h - 1, 2), ("P", h - 1, 3)]
                dve_o.append(("E", h - 1, 2)); act_o.append(("E", h - 1, 3))
            if p is not None:
                if softmax: dve_o.append(("O", p))
                pool_o += [("OH", p), ("OL", p)]
            if h % GRP == 1 and h // GRP + 1 < KVH:
                g = h // GRP + 1
                pe_o += [("Q", g, 0), ("Q", g, 1)]
                dve_o += [("QR", g, 0), ("QR", g, 1)]
                pool_o += [("QY", g), ("QH", g), ("QL", g)]
        pe_o += [("W", t) for t in range(TT)]
        for t in range(TT + 1):
            if t < TT:
                dve_o += [("F", t), ("B", t), ("G", t)]; pool_o += [("EPS", t), ("RSTD", t)]
            if t >= 1: dve_o.append(("N", t - 1))
        pe_s, dve_s = Steps(sem("tensor_steps"), pe_o), Steps(sem("vector_steps"), dve_o)
        act_s, pool_s = Steps(sem("scalar_steps"), act_o), Steps(sem("gpsimd_steps"), pool_o)

        misc = [k for k in pe_o if k[0] in "TKVQRAW"]
        assert len(misc) % 2 == 0
        bank = {k: n % 2 for n, k in enumerate(misc)}
        emptied = {"T": lambda k: (dve_s, ("XL", k[1])), "K": lambda k: (dve_s, ("KR", k[1])),
                   "V": lambda k: (act_s, ("V", k[1])), "Q": lambda k: (dve_s, ("QR", k[1], k[2])),
                   "R": lambda k: (act_s, ("RC", k[1])),
                   "A": lambda k: (dve_s, ("O", k[1])) if softmax else (act_s, ("RC", k[1])),
                   "W": lambda k: (dve_s, ("F", k[1]))}

        def wait_misc_bank(pe, i, key):
            n = misc.index(key)
            prev = misc[n - 2] if n >= 2 else misc[n - 2 + len(misc)]
            steps, k = emptied[prev[0]](prev)
            pe.wait_ge(steps.sem, steps.at(i, *k) if n >= 2 else steps.before(i, *k))

        WSPLIT = 3
        n_in = 5

        def raw_and_parts():
            q0, o0 = KD * 2 * KVH * HD, KD * 2 * KVH * HD + KD * INNER
            return ((pt[:, 0:q0], wkh, wkl), (pt[:, q0:o0], wqh, wql), (pt[:, o0:o0 + PAIRS * D], woh, wol))

        with nc.Block() as block:

            @block.sync
            def _(sp):
                for s in range(2):
                    sp.sem_inc(q_stacked[s], 2 * QN)
                    sp.sem_inc(stored[s], 32)
                raw_kv, raw_q, raw_o = (raw for raw, _, _ in raw_and_parts())
                sp.dma_start(raw_kv.rearrange("p (k n) -> p k n", k=KD), w_kv.rearrange("(k p) n -> p k n", p=P)).then_inc(weights_in, 16)
                sp.dma_start(raw_q.rearrange("p (k n) -> p k n", k=KD), w_q.rearrange("(k p) n -> p k n", p=P)).then_inc(weights_in, 16)
                sp.dma_start(raw_o.rearrange("p (k n) -> p k n", k=PAIRS), w_o.rearrange("(k p) n -> p k n", p=P)).then_inc(weights_in, 16)
                sp.dma_start(rope[:, :, :], rope_tab).then_inc(weights_in, 16)
                if not softmax:
                    sp.dma_start(dec[:, :, :], decay_tab).then_inc(weights_in, 16)
                if out_bias is not None:
                    sp.dma_start(bias[:, :], out_bias.partition_broadcast(P)).then_inc(weights_in, 16)
                with sp.Fori(0, BATCH) as i:
                    hold(sp, pe_s.sem, pe_s.before(i, "T", 1))
                    hold(sp, dve_s.sem, dve_s.before(i, "XB"))
                    sp.dma_start(xc[:, :, :], x_in[bass.ds(i, 1), :, :].rearrange("o (t p) d -> p (o t) d", p=P)).then_inc(x_loaded, 16)
                    hold(sp, pe_s.sem, pe_s.before(i, "S", HEADS - 1, 3))
                    hold(sp, pool_s.sem, pool_s.at(i, "KL"))
                    for dst, src in ((ksh, yh[:, :, :].bitcast(F32)), (ksl, y[:, :, :])):
                        for part in range(4):
                            for g in range(KVH):
                                sp.dma_start(dst[32 * part:32 * part + 32, g, :].bitcast(F32), src[32 * g:32 * g + 32, part % 2, :]).then_inc(k_stacked, 16)
                    for g in range(KVH):
                        slot = g % 2
                        if g >= 2:
                            hold(sp, pe_s.sem, pe_s.at(i, "S", GRP * (g - 1) - 1, 3))
                        else:
                            hold(sp, pe_s.sem, pe_s.before(i, "S", GRP * (g + 3) - 1, 3))
                        hold(sp, pool_s.sem, pool_s.at(i, "QL", g))
                        for lo, src in ((0, yh[:, :, :].bitcast(F32)), (64, y[:, :, :])):
                            for half in range(2):
                                for a in range(GRP):
                                    sp.dma_start(qs[lo + 32 * half:lo + 32 * half + 32, slot, a, :].bitcast(F32), src[32 * a:32 * a + 32, half, :]).then_inc(q_stacked[slot], 16)
                    for t in range(TT):
                        hold(sp, dve_s.sem, dve_s.at(i, "N", t))
                        sp.dma_start(x_out[bass.ds(i, 1), P * t:P * t + P, :].rearrange("o p d -> p (o d)"), outt[:, t % 2, :]).then_inc(stored[t % 2], 16)
                for s in range(2):
                    hold(sp, stored[s], 32 * BATCH + 32)

            def split3(out, a_hi, a_lo, b_hi, b_lo, kt):
                for k in range(kt):
                    for n, (a, b) in enumerate(((a_hi, b_hi), (a_hi, b_lo), (a_lo, b_hi))):
                        last = nc.tensor.matmul(out, a(k), b(k), start=(k == 0 and n == 0), stop=(k == kt - 1 and n == 2))
                return last

            @block.tensor
            def _(pe):
                pe.sem_inc(pe_s.sem, pe_s.per)
                pe.wait_ge(weights_split, WSPLIT)
                pe.wait_ge(const["ready"], const["count"])
                with pe.Fori(0, BATCH) as i:
                    for key in pe_o:
                        kind = key[0]
                        if kind in "TKVQRAW":
                            wait_misc_bank(pe, i, key)
                            m = ps_m[:, bank[key], :]
                        if kind == "T":
                            k = key[1]
                            if k == 0:
                                pe.wait_ge(x_loaded, 16 * i + 16)
                            for t in range(TT):
                                last = nc.tensor.transpose(m[:, P * t:P * t + P], xc[:, t, P * k:P * k + P], ident[:, :])
                        elif kind == "K":
                            c = key[1]
                            if c == 0:
                                pe.wait_ge(dve_s.sem, dve_s.at(i, "XL", 1))
                            cols = slice(P * c, P * c + P)
                            last = split3(m, lambda k: wkh[:, k, cols], lambda k: wkl[:, k, cols],
                                          lambda k: xth[:, k, :], lambda k: xtl[:, k, :], KD)
                        elif kind == "V":
                            t = key[1]
                            tok = slice(P * t, P * t + P)
                            last = split3(m[:, 0:KVH * HD], lambda k: xth[:, k, tok], lambda k: xtl[:, k, tok],
                                          lambda k: wkh[:, k, KVH * HD:], lambda k: wkl[:, k, KVH * HD:], KD)
                        elif kind == "Q":
                            g, c = key[1:]
                            cols = slice(P * (2 * g + c), P * (2 * g + c) + P)
                            last = split3(m, lambda k: wqh[:, k, cols], lambda k: wql[:, k, cols],
                                          lambda k: xth[:, k, :], lambda k: xtl[:, k, :], KD)
                        elif kind == "S":
                            h, t = key[1:]
                            g, slot = h // GRP, (h // GRP) % 2
                            if h == 0 and t == 0:
                                pe.wait_ge(k_stacked, 16 * 32 * i + 16 * 32)
                            if h % GRP == 0 and t == 0:
                                pe.wait_ge(q_stacked[slot], 2 * QN * i + QN * (g // 2 + 1) + 2 * QN)
                            if softmax:
                                pe.wait_ge(act_s.sem, act_s.at(i, "X", h - 1, t) if h else act_s.before(i, "X", HEADS - 1, t))
                                for n, ks in enumerate((ksh, ksl)):
                                    last = nc.tensor.matmul(ps_s[:, t, :], qs[:, slot, h % GRP, P * t:P * t + P], ks[:, g, :], start=(n == 0), stop=(n == 1))
                            else:
                                pe.wait_ge(dve_s.sem, dve_s.at(i, "M", h - 1, t) if h else dve_s.before(i, "M", HEADS - 1, t))
                                for n, ks in enumerate((ksh, ksl)):
                                    last = nc.tensor.matmul(ps_s[:, t, P * t:SEQ], ks[:, g, P * t:P * t + P], qs[:, slot, h % GRP, P * t:SEQ], start=(n == 0), stop=(n == 1))
                        elif kind == "P":
                            h, j = key[1:]
                            if j == 0:
                                pe.wait_ge(act_s.sem, act_s.at(i, "X", h, 3))
                            if (h, j) == (0, 0):
                                pe.wait_ge(dve_s.sem, dve_s.before(i, "E", HEADS - 1, 2))
                            elif (h, j) == (0, 1):
                                pe.wait_ge(act_s.sem, act_s.before(i, "E", HEADS - 1, 3))
                            else:
                                ph, pj = (h, j - 2) if j >= 2 else (h - 1, j + 2)
                                s_ = dve_s if pj % 2 == 0 else act_s
                                pe.wait_ge(s_.sem, s_.at(i, "E", ph, pj))
                            for t in range(TT):
                                last = nc.tensor.transpose(ps_p[:, j % 2, P * t:P * t + P], pe_[:, h % 2, t, P * j:P * j + P], ident[:, :])
                        elif kind == "R":
                            p = key[1]
                            pe.wait_ge(dve_s.sem, dve_s.at(i, "I", 2 * p + 1))
                            for t in range(TT):
                                for s in range(2):
                                    last = nc.tensor.matmul(m[HD * s:HD * s + HD, P * t:P * t + P], ri[:, t, 2 * p + s:2 * p + s + 1].broadcast_to([P, HD]), ident[:, :], start=True, stop=True)
                        elif kind == "A":
                            p = key[1]
                            g = 2 * p // GRP
                            pe.wait_ge(act_s.sem, act_s.at(i, "V", TT - 1))
                            if softmax:
                                pe.wait_ge(dve_s.sem, dve_s.at(i, "E", 2 * p + 1, 2))
                                pe.wait_ge(act_s.sem, act_s.at(i, "E", 2 * p + 1, 3))
                            else:
                                pe.wait_ge(dve_s.sem, dve_s.at(i, "M", 2 * p + 1, 3))
                            for j in range(TT):
                                c0 = first_q[j]
                                for s in range(2):
                                    last = nc.tensor.matmul(m[HD * s:HD * s + HD, c0:SEQ], v[:, j, HD * g:HD * g + HD],
                                                            weights_of(2 * p + s, j), start=(j == 0), stop=(j == TT - 1))
                        elif kind == "W":
                            t = key[1]
                            tok = slice(P * t, P * t + P)
                            if t == 0:
                                pe.wait_ge(pool_s.sem, pool_s.at(i, "OL", PAIRS - 1))
                            last = split3(m[:, 0:D], lambda k: ath[:, k, tok], lambda k: atl[:, k, tok],
                                          lambda k: woh[:, k, :], lambda k: wol[:, k, :], PAIRS)
                        last.then_inc(pe_s.sem, 1)

            @block.vector
            def _(dve):
                dve.sem_inc(dve_s.sem, dve_s.per)
                dve.wait_ge(weights_in, 16 * n_in)
                if softmax:
                    keys = raw_and_parts()[0][0].rearrange("p (k n) -> p k n", k=KD)[:, :, 0:KVH * HD]
                    nc.vector.tensor_scalar(keys, keys, HD ** -0.5, None, ALU.mult).then_inc(keys_scaled, 1)
                for n, (raw, hi, lo) in enumerate(raw_and_parts()):
                    dve.wait_ge(hi_split, n + 1)
                    flat = lambda x: x[:, :, :].rearrange("p k n -> p (k n)")
                    nc.vector.tensor_tensor(flat(lo), raw, flat(hi).bitcast(F32), ALU.subtract).then_inc(weights_split, 1)
                with dve.Fori(0, BATCH) as i:
                    for key in dve_o:
                        kind = key[0]
                        if kind == "XH":
                            k = key[1]
                            dve.wait_ge(pe_s.sem, pe_s.at(i, "T", k))
                            if k == 0:
                                dve.wait_ge(pe_s.sem, pe_s.before(i, "Q", KVH - 1, 1))
                            op = nc.vector.tensor_copy(xth[:, k, :], ps_m[:, bank["T", k], :])
                        elif kind == "XL":
                            k = key[1]
                            dve.wait_ge(dve_s.sem, dve_s.at(i, "XH", k))
                            op = nc.vector.tensor_tensor(xtl[:, k, :], ps_m[:, bank["T", k], :], xth[:, k, :].bitcast(F32), ALU.subtract)
                        elif kind == "XB":
                            dve.wait_ge(dve_s.sem, dve_s.before(i, "F", TT - 1))
                            if out_bias is not None:
                                op = nc.vector.tensor_tensor(xb[:, :, :], xc[:, :, :], bias[:, :].unsqueeze(1).broadcast_to([P, TT, D]), ALU.add)
                            else:
                                op = nc.vector.tensor_copy(xb[:, :, :], xc[:, :, :])
                        elif kind in ("KR", "QR"):
                            c = key[-1]
                            src = ("K", c) if kind == "KR" else ("Q", key[1], c)
                            dve.wait_ge(pe_s.sem, pe_s.at(i, *src))
                            if c == 0:
                                prev = ("KY",) if kind == "QR" and key[1] == 0 else ("QY", key[1] - 1) if kind == "QR" else ("QY", KVH - 1)
                                dve.wait_ge(pool_s.sem, pool_s.before(i, *prev) if kind == "KR" else pool_s.at(i, *prev))
                            op = nc.vector.tensor_tensor(rt[:, c, :, :], ps_m[:, bank[src], :].unsqueeze(1).broadcast_to([P, 2, SEQ]),
                                                         rope[:, 1 - c:3 - c, :], ALU.mult)
                        elif kind == "M":
                            h, t = key[1:]
                            dve.wait_ge(pe_s.sem, pe_s.at(i, "S", h, t))
                            if softmax:
                                if t == 0:
                                    dve.wait_ge(act_s.sem, act_s.before(i, "X", h, TT - 1))
                                op = nc.vector.tensor_reduce(out=mx[:, h, t:t + 1], in_=ps_s[:, t, :], axis=AX.X, op=ALU.max, negate=True)
                            else:
                                if t == 0 and h % 2 == 0:
                                    p = h // 2
                                    dve.wait_ge(pe_s.sem, pe_s.at(i, "A", p - 2) if p >= 2 else pe_s.before(i, "A", p + PAIRS - 2))
                                op = nc.vector.tensor_tensor(weights_of(h, t), ps_s[:, t, P * t:SEQ], dec[:, h, 0:SEQ - P * t], ALU.mult)
                        elif kind == "I":
                            h = key[1]
                            dve.wait_ge(act_s.sem, act_s.at(i, "X", h, TT - 1))
                            if h == 0:
                                dve.wait_ge(pe_s.sem, pe_s.before(i, "R", PAIRS - 1))
                            op = nc.vector.reciprocal(ri[:, :, h], rs[:, h, :])
                        elif kind == "E":
                            h, j = key[1:]
                            dve.wait_ge(pe_s.sem, pe_s.at(i, "P", h, j))
                            if j == 0:
                                p = h // 2
                                dve.wait_ge(pe_s.sem, pe_s.at(i, "A", p - 2) if p >= 2 else pe_s.before(i, "A", p + PAIRS - 2))
                            op = nc.vector.tensor_copy(weights_of(h, j), ps_p[:, j % 2, :])
                        elif kind == "O":
                            p = key[1]
                            dve.wait_ge(pe_s.sem, pe_s.at(i, "A", p))
                            dve.wait_ge(act_s.sem, act_s.at(i, "RC", p))
                            dve.wait_ge(pool_s.sem, pool_s.at(i, "OL", p - 1) if p else pool_s.before(i, "OL", PAIRS - 1))
                            op = nc.vector.tensor_tensor(ot[:, :], ps_m[:, bank["A", p], :], rrep[:, :], ALU.mult)
                        elif kind == "F":
                            t = key[1]
                            dve.wait_ge(pe_s.sem, pe_s.at(i, "W", t))
                            if t == 0:
                                dve.wait_ge(dve_s.sem, dve_s.at(i, "XB"))
                            dve.wait_ge(dve_s.sem, dve_s.at(i, "N", t - 2) if t >= 2 else dve_s.before(i, "N", t + 2))
                            op = nc.vector.tensor_tensor(r[:, t % 2, :], ps_m[:, bank["W", t], 0:D], xb[:, t, :], ALU.add)
                        elif kind == "B":
                            t = key[1]
                            dve.wait_ge(dve_s.sem, dve_s.at(i, "F", t))
                            op = nc.vector.bn_stats(st6[:, t % 2, :], r[:, t % 2, :])
                        elif kind == "G":
                            t = key[1]
                            hold(dve, dve_s.sem, dve_s.at(i, "B", t))
                            op = nc.vector.bn_aggr(mv[:, t % 2, :], st6[:, t % 2, :])
                        elif kind == "N":
                            t = key[1]
                            dve.wait_ge(pool_s.sem, pool_s.at(i, "RSTD", t))
                            if t >= 2:
                                dve.wait_ge(stored[t % 2], 32 * i + 16 * (t // 2) + 32)
                            else:
                                dve.wait_ge(stored[t % 2], 32 * i + 32)
                            op = nc.vector.tensor_scalar(outt[:, t % 2, :], r[:, t % 2, :], mv[:, t % 2, 0:1], rstd[:, t % 2, :], ALU.subtract, ALU.mult)
                        op.then_inc(dve_s.sem, 1)

            @block.scalar
            def _(act):
                act.sem_inc(act_s.sem, act_s.per)
                act.wait_ge(weights_in, 16 * n_in)
                if softmax:
                    act.wait_ge(keys_scaled, 1)
                for raw, hi, _ in raw_and_parts():
                    nc.scalar.copy(hi[:, :, :].rearrange("p k n -> p (k n)"), raw).then_inc(hi_split, 1)
                with act.Fori(0, BATCH) as i:
                    for key in act_o:
                        kind = key[0]
                        if kind == "V":
                            t = key[1]
                            act.wait_ge(pe_s.sem, pe_s.at(i, "V", t))
                            if t == 0:
                                act.wait_ge(pe_s.sem, pe_s.before(i, "A", PAIRS - 1))
                            op = nc.scalar.copy(v[:, t, :], ps_m[:, bank[key], 0:KVH * HD])
                        elif kind == "X":
                            h, t = key[1:]
                            act.wait_ge(dve_s.sem, dve_s.at(i, "M", h, t))
                            if t == 0:
                                act.wait_ge(pe_s.sem, pe_s.at(i, "P", h - 2, TT - 1) if h >= 2 else pe_s.before(i, "P", h + HEADS - 2, TT - 1))
                                act.wait_ge(dve_s.sem, dve_s.before(i, "I", h))
                            op = nc.scalar.activation(pe_[:, h % 2, t, :], ps_s[:, t, :], ACT.Exp, bias=mx[:, h, t:t + 1], scale=1.0,
                                                      accum_out=rs[:, h, t:t + 1])
                        elif kind == "E":
                            h, j = key[1:]
                            act.wait_ge(pe_s.sem, pe_s.at(i, "P", h, j))
                            p = h // 2
                            act.wait_ge(pe_s.sem, pe_s.at(i, "A", p - 2) if p >= 2 else pe_s.before(i, "A", p + PAIRS - 2))
                            op = nc.scalar.copy(weights_of(h, j), ps_p[:, j % 2, :])
                        elif kind == "RC":
                            p = key[1]
                            if softmax:
                                act.wait_ge(pe_s.sem, pe_s.at(i, "R", p))
                                act.wait_ge(dve_s.sem, dve_s.at(i, "O", p - 1) if p else dve_s.before(i, "O", PAIRS - 1))
                                op = nc.scalar.copy(rrep[:, :], ps_m[:, bank["R", p], :])
                            else:
                                act.wait_ge(pe_s.sem, pe_s.at(i, "A", p))
                                act.wait_ge(pool_s.sem, pool_s.at(i, "OL", p - 1) if p else pool_s.before(i, "OL", PAIRS - 1))
                                op = nc.scalar.copy(ot[:, :], ps_m[:, bank["A", p], :])
                        op.then_inc(act_s.sem, 1)

            @block.gpsimd
            def _(pool):
                pool.sem_inc(pool_s.sem, pool_s.per)
                with pool.Fori(0, BATCH) as i:
                    for key in pool_o:
                        kind = key[0]
                        if kind in ("KY", "QY"):
                            src = ("KR", 1) if kind == "KY" else ("QR", key[1], 1)
                            hold(pool, dve_s.sem, dve_s.at(i, *src))
                            if kind == "KY":
                                hold(pool, q_stacked[(KVH - 1) % 2], 2 * QN * i + 2 * QN)
                            elif key[1] == 0:
                                hold(pool, k_stacked, 16 * 32 * i + 16 * 32)
                            else:
                                hold(pool, q_stacked[(key[1] - 1) % 2], 2 * QN * i + QN * ((key[1] - 1) // 2 + 1) + 2 * QN)
                            op = nc.gpsimd.tensor_tensor(y[:, :, :], rt[:, 0, :, :], rt[:, 1, :, :], ALU.add)
                        elif kind in ("KH", "QH"):
                            hold(pool, pool_s.sem, pool_s.at(i, kind[0] + "Y", *key[1:]))
                            op = nc.gpsimd.tensor_copy(yh[:, :, :], y[:, :, :])
                        elif kind in ("KL", "QL"):
                            hold(pool, pool_s.sem, pool_s.at(i, kind[0] + "H", *key[1:]))
                            op = nc.gpsimd.tensor_tensor(y[:, :, :].bitcast(F32R), y[:, :, :], yh[:, :, :].bitcast(F32), ALU.subtract)
                        elif kind == "OH":
                            p = key[1]
                            src = (dve_s, "O") if softmax else (act_s, "RC")
                            hold(pool, src[0].sem, src[0].at(i, src[1], p))
                            if p == 0:
                                hold(pool, pe_s.sem, pe_s.before(i, "W", TT - 1))
                            op = nc.gpsimd.tensor_copy(ath[:, p, :], ot[:, :])
                        elif kind == "OL":
                            p = key[1]
                            hold(pool, pool_s.sem, pool_s.at(i, "OH", p))
                            op = nc.gpsimd.tensor_tensor(atl[:, p, :], ot[:, :], ath[:, p, :].bitcast(F32), ALU.subtract)
                        elif kind == "EPS":
                            t = key[1]
                            hold(pool, dve_s.sem, dve_s.at(i, "G", t))
                            hold(pool, dve_s.sem, dve_s.at(i, "N", t - 2) if t >= 2 else dve_s.before(i, "N", t + 2))
                            op = nc.gpsimd.tensor_scalar(vare[:, t % 2, :], mv[:, t % 2, 1:2], EPS, None, ALU.add)
                        elif kind == "RSTD":
                            t = key[1]
                            hold(pool, pool_s.sem, pool_s.at(i, "EPS", t))
                            op = nc.gpsimd.tensor_tensor(rstd[:, t % 2, :], vare[:, t % 2, :], const["minus_half"][:, :], ALU.pow)
                        op.then_inc(pool_s.sem, 1)


def gated_hold(nc_sem):
    def hold(eng, semaphore, value):
        eng.wait_ge(semaphore, value)
        eng.sem_inc(nc_sem, 1)
    return hold


def sum_of_parts(nc, out, a_hi, a_lo, b_hi, b_lo, tiles):
    for k in range(tiles):
        for n, (a, b) in enumerate(((a_hi, b_hi), (a_hi, b_lo), (a_lo, b_hi))):
            last = nc.tensor.matmul(out, a(k), b(k), start=(k == 0 and n == 0), stop=(k == tiles - 1 and n == 2))
    return last


def quantized_ffn(nc, const, x_in, x_out, gamma_beta, q1, s1, b1, q2, s2, b2, name):
    F = q1.shape[1]
    FT = F // P
    ctx = ExitStack()
    with ctx:
        sb = lambda n, s, dt=F32: ctx.enter_context(nc.sbuf_tensor(f"{name}_{n}", s, dt))
        sem = lambda n: ctx.enter_context(nc.semaphore(f"{name}_{n}"))
        ident = const["ident"]
        qi1, qi2 = sb("qi1", [P, KD, F], I32), sb("qi2", [P, FT, D], I32)
        sc1, sc2 = sb("sc1", [P, KD, F]), sb("sc2", [P, FT, D])
        w1h, w1l = (sb(n, [P, KD, F], F32R) for n in ("w1h", "w1l"))
        w2h, w2l = (sb(n, [P, FT, D], F32R) for n in ("w2h", "w2l"))
        gb = sb("gb", [P, 2, KD])
        b1c = sb("b1c", [P, FT])
        b2r = sb("b2r", [P, D])
        xc = sb("xc", [P, TT, D])
        xb = sb("xb", [P, TT, D])
        xn = sb("xn", [P, TT, D])
        ht = sb("ht", [P, KD, SEQ])
        hth, htl = (sb(n, [P, KD, SEQ], F32R) for n in ("hth", "htl"))
        s = sb("s", [P, 2, SEQ])
        sh, sl = (sb(n, [P, FT, SEQ], F32R) for n in ("sh", "sl"))
        r = sb("r", [P, 2, D])
        st6, st6x = sb("st6", [P, 2, 6]), sb("st6x", [P, TT, 6])
        mv, mvx = sb("mv", [P, 2, 2]), sb("mvx", [P, TT, 2])
        vare, varex = sb("vare", [P, 2, 1]), sb("varex", [P, TT, 1])
        rstd, rstdx = sb("rstd", [P, 2, 1]), sb("rstdx", [P, TT, 1])
        outt = sb("outt", [P, 2, D])
        ps = ctx.enter_context(nc.psum_tensor(f"{name}_ps", [P, 8, SEQ], F32))
        weights_in, weight_steps, hi_split, weights_split = sem("weights_in"), sem("weight_steps"), sem("hi_split"), sem("weights_split")
        x_loaded = sem("x_loaded")
        stored = [sem(f"stored{k}") for k in range(2)]
        hold = gated_hold(sem("held"))

        pe_o = [("T", k) for k in range(KD)] + [("H", m) for m in range(FT)] + [("W", t) for t in range(TT)]
        dve_o = [(n, t) for t in range(TT) for n in ("BX", "GX")] + [("NX", t) for t in range(TT)] + [("XB",)]
        dve_o += [(n, k) for k in range(KD) for n in ("XH", "XL")]
        dve_o += [(n, m) for m in range(FT) for n in ("SH", "SL")]
        act_o = [("HT", k) for k in range(KD)] + [("S", m) for m in range(FT)]
        pool_o = [("EPSX",), ("RSTDX",)]
        for t in range(TT + 1):
            if t < TT:
                dve_o += [("F", t), ("B", t), ("G", t)]; pool_o += [("EPS", t), ("RSTD", t)]
            if t >= 1: dve_o.append(("N", t - 1))
        pe_s, dve_s = Steps(sem("tensor_steps"), pe_o), Steps(sem("vector_steps"), dve_o)
        act_s, pool_s = Steps(sem("scalar_steps"), act_o), Steps(sem("gpsimd_steps"), pool_o)
        BANKS = 7
        assert len(pe_o) % BANKS == 0
        bank = {k: n % BANKS for n, k in enumerate(pe_o)}

        with nc.Block() as block:

            @block.sync
            def _(sp):
                for k in range(2):
                    sp.sem_inc(stored[k], 32)
                sp.dma_start(qi1[:, :, :], q1.rearrange("(k p) n -> p k n", p=P)).then_inc(weights_in, 16)
                sp.dma_start(sc1[:, :, :].rearrange("p k n -> p (k n)"), s1.rearrange("k n -> (k n)").partition_broadcast(P)).then_inc(weights_in, 16)
                sp.dma_start(qi2[:, :, :], q2.rearrange("(k p) n -> p k n", p=P)).then_inc(weights_in, 16)
                sp.dma_start(sc2[:, :, :].rearrange("p k n -> p (k n)"), s2.rearrange("k n -> (k n)").partition_broadcast(P)).then_inc(weights_in, 16)
                sp.dma_start(gb[:, :, :], gamma_beta).then_inc(weights_in, 16)
                sp.dma_start(b1c[:, :], b1).then_inc(weights_in, 16)
                sp.dma_start(b2r[:, :], b2.partition_broadcast(P)).then_inc(weights_in, 16)
                with sp.Fori(0, BATCH) as i:
                    hold(sp, dve_s.sem, dve_s.before(i, "XB"))
                    sp.dma_start(xc[:, :, :], x_in[bass.ds(i, 1), :, :].rearrange("o (t p) d -> p (o t) d", p=P)).then_inc(x_loaded, 16)
                    for t in range(TT):
                        hold(sp, dve_s.sem, dve_s.at(i, "N", t))
                        sp.dma_start(x_out[bass.ds(i, 1), P * t:P * t + P, :].rearrange("o p d -> p (o d)"), outt[:, t % 2, :]).then_inc(stored[t % 2], 16)
                for k in range(2):
                    hold(sp, stored[k], 32 * BATCH + 32)

            @block.tensor
            def _(pe):
                pe.sem_inc(pe_s.sem, pe_s.per)
                pe.wait_ge(weights_split, 2)
                with pe.Fori(0, BATCH) as i:
                    for n, key in enumerate(pe_o):
                        kind = key[0]
                        m = ps[:, bank[key], :]
                        was = pe_o[n - BANKS]
                        reader, rk = {"T": (act_s, ("HT",)), "H": (act_s, ("S",)), "W": (dve_s, ("F",))}[was[0]]
                        value = reader.at if n >= BANKS else reader.before
                        pe.wait_ge(reader.sem, value(i, rk[0], was[1]))
                        if kind == "T":
                            k = key[1]
                            if k == 0:
                                pe.wait_ge(dve_s.sem, dve_s.at(i, "NX", TT - 1))
                            for t in range(TT):
                                last = nc.tensor.transpose(m[:, P * t:P * t + P], xn[:, t, P * k:P * k + P], ident[:, :])
                        elif kind == "H":
                            cols = slice(P * key[1], P * key[1] + P)
                            if key[1] == 0:
                                pe.wait_ge(dve_s.sem, dve_s.at(i, "XL", KD - 1))
                            last = sum_of_parts(nc, m, lambda k: w1h[:, k, cols], lambda k: w1l[:, k, cols],
                                                lambda k: hth[:, k, :], lambda k: htl[:, k, :], KD)
                        elif kind == "W":
                            t = key[1]
                            tok = slice(P * t, P * t + P)
                            if t == 0:
                                pe.wait_ge(dve_s.sem, dve_s.at(i, "SL", FT - 1))
                            last = sum_of_parts(nc, m[:, 0:D], lambda k: sh[:, k, tok], lambda k: sl[:, k, tok],
                                                lambda k: w2h[:, k, :], lambda k: w2l[:, k, :], FT)
                        last.then_inc(pe_s.sem, 1)

            flat = lambda x: x[:, :, :].rearrange("p k n -> p (k n)")

            @block.vector
            def _(dve):
                dve.sem_inc(dve_s.sem, dve_s.per)
                dve.wait_ge(weights_in, 16 * 7)
                nc.vector.tensor_scalar(b2r[:, :], b2r[:, :], 0.5, None, ALU.mult).then_inc(weight_steps, 1)
                for qi, sc in ((qi1, sc1), (qi2, sc2)):
                    nc.vector.scalar_tensor_tensor(out=flat(sc), in0=flat(qi), scalar=-128.0, in1=flat(sc), op0=ALU.add, op1=ALU.mult).then_inc(weight_steps, 1)
                for n, (raw, hi, lo) in enumerate(((sc1, w1h, w1l), (sc2, w2h, w2l))):
                    dve.wait_ge(hi_split, n + 1)
                    nc.vector.tensor_tensor(flat(lo), flat(raw), flat(hi).bitcast(F32), ALU.subtract).then_inc(weights_split, 1)
                with dve.Fori(0, BATCH) as i:
                    for key in dve_o:
                        kind = key[0]
                        t = k = m = key[1] if len(key) > 1 else 0
                        if kind == "BX":
                            if t == 0:
                                dve.wait_ge(x_loaded, 16 * i + 16)
                                dve.wait_ge(dve_s.sem, dve_s.before(i, "NX", TT - 1))
                            op = nc.vector.bn_stats(st6x[:, t, :], xc[:, t, :])
                        elif kind == "GX":
                            hold(dve, dve_s.sem, dve_s.at(i, "BX", t))
                            op = nc.vector.bn_aggr(mvx[:, t, :], st6x[:, t, :])
                        elif kind == "NX":
                            if t == 0:
                                dve.wait_ge(pool_s.sem, pool_s.at(i, "RSTDX"))
                                dve.wait_ge(pe_s.sem, pe_s.before(i, "T", KD - 1))
                            op = nc.vector.tensor_scalar(xn[:, t, :], xc[:, t, :], mvx[:, t, 0:1], rstdx[:, t, :], ALU.subtract, ALU.mult)
                        elif kind == "XB":
                            dve.wait_ge(dve_s.sem, dve_s.before(i, "F", TT - 1))
                            op = nc.vector.scalar_tensor_tensor(out=xb[:, :, :], in0=xc[:, :, :], scalar=2.0,
                                                                in1=b2r[:, :].unsqueeze(1).broadcast_to([P, TT, D]), op0=ALU.mult, op1=ALU.add)
                        elif kind == "XH":
                            dve.wait_ge(act_s.sem, act_s.at(i, "HT", k))
                            if k == 0:
                                dve.wait_ge(pe_s.sem, pe_s.before(i, "H", FT - 1))
                            op = nc.vector.tensor_copy(hth[:, k, :], ht[:, k, :])
                        elif kind == "XL":
                            dve.wait_ge(dve_s.sem, dve_s.at(i, "XH", k))
                            op = nc.vector.tensor_tensor(htl[:, k, :], ht[:, k, :], hth[:, k, :].bitcast(F32), ALU.subtract)
                        elif kind == "SH":
                            dve.wait_ge(act_s.sem, act_s.at(i, "S", m))
                            if m == 0:
                                dve.wait_ge(pe_s.sem, pe_s.before(i, "W", TT - 1))
                            op = nc.vector.tensor_copy(sh[:, m, :], s[:, m % 2, :])
                        elif kind == "SL":
                            dve.wait_ge(dve_s.sem, dve_s.at(i, "SH", m))
                            op = nc.vector.tensor_tensor(sl[:, m, :], s[:, m % 2, :], sh[:, m, :].bitcast(F32), ALU.subtract)
                        elif kind == "F":
                            dve.wait_ge(pe_s.sem, pe_s.at(i, "W", t))
                            dve.wait_ge(dve_s.sem, dve_s.at(i, "N", t - 2) if t >= 2 else dve_s.before(i, "N", t + 2))
                            op = nc.vector.scalar_tensor_tensor(out=r[:, t % 2, :], in0=ps[:, bank["W", t], 0:D], scalar=0.5, in1=xb[:, t, :], op0=ALU.mult, op1=ALU.add)
                        elif kind == "B":
                            dve.wait_ge(dve_s.sem, dve_s.at(i, "F", t))
                            op = nc.vector.bn_stats(st6[:, t % 2, :], r[:, t % 2, :])
                        elif kind == "G":
                            hold(dve, dve_s.sem, dve_s.at(i, "B", t))
                            op = nc.vector.bn_aggr(mv[:, t % 2, :], st6[:, t % 2, :])
                        elif kind == "N":
                            dve.wait_ge(pool_s.sem, pool_s.at(i, "RSTD", t))
                            dve.wait_ge(stored[t % 2], 32 * i + 16 * (t // 2) + 32)
                            op = nc.vector.tensor_scalar(outt[:, t % 2, :], r[:, t % 2, :], mv[:, t % 2, 0:1], rstd[:, t % 2, :], ALU.subtract, ALU.mult)
                        op.then_inc(dve_s.sem, 1)

            @block.scalar
            def _(act):
                act.sem_inc(act_s.sem, act_s.per)
                for n, (raw, hi) in enumerate(((sc1, w1h), (sc2, w2h))):
                    act.wait_ge(weight_steps, n + 2)
                    nc.scalar.copy(flat(hi), flat(raw)).then_inc(hi_split, 1)
                with act.Fori(0, BATCH) as i:
                    for key in act_o:
                        kind, k = key
                        if kind == "HT":
                            act.wait_ge(pe_s.sem, pe_s.at(i, "T", k))
                            act.wait_ge(dve_s.sem, dve_s.before(i, "XL", k))
                            op = nc.scalar.activation(ht[:, k, :], ps[:, bank["T", k], :], ACT.Identity, bias=gb[:, 1, k:k + 1], scale=gb[:, 0, k:k + 1])
                        else:
                            act.wait_ge(pe_s.sem, pe_s.at(i, "H", k))
                            act.wait_ge(dve_s.sem, dve_s.at(i, "SL", k - 2) if k >= 2 else dve_s.before(i, "SL", k + FT - 2))
                            op = nc.scalar.activation(s[:, k % 2, :], ps[:, bank["H", k], :], ACT.Silu, bias=b1c[:, k:k + 1], scale=1.0)
                        op.then_inc(act_s.sem, 1)

            @block.gpsimd
            def _(pool):
                pool.sem_inc(pool_s.sem, pool_s.per)
                with pool.Fori(0, BATCH) as i:
                    for key in pool_o:
                        kind = key[0]
                        if kind == "EPSX":
                            hold(pool, dve_s.sem, dve_s.at(i, "GX", TT - 1))
                            op = nc.gpsimd.tensor_scalar(varex[:, :, :], mvx[:, :, 1:2], EPS, None, ALU.add)
                        elif kind == "RSTDX":
                            hold(pool, pool_s.sem, pool_s.at(i, "EPSX"))
                            hold(pool, dve_s.sem, dve_s.before(i, "NX", TT - 1))
                            op = nc.gpsimd.tensor_tensor(rstdx[:, :, :], varex[:, :, :], const["minus_half"][:, :].unsqueeze(1).broadcast_to([P, TT, 1]), ALU.pow)
                        elif kind == "EPS":
                            t = key[1]
                            hold(pool, dve_s.sem, dve_s.at(i, "G", t))
                            op = nc.gpsimd.tensor_scalar(vare[:, t % 2, :], mv[:, t % 2, 1:2], EPS, None, ALU.add)
                        elif kind == "RSTD":
                            t = key[1]
                            hold(pool, pool_s.sem, pool_s.at(i, "EPS", t))
                            hold(pool, dve_s.sem, dve_s.at(i, "N", t - 2) if t >= 2 else dve_s.before(i, "N", t + 2))
                            op = nc.gpsimd.tensor_tensor(rstd[:, t % 2, :], vare[:, t % 2, :], const["minus_half"][:, :], ALU.pow)
                        op.then_inc(pool_s.sem, 1)


MH, KPH, VAR = 16, 8, 4
QUADS = MH // 4
E_ = 8


def latent_attention(nc, const, x_in, m_out, comb_out, w, name):
    ctx = ExitStack()
    with ctx:
        sb = lambda n, s, dt=F32: ctx.enter_context(nc.sbuf_tensor(f"{name}_{n}", s, dt))
        sem = lambda n: ctx.enter_context(nc.semaphore(f"{name}_{n}"))
        ident = const["ident"]
        LAT = MH * KPH
        raw_y = sb("raw_y", [P, KD, 2 * 4 * LAT])
        raw_v = sb("raw_v", [P, KD, LAT])
        raw_r = sb("raw_r", [P, KD, E_])
        raw_o = sb("raw_o", [P, 1, D])
        wyh, wyl = (sb(n, [P, KD, 2 * 4 * LAT], F32R) for n in ("wyh", "wyl"))
        wvh, wvl = (sb(n, [P, KD, LAT], F32R) for n in ("wvh", "wvl"))
        wrh, wrl = (sb(n, [P, KD, E_], F32R) for n in ("wrh", "wrl"))
        woh, wol = (sb(n, [P, 1, D], F32R) for n in ("woh", "wol"))
        yb = sb("yb", [P, 2 * QUADS])
        minus_lo = sb("minus_lo", [P, 2])
        vb, orow, rrow = sb("vb", [P, LAT]), sb("orow", [P, D]), sb("rrow", [P, E_])
        ocol = sb("ocol", [P, KD])
        rev = sb("rev", [P, E_])
        xc = sb("xc", [P, TT, D])
        xth, xtl = (sb(n, [P, KD, SEQ], F32R) for n in ("xth", "xtl"))
        y = sb("y", [P, 2, SEQ])
        yh = sb("yh", [P, 2, SEQ], F32R)
        stack = sb("stack", [P, 2 * QUADS, SEQ], F32R)
        v = sb("v", [P, TT, MH, 32])
        probs = sb("probs", [P, 2, TT, SEQ])
        rs = sb("rs", [P, MH, TT])
        ri = sb("ri", [P, TT, MH])
        mx = sb("mx", [P, MH, TT])
        pt = sb("pt", [P, 8, TT, SEQ])
        ot = sb("ot", [P, QUADS, SEQ])
        ao = sb("ao", [P, TT, LAT])
        ch, cl = (sb(n, [P, SEQ], F32R) for n in ("ch", "cl"))
        mt = sb("mt", [P, KD, SEQ])
        mth, mtl = (sb(n, [P, KD, SEQ], F32R) for n in ("mth", "mtl"))
        mo = sb("mo", [P, 2, D])
        small = lambda n: sb(n, [P, TT, E_])
        lg, ex, pr, eq, key_, oh1, p2, oh2, oh, wt, comb = (small(n) for n in ("lg", "ex", "pr", "eq", "key", "oh1", "p2", "oh2", "oh", "wt", "comb"))
        one = lambda n: sb(n, [P, TT, 1])
        lm, es, er, v1, k1, v2, k2, tw, tr = (one(n) for n in ("lm", "es", "er", "v1", "k1", "v2", "k2", "tw", "tr"))
        ps_s = ctx.enter_context(nc.psum_tensor(f"{name}_ps_s", [P, 4, SEQ], F32))
        ps_p = ctx.enter_context(nc.psum_tensor(f"{name}_ps_p", [P, 2, SEQ], F32))
        ps_m = ctx.enter_context(nc.psum_tensor(f"{name}_ps_m", [P, 2, SEQ], F32))
        weights_in, hi_split, weights_split, zeroed = sem("weights_in"), sem("hi_split"), sem("weights_split"), sem("zeroed")
        x_loaded, comb_stored = sem("x_loaded"), sem("comb_stored")
        stored = [sem(f"stored{k}") for k in range(2)]
        hold = gated_hold(sem("held"))

        pe_o = [("T", k) for k in range(KD)] + [("Y", n) for n in range(2 * QUADS)] + [("V", t) for t in range(TT)]
        dve_o = [(n, k) for k in range(KD) for n in ("XH", "XL")]
        for n in range(2 * QUADS + 1):
            if n < 2 * QUADS: dve_o.append(("YB", n))
            if n >= 1: dve_o.append(("YS", n - 1))
        pool_o = [("YH", n) for n in range(2 * QUADS)]
        dve_o += [("VB", t) for t in range(TT)]
        act_o = []
        for h in range(MH + 2):
            now, old = h < MH, 0 <= h - 1 < MH
            a = (h - 5) // 4 if h >= 5 and (h - 5) % 4 == 0 else None
            for t in range(3):
                if now:
                    pe_o.append(("S", h, t)); dve_o.append(("M", h, t)); act_o.append(("X", h, t))
            if old: dve_o.append(("I", h - 1))
            if a is not None:
                pe_o.append(("A", a)); act_o.append(("OT", a))
            if old:
                pe_o += [("P", h - 1, 0), ("P", h - 1, 1)]
                dve_o.append(("E", h - 1, 0)); act_o.append(("E", h - 1, 1))
            if now:
                pe_o.append(("S", h, 3)); dve_o.append(("M", h, 3)); act_o.append(("X", h, 3))
            if old:
                pe_o += [("P", h - 1, 2), ("P", h - 1, 3)]
                dve_o.append(("E", h - 1, 2)); act_o.append(("E", h - 1, 3))
        pe_o += [("BT", t) for t in range(TT)] + [("CT",)] + [("MT", c) for c in range(KD)] + [("MO", t) for t in range(TT)] + [("RL",)]
        dve_o += [("AO", t) for t in range(TT)] + [("CH",), ("CL",)] + [(n, c) for c in range(KD) for n in ("MB", "MH", "ML")]
        dve_o += [("MO", t) for t in range(TT)]
        ROUTE = ["LG", "LM", "LD"]
        ROUTE2 = ["ES", "ER", "PR", "V1", "EQ1", "KY1", "K1", "OH1", "P2", "V2", "EQ2", "KY2", "K2", "OH2", "OH", "TW", "TR", "WT", "COMB"]
        dve_o += [(n,) for n in ROUTE + ROUTE2]
        act_o += [("EX",)]
        pe_s, dve_s = Steps(sem("tensor_steps"), pe_o), Steps(sem("vector_steps"), dve_o)
        act_s, pool_s = Steps(sem("scalar_steps"), act_o), Steps(sem("gpsimd_steps"), pool_o)
        misc = [k for k in pe_o if k[0] not in ("S", "P")]
        assert len(misc) % 2 == 0, len(misc)
        bank = {k: n % 2 for n, k in enumerate(misc)}
        reader = {"T": (dve_s, "XL"), "Y": (dve_s, "YB"), "V": (dve_s, "VB"), "A": (act_s, "OT"), "BT": (dve_s, "AO"), "CT": (dve_s, "CL"),
                  "MT": (dve_s, "MB"), "MO": (dve_s, "MO"), "RL": (dve_s, "LG")}

        with nc.Block() as block:

            @block.sync
            def _(sp):
                for k in range(2):
                    sp.sem_inc(stored[k], 32)
                sp.sem_inc(comb_stored, 16)
                loads = [(raw_y[:, :, :], w["stacks"].rearrange("(k p) n -> p k n", p=P)), (raw_v[:, :, :], w["v_w"].rearrange("(k p) n -> p k n", p=P)),
                         (raw_r[:, :, :], w["router_w"].rearrange("(k p) n -> p k n", p=P)), (raw_o[:, 0, :], w["o_w"][0:P, :]),
                         (yb[:, :], w["stack_b"]), (minus_lo[:, :], w["minus_lo"]), (vb[:, :], w["v_b"].partition_broadcast(P)),
                         (orow[:, :], w["o_b"].partition_broadcast(P)), (rrow[:, :], w["router_b"].partition_broadcast(P)),
                         (ocol[:, :], w["o_b_cols"]), (rev[:, :], w["rev"].partition_broadcast(P))]
                for dst, src in loads:
                    sp.dma_start(dst, src).then_inc(weights_in, 16)
                with sp.Fori(0, BATCH) as i:
                    hold(sp, pe_s.sem, pe_s.before(i, "T", KD - 1))
                    sp.dma_start(xc[:, :, :], x_in[bass.ds(i, 1), :, :].rearrange("o (t p) d -> p (o t) d", p=P)).then_inc(x_loaded, 16)
                    for t in range(TT):
                        hold(sp, dve_s.sem, dve_s.at(i, "MO", t))
                        sp.dma_start(m_out[bass.ds(i, 1), P * t:P * t + P, :].rearrange("o p d -> p (o d)"), mo[:, t % 2, :]).then_inc(stored[t % 2], 16)
                    hold(sp, dve_s.sem, dve_s.at(i, "COMB"))
                    sp.dma_start(comb_out[bass.ds(i, 1), :, :].rearrange("o (t p) e -> p (o t) e", p=P), comb[:, :, :]).then_inc(comb_stored, 16)
                for k in range(2):
                    hold(sp, stored[k], 32 * BATCH + 32)
                hold(sp, comb_stored, 16 * BATCH + 16)

            @block.tensor
            def _(pe):
                pe.sem_inc(pe_s.sem, pe_s.per)
                pe.wait_ge(weights_split, 4)
                pe.wait_ge(zeroed, 1)
                with pe.Fori(0, BATCH) as i:
                    for key in pe_o:
                        kind = key[0]
                        if kind not in ("S", "P"):
                            n = misc.index(key)
                            was = misc[n - 2]
                            steps, rk = reader[was[0]]
                            pe.wait_ge(steps.sem, (steps.at if n >= 2 else steps.before)(i, rk, *was[1:]))
                            m = ps_m[:, bank[key], :]
                        if kind == "T":
                            k = key[1]
                            if k == 0:
                                pe.wait_ge(x_loaded, 16 * i + 16)
                            for t in range(TT):
                                last = nc.tensor.transpose(m[:, P * t:P * t + P], xc[:, t, P * k:P * k + P], ident[:, :])
                        elif kind == "Y":
                            n = key[1]
                            if n == 0:
                                pe.wait_ge(dve_s.sem, dve_s.at(i, "XL", KD - 1))
                            cols = slice(P * n, P * n + P)
                            last = sum_of_parts(nc, m, lambda k: wyh[:, k, cols], lambda k: wyl[:, k, cols], lambda k: xth[:, k, :], lambda k: xtl[:, k, :], KD)
                        elif kind == "V":
                            tok = slice(P * key[1], P * key[1] + P)
                            last = sum_of_parts(nc, m[:, 0:LAT], lambda k: xth[:, k, tok], lambda k: xtl[:, k, tok], lambda k: wvh[:, k, :], lambda k: wvl[:, k, :], KD)
                        elif kind == "S":
                            h, t = key[1:]
                            a, rows = h // 4, slice(32 * (h % 4), 32 * (h % 4) + 32)
                            if h == 0 and t == 0:
                                pe.wait_ge(dve_s.sem, dve_s.at(i, "YS", 2 * QUADS - 1))
                            pe.wait_ge(act_s.sem, act_s.at(i, "X", h - 1, t) if h else act_s.before(i, "X", MH - 1, t))
                            last = nc.tensor.matmul(ps_s[:, t, :], stack[rows, QUADS + a, P * t:P * t + P], stack[rows, a, :], start=True, stop=True)
                        elif kind == "P":
                            h, j = key[1:]
                            if j == 0:
                                pe.wait_ge(act_s.sem, act_s.at(i, "X", h, 3))
                            if (h, j) == (0, 0):
                                pe.wait_ge(dve_s.sem, dve_s.before(i, "E", MH - 1, 2))
                            elif (h, j) == (0, 1):
                                pe.wait_ge(act_s.sem, act_s.before(i, "E", MH - 1, 3))
                            else:
                                ph, pj = (h, j - 2) if j >= 2 else (h - 1, j + 2)
                                s_ = dve_s if pj % 2 == 0 else act_s
                                pe.wait_ge(s_.sem, s_.at(i, "E", ph, pj))
                            for t in range(TT):
                                last = nc.tensor.transpose(ps_p[:, j % 2, P * t:P * t + P], probs[:, h % 2, t, P * j:P * j + P], ident[:, :])
                        elif kind == "A":
                            a = key[1]
                            pe.wait_ge(dve_s.sem, dve_s.at(i, "VB", TT - 1))
                            pe.wait_ge(dve_s.sem, dve_s.at(i, "E", 4 * a + 3, 2))
                            pe.wait_ge(act_s.sem, act_s.at(i, "E", 4 * a + 3, 3))
                            for j in range(TT):
                                for s in range(4):
                                    last = nc.tensor.matmul(m[32 * s:32 * s + 32, :], v[:, j, 4 * a + s, :], pt[:, (4 * a + s) % 8, j, :], start=(j == 0), stop=(j == TT - 1), tile_position=(0, 32 * s))
                        elif kind == "BT":
                            t = key[1]
                            pe.wait_ge(act_s.sem, act_s.at(i, "OT", QUADS - 1))
                            for a in range(QUADS):
                                last = nc.tensor.transpose(m[:, P * a:P * a + P], ot[:, a, P * t:P * t + P], ident[:, :])
                        elif kind == "CT":
                            pe.wait_ge(dve_s.sem, dve_s.at(i, "AO", TT - 1))
                            for t in range(TT):
                                last = nc.tensor.transpose(m[:, P * t:P * t + P], ao[:, t, :], ident[:, :])
                        elif kind == "MT":
                            c = key[1]
                            pe.wait_ge(dve_s.sem, dve_s.at(i, "CL"))
                            cols = slice(P * c, P * c + P)
                            last = sum_of_parts(nc, m, lambda k: woh[:, k, cols], lambda k: wol[:, k, cols], lambda k: ch[:, :], lambda k: cl[:, :], 1)
                        elif kind == "MO":
                            tok = slice(P * key[1], P * key[1] + P)
                            last = sum_of_parts(nc, m[:, 0:D], lambda k: ch[:, tok], lambda k: cl[:, tok], lambda k: woh[:, k, :], lambda k: wol[:, k, :], 1)
                        elif kind == "RL":
                            pe.wait_ge(dve_s.sem, dve_s.at(i, "ML", KD - 1))
                            for t in range(TT):
                                tok = slice(P * t, P * t + P)
                                last = sum_of_parts(nc, m[:, E_ * t:E_ * t + E_], lambda k: mth[:, k, tok], lambda k: mtl[:, k, tok], lambda k: wrh[:, k, :], lambda k: wrl[:, k, :], KD)
                        last.then_inc(pe_s.sem, 1)

            flat = lambda x: x[:, :, :].rearrange("p k n -> p (k n)")
            splits = ((raw_y, wyh, wyl), (raw_v, wvh, wvl), (raw_r, wrh, wrl), (raw_o, woh, wol))

            @block.vector
            def _(dve):
                dve.sem_inc(dve_s.sem, dve_s.per)
                nc.vector.memset(v[:, :, :, :], 0.0).then_inc(zeroed, 1)
                dve.wait_ge(zeroed, 1)
                for n, (raw, hi, lo) in enumerate(splits):
                    dve.wait_ge(hi_split, n + 1)
                    nc.vector.tensor_tensor(flat(lo), flat(raw), flat(hi).bitcast(F32), ALU.subtract).then_inc(weights_split, 1)
                vv = nc.vector
                per_token = lambda s: s[:, :, :].broadcast_to([P, TT, E_])
                per_expert = lambda s: s[:, :].unsqueeze(1).broadcast_to([P, TT, E_])
                A3 = lambda s: s[:, :, :]
                route = {
                    "LM": lambda: vv.tensor_reduce(out=A3(lm), in_=A3(lg), axis=AX.X, op=ALU.max),
                    "LD": lambda: vv.tensor_tensor(A3(ex), A3(lg), per_token(lm), ALU.subtract),
                    "ES": lambda: vv.tensor_reduce(out=A3(es), in_=A3(pr), axis=AX.X, op=ALU.add),
                    "ER": lambda: vv.reciprocal(A3(er), A3(es)),
                    "PR": lambda: vv.tensor_tensor(A3(wt), A3(pr), per_token(er), ALU.mult),
                    "V1": lambda: vv.tensor_reduce(out=A3(v1), in_=A3(wt), axis=AX.X, op=ALU.max),
                    "EQ1": lambda: vv.tensor_tensor(A3(eq), A3(wt), per_token(v1), ALU.is_equal),
                    "KY1": lambda: vv.tensor_tensor(A3(key_), A3(eq), per_expert(rev), ALU.mult),
                    "K1": lambda: vv.tensor_reduce(out=A3(k1), in_=A3(key_), axis=AX.X, op=ALU.max),
                    "OH1": lambda: vv.tensor_tensor(A3(oh1), per_expert(rev), per_token(k1), ALU.is_equal),
                    "P2": lambda: vv.scalar_tensor_tensor(out=A3(p2), in0=A3(oh1), scalar=-2.0, in1=A3(wt), op0=ALU.mult, op1=ALU.add),
                    "V2": lambda: vv.tensor_reduce(out=A3(v2), in_=A3(p2), axis=AX.X, op=ALU.max),
                    "EQ2": lambda: vv.tensor_tensor(A3(eq), A3(p2), per_token(v2), ALU.is_equal),
                    "KY2": lambda: vv.tensor_tensor(A3(key_), A3(eq), per_expert(rev), ALU.mult),
                    "K2": lambda: vv.tensor_reduce(out=A3(k2), in_=A3(key_), axis=AX.X, op=ALU.max),
                    "OH2": lambda: vv.tensor_tensor(A3(oh2), per_expert(rev), per_token(k2), ALU.is_equal),
                    "OH": lambda: vv.tensor_tensor(A3(oh), A3(oh1), A3(oh2), ALU.add),
                    "TW": lambda: vv.scalar_tensor_tensor(out=A3(tw), in0=A3(v1), scalar=1e-8, in1=A3(v2), op0=ALU.add, op1=ALU.add),
                    "TR": lambda: vv.reciprocal(A3(tr), A3(tw)),
                    "WT": lambda: vv.tensor_tensor(A3(p2), A3(wt), A3(oh), ALU.mult),
                    "COMB": lambda: vv.tensor_tensor(A3(comb), A3(p2), per_token(tr), ALU.mult),
                }
                with dve.Fori(0, BATCH) as i:
                    for n_, key in enumerate(dve_o):
                        kind = key[0]
                        if kind == "XH":
                            k = key[1]
                            dve.wait_ge(pe_s.sem, pe_s.at(i, "T", k))
                            if k == 0:
                                dve.wait_ge(pe_s.sem, pe_s.before(i, "V", TT - 1))
                            op = vv.tensor_copy(xth[:, k, :], ps_m[:, bank["T", k], :])
                        elif kind == "XL":
                            k = key[1]
                            dve.wait_ge(dve_s.sem, dve_s.at(i, "XH", k))
                            op = vv.tensor_tensor(xtl[:, k, :], ps_m[:, bank["T", k], :], xth[:, k, :].bitcast(F32), ALU.subtract)
                        elif kind == "YB":
                            n = key[1]
                            dve.wait_ge(pe_s.sem, pe_s.at(i, "Y", n))
                            dve.wait_ge(dve_s.sem, dve_s.at(i, "YS", n - 2) if n >= 2 else dve_s.before(i, "YS", n + 2 * QUADS - 2))
                            op = vv.tensor_scalar(y[:, n % 2, :], ps_m[:, bank["Y", n], :], yb[:, n:n + 1], 1.0 if n < QUADS else KPH ** -0.5, ALU.add, ALU.mult)
                        elif kind == "YS":
                            n = key[1]
                            dve.wait_ge(pool_s.sem, pool_s.at(i, "YH", n))
                            if n == 0:
                                dve.wait_ge(pe_s.sem, pe_s.before(i, "S", MH - 1, 3))
                            op = vv.scalar_tensor_tensor(out=stack[:, n, :], in0=yh[:, n % 2, :].bitcast(F32), scalar=minus_lo[:, n // QUADS:n // QUADS + 1],
                                                         in1=y[:, n % 2, :], op0=ALU.mult, op1=ALU.add)
                        elif kind == "VB":
                            t = key[1]
                            dve.wait_ge(pe_s.sem, pe_s.at(i, "V", t))
                            if t == 0:
                                dve.wait_ge(pe_s.sem, pe_s.before(i, "A", QUADS - 1))
                            op = vv.tensor_tensor(v[:, t, :, 0:KPH], ps_m[:, bank["V", t], 0:LAT].rearrange("p (h e) -> p h e", e=KPH),
                                                  vb[:, :].rearrange("p (h e) -> p h e", e=KPH), ALU.add)
                        elif kind == "M":
                            h, t = key[1:]
                            dve.wait_ge(pe_s.sem, pe_s.at(i, "S", h, t))
                            if t == 0:
                                dve.wait_ge(act_s.sem, act_s.before(i, "X", h, TT - 1))
                            op = vv.tensor_reduce(out=mx[:, h, t:t + 1], in_=ps_s[:, t, :], axis=AX.X, op=ALU.max, negate=True)
                        elif kind == "I":
                            h = key[1]
                            dve.wait_ge(act_s.sem, act_s.at(i, "X", h, TT - 1))
                            if h == 0:
                                dve.wait_ge(dve_s.sem, dve_s.before(i, "AO", TT - 1))
                            op = vv.reciprocal(ri[:, :, h], rs[:, h, :])
                        elif kind == "E":
                            h, j = key[1:]
                            dve.wait_ge(pe_s.sem, pe_s.at(i, "P", h, j))
                            if j == 0 and h % 4 == 0:
                                a = h // 4
                                dve.wait_ge(pe_s.sem, pe_s.at(i, "A", a - 2) if a >= 2 else pe_s.before(i, "A", a + QUADS - 2))
                            op = vv.tensor_copy(pt[:, h % 8, j, :], ps_p[:, j % 2, :])
                        elif kind == "AO":
                            t = key[1]
                            dve.wait_ge(pe_s.sem, pe_s.at(i, "BT", t))
                            if t == 0:
                                dve.wait_ge(dve_s.sem, dve_s.at(i, "I", MH - 1))
                                dve.wait_ge(pe_s.sem, pe_s.before(i, "CT"))
                            op = vv.tensor_tensor(ao[:, t, :].rearrange("p (h e) -> p h e", e=KPH),
                                                  ps_m[:, bank["BT", t], :].rearrange("p (h e) -> p h e", e=32)[:, :, 0:KPH],
                                                  ri[:, t, :].unsqueeze(2).broadcast_to([P, MH, KPH]), ALU.mult)
                        elif kind == "CH":
                            dve.wait_ge(pe_s.sem, pe_s.at(i, "CT"))
                            dve.wait_ge(pe_s.sem, pe_s.before(i, "MO", TT - 1))
                            op = vv.tensor_copy(ch[:, :], ps_m[:, bank["CT",], :])
                        elif kind == "CL":
                            dve.wait_ge(dve_s.sem, dve_s.at(i, "CH"))
                            op = vv.tensor_tensor(cl[:, :], ps_m[:, bank["CT",], :], ch[:, :].bitcast(F32), ALU.subtract)
                        elif kind == "MB":
                            c = key[1]
                            dve.wait_ge(pe_s.sem, pe_s.at(i, "MT", c))
                            hold(dve, dve_s.sem, dve_s.before(i, "ML", c))
                            op = vv.tensor_scalar(mt[:, c, :], ps_m[:, bank["MT", c], :], ocol[:, c:c + 1], None, ALU.add)
                        elif kind == "MH":
                            c = key[1]
                            dve.wait_ge(dve_s.sem, dve_s.at(i, "MB", c))
                            if c == 0:
                                dve.wait_ge(pe_s.sem, pe_s.before(i, "RL"))
                            op = vv.tensor_copy(mth[:, c, :], mt[:, c, :])
                        elif kind == "ML":
                            c = key[1]
                            dve.wait_ge(dve_s.sem, dve_s.at(i, "MH", c))
                            op = vv.tensor_tensor(mtl[:, c, :], mt[:, c, :], mth[:, c, :].bitcast(F32), ALU.subtract)
                        elif kind == "MO":
                            t = key[1]
                            dve.wait_ge(pe_s.sem, pe_s.at(i, "MO", t))
                            dve.wait_ge(stored[t % 2], 32 * i + 16 * (t // 2) + 32)
                            op = vv.tensor_tensor(mo[:, t % 2, :], ps_m[:, bank["MO", t], 0:D], orow[:, :], ALU.add)
                        elif kind == "LG":
                            dve.wait_ge(pe_s.sem, pe_s.at(i, "RL"))
                            dve.wait_ge(dve_s.sem, dve_s.before(i, "COMB"))
                            op = vv.tensor_tensor(A3(lg), ps_m[:, bank["RL",], 0:TT * E_].rearrange("p (t e) -> p t e", e=E_), per_expert(rrow), ALU.add)
                        else:
                            if kind == "LD":
                                dve.wait_ge(act_s.sem, act_s.before(i, "EX"))
                            if kind == "ES":
                                dve.wait_ge(act_s.sem, act_s.at(i, "EX"))
                            if kind == "COMB":
                                dve.wait_ge(comb_stored, 16 * i + 16)
                            dve.wait_ge(dve_s.sem, dve_s.at(i, *dve_o[n_ - 1]))
                            op = route[kind]()
                        op.then_inc(dve_s.sem, 1)

            @block.scalar
            def _(act):
                act.sem_inc(act_s.sem, act_s.per)
                act.wait_ge(weights_in, 16 * 11)
                for raw, hi, _ in splits:
                    nc.scalar.copy(flat(hi), flat(raw)).then_inc(hi_split, 1)
                with act.Fori(0, BATCH) as i:
                    for key in act_o:
                        kind = key[0]
                        if kind == "X":
                            h, t = key[1:]
                            act.wait_ge(dve_s.sem, dve_s.at(i, "M", h, t))
                            if t == 0:
                                act.wait_ge(pe_s.sem, pe_s.at(i, "P", h - 2, TT - 1) if h >= 2 else pe_s.before(i, "P", h + MH - 2, TT - 1))
                                act.wait_ge(dve_s.sem, dve_s.before(i, "I", h))
                            op = nc.scalar.activation(probs[:, h % 2, t, :], ps_s[:, t, :], ACT.Exp, bias=mx[:, h, t:t + 1], scale=1.0, accum_out=rs[:, h, t:t + 1])
                        elif kind == "E":
                            h, j = key[1:]
                            act.wait_ge(pe_s.sem, pe_s.at(i, "P", h, j))
                            if j == 1 and h % 4 == 0:
                                a = h // 4
                                act.wait_ge(pe_s.sem, pe_s.at(i, "A", a - 2) if a >= 2 else pe_s.before(i, "A", a + QUADS - 2))
                            op = nc.scalar.copy(pt[:, h % 8, j, :], ps_p[:, j % 2, :])
                        elif kind == "OT":
                            a = key[1]
                            act.wait_ge(pe_s.sem, pe_s.at(i, "A", a))
                            act.wait_ge(pe_s.sem, pe_s.before(i, "BT", TT - 1))
                            op = nc.scalar.copy(ot[:, a, :], ps_m[:, bank["A", a], :])
                        elif kind == "EX":
                            act.wait_ge(dve_s.sem, dve_s.at(i, "LD"))
                            op = nc.scalar.activation(pr[:, :, :].rearrange("p t e -> p (t e)"), ex[:, :, :].rearrange("p t e -> p (t e)"), ACT.Exp)
                        op.then_inc(act_s.sem, 1)

            @block.gpsimd
            def _(pool):
                pool.sem_inc(pool_s.sem, pool_s.per)
                with pool.Fori(0, BATCH) as i:
                    for _, n in pool_o:
                        hold(pool, dve_s.sem, dve_s.at(i, "YB", n))
                        hold(pool, dve_s.sem, dve_s.at(i, "YS", n - 2) if n >= 2 else dve_s.before(i, "YS", n + 2 * QUADS - 2))
                        nc.gpsimd.tensor_copy(yh[:, n % 2, :], y[:, n % 2, :]).then_inc(pool_s.sem, 1)


def dense_experts(nc, const, x_in, m_in, comb_in, w1, b1, w2, b2, x_out, name):
    F = w1.shape[2]
    FT = F // P
    ctx = ExitStack()
    with ctx:
        sb = lambda n, s, dt=F32: ctx.enter_context(nc.sbuf_tensor(f"{name}_{n}", s, dt))
        sem = lambda n: ctx.enter_context(nc.semaphore(f"{name}_{n}"))
        ident = const["ident"]
        w1h, w1l = (sb(n, [P, E_, KD, F], F32R) for n in ("w1h", "w1l"))
        w2h, w2l = (sb(n, [P, E_, FT, D], F32R) for n in ("w2h", "w2l"))
        b1c = sb("b1c", [P, E_, FT])
        b2r = sb("b2r", [E_, D])
        work = sb("work", [P, 4, TT * D])
        xc, mc, xb, acc = (work[:, n, :].rearrange("p (t d) -> p t d", d=D) for n in range(4))
        comb = sb("comb", [P, TT, E_])
        combt = sb("combt", [E_, SEQ])
        xth, xtl = (sb(n, [P, KD, SEQ], F32R) for n in ("xth", "xtl"))
        g = sb("g", [P, 2, SEQ])
        gh, gl = (sb(n, [P, 2, FT, SEQ], F32R) for n in ("gh", "gl"))
        st6, mv, vare, rstd = sb("st6", [P, TT, 6]), sb("mv", [P, TT, 2]), sb("vare", [P, TT, 1]), sb("rstd", [P, TT, 1])
        ps = ctx.enter_context(nc.psum_tensor(f"{name}_ps", [P, 8, SEQ], F32))
        small_in, staged, hi_split, lo_split = sem("small_in"), [sem(f"staged{k}") for k in range(4)], sem("hi_split"), sem("lo_split")
        x_loaded, stored = sem("x_loaded"), sem("stored")
        hold = gated_hold(sem("held"))

        pe_o = [("T", k) for k in range(KD)] + [("C", n) for n in range(2)] + [("Z", t) for t in range(TT)]
        dve_o = [(n, k) for k in range(KD) for n in ("XH", "XL")] + [("CC", n) for n in range(2)] + [("XB",)] + [("ZA", t) for t in range(TT)]
        act_o, pool_o = [], []
        for e in range(E_ + 1):
            if e < E_:
                pe_o += [("H", e, m) for m in range(FT)]
                act_o += [("G", e, m) for m in range(FT)]
                dve_o += [(n, e, m) for m in range(FT) for n in ("GH", "GL")]
            if e >= 1:
                pe_o += [("Y", e - 1, t) for t in range(TT)]
                dve_o += [("AC", e - 1, t) for t in range(TT)]
        for t in range(TT):
            dve_o += [("F", t)]
        for t in range(TT):
            dve_o += [("B", t)]
        for t in range(TT):
            dve_o += [("S", t)]
        pool_o += [("EPS",), ("RSTD",)]
        dve_o += [("N", t) for t in range(TT)]
        pe_s, dve_s = Steps(sem("tensor_steps"), pe_o), Steps(sem("vector_steps"), dve_o)
        act_s, pool_s = Steps(sem("scalar_steps"), act_o), Steps(sem("gpsimd_steps"), pool_o)
        BANKS = 8
        assert len(pe_o) % BANKS == 0, len(pe_o)
        bank = {k: n % BANKS for n, k in enumerate(pe_o)}
        reader = {"T": (dve_s, "XL"), "C": (dve_s, "CC"), "Z": (dve_s, "ZA"), "H": (act_s, "G"), "Y": (dve_s, "AC")}
        pieces = [(e, n) for e in range(E_) for n in range(2)]

        def piece(e, n):
            raw = work[:, (2 * e + n) % 4, :]
            hi, lo = ((w1h, w1l), (w2h, w2l))[n]
            f = lambda x: x[:, e, :, :].rearrange("p k n -> p (k n)")
            return raw, f(hi), f(lo)

        with nc.Block() as block:

            @block.sync
            def _(sp):
                sp.sem_inc(stored, 64)
                sp.dma_start(b1c[:, :, :], b1).then_inc(small_in, 16)
                sp.dma_start(b2r[:, :], b2).then_inc(small_in, 16)
                for c, (e, n) in enumerate(pieces):
                    if c >= 4:
                        hold(sp, lo_split, c - 3)
                    src = (w1, w2)[n][e].rearrange("(k p) n -> p k n", p=P)
                    sp.dma_start(piece(e, n)[0].rearrange("p (k n) -> p k n", n=src.shape[2]), src).then_inc(staged[c % 4], 16)
                hold(sp, lo_split, len(pieces))
                with sp.Fori(0, BATCH) as i:
                    hold(sp, dve_s.sem, dve_s.before(i, "AC", E_ - 1, TT - 1))
                    tok = "o (t p) d -> p (o t) d"
                    sp.dma_start(mc, m_in[bass.ds(i, 1), :, :].rearrange(tok, p=P)).then_inc(x_loaded, 16)
                    sp.dma_start(xc, x_in[bass.ds(i, 1), :, :].rearrange(tok, p=P)).then_inc(x_loaded, 16)
                    sp.dma_start(comb[:, :, :], comb_in[bass.ds(i, 1), :, :].rearrange(tok, p=P)).then_inc(x_loaded, 16)
                    for t in range(TT):
                        hold(sp, dve_s.sem, dve_s.at(i, "N", t))
                        sp.dma_start(x_out[bass.ds(i, 1), P * t:P * t + P, :].rearrange("o p d -> p (o d)"), acc[:, t, :]).then_inc(stored, 16)
                hold(sp, stored, 64 * BATCH + 64)

            @block.tensor
            def _(pe):
                pe.sem_inc(pe_s.sem, pe_s.per)
                pe.wait_ge(lo_split, len(pieces))
                with pe.Fori(0, BATCH) as i:
                    for n, key in enumerate(pe_o):
                        kind = key[0]
                        m = ps[:, bank[key], :]
                        was = pe_o[n - BANKS]
                        steps, rk = reader[was[0]]
                        pe.wait_ge(steps.sem, (steps.at if n >= BANKS else steps.before)(i, rk, *was[1:]))
                        if kind == "T":
                            if key[1] == 0:
                                pe.wait_ge(x_loaded, 48 * i + 48)
                            for t in range(TT):
                                last = nc.tensor.transpose(m[:, P * t:P * t + P], mc[:, t, P * key[1]:P * key[1] + P], ident[:, :])
                        elif kind == "C":
                            for t in (2 * key[1], 2 * key[1] + 1):
                                last = nc.tensor.transpose(m[0:E_, P * (t % 2):P * (t % 2) + P], comb[:, t, :], ident[:, :])
                        elif kind == "Z":
                            t = key[1]
                            if t == 0:
                                pe.wait_ge(dve_s.sem, dve_s.at(i, "CC", 1))
                                pe.wait_ge(small_in, 32)
                            last = nc.tensor.matmul(m[:, 0:D], combt[:, P * t:P * t + P], b2r[:, :], start=True, stop=True)
                        elif kind == "H":
                            e, f = key[1:]
                            if (e, f) == (0, 0):
                                pe.wait_ge(dve_s.sem, dve_s.at(i, "XL", KD - 1))
                            cols = slice(P * f, P * f + P)
                            last = sum_of_parts(nc, m, lambda k: w1h[:, e, k, cols], lambda k: w1l[:, e, k, cols], lambda k: xth[:, k, :], lambda k: xtl[:, k, :], KD)
                        elif kind == "Y":
                            e, t = key[1:]
                            tok = slice(P * t, P * t + P)
                            if t == 0:
                                pe.wait_ge(dve_s.sem, dve_s.at(i, "GL", e, FT - 1))
                            last = sum_of_parts(nc, m[:, 0:D], lambda k: gh[:, e % 2, k, tok], lambda k: gl[:, e % 2, k, tok], lambda k: w2h[:, e, k, :], lambda k: w2l[:, e, k, :], FT)
                        last.then_inc(pe_s.sem, 1)

            @block.vector
            def _(dve):
                dve.sem_inc(dve_s.sem, dve_s.per)
                for c, (e, n) in enumerate(pieces):
                    raw, hi, lo = piece(e, n)
                    dve.wait_ge(hi_split, c + 1)
                    nc.vector.tensor_tensor(lo, raw, hi.bitcast(F32), ALU.subtract).then_inc(lo_split, 1)
                with dve.Fori(0, BATCH) as i:
                    for key in dve_o:
                        kind = key[0]
                        t = k = key[-1]
                        if kind == "XH":
                            dve.wait_ge(pe_s.sem, pe_s.at(i, "T", k))
                            if k == 0:
                                dve.wait_ge(pe_s.sem, pe_s.before(i, "H", E_ - 1, FT - 1))
                            op = nc.vector.tensor_copy(xth[:, k, :], ps[:, bank["T", k], :])
                        elif kind == "XL":
                            dve.wait_ge(dve_s.sem, dve_s.at(i, "XH", k))
                            op = nc.vector.tensor_tensor(xtl[:, k, :], ps[:, bank["T", k], :], xth[:, k, :].bitcast(F32), ALU.subtract)
                        elif kind == "CC":
                            dve.wait_ge(pe_s.sem, pe_s.at(i, "C", k))
                            dve.wait_ge(pe_s.sem, pe_s.before(i, "Z", TT - 1))
                            op = nc.vector.tensor_copy(combt[:, 2 * P * k:2 * P * k + 2 * P], ps[0:E_, bank["C", k], 0:2 * P])
                        elif kind == "XB":
                            dve.wait_ge(dve_s.sem, dve_s.before(i, "N", TT - 1))
                            op = nc.vector.tensor_scalar(xb, xc, 2.0, None, ALU.mult)
                        elif kind == "ZA":
                            dve.wait_ge(pe_s.sem, pe_s.at(i, "Z", t))
                            if t == 0:
                                dve.wait_ge(stored, 64 * i + 64)
                            op = nc.vector.tensor_copy(acc[:, t, :], ps[:, bank["Z", t], 0:D])
                        elif kind == "GH":
                            e, m = key[1:]
                            dve.wait_ge(act_s.sem, act_s.at(i, "G", e, m))
                            if m == 0:
                                dve.wait_ge(pe_s.sem, pe_s.at(i, "Y", e - 2, TT - 1) if e >= 2 else pe_s.before(i, "Y", e + E_ - 2, TT - 1))
                            op = nc.vector.tensor_copy(gh[:, e % 2, m, :], g[:, m % 2, :])
                        elif kind == "GL":
                            e, m = key[1:]
                            dve.wait_ge(dve_s.sem, dve_s.at(i, "GH", e, m))
                            op = nc.vector.tensor_tensor(gl[:, e % 2, m, :], g[:, m % 2, :], gh[:, e % 2, m, :].bitcast(F32), ALU.subtract)
                        elif kind == "AC":
                            e = key[1]
                            dve.wait_ge(pe_s.sem, pe_s.at(i, "Y", e, t))
                            dve.wait_ge(dve_s.sem, dve_s.at(i, "AC", e - 1, t) if e else dve_s.at(i, "ZA", t))
                            op = nc.vector.scalar_tensor_tensor(out=acc[:, t, :], in0=ps[:, bank[("Y", e, t)], 0:D], scalar=comb[:, t, e:e + 1], in1=acc[:, t, :], op0=ALU.mult, op1=ALU.add)
                        elif kind == "F":
                            dve.wait_ge(dve_s.sem, dve_s.at(i, "AC", E_ - 1, t))
                            op = nc.vector.scalar_tensor_tensor(out=xb[:, t, :], in0=acc[:, t, :], scalar=0.3, in1=xb[:, t, :], op0=ALU.mult, op1=ALU.add)
                        elif kind == "B":
                            dve.wait_ge(dve_s.sem, dve_s.at(i, "F", t))
                            op = nc.vector.bn_stats(st6[:, t, :], xb[:, t, :])
                        elif kind == "S":
                            hold(dve, dve_s.sem, dve_s.at(i, "B", t))
                            op = nc.vector.bn_aggr(mv[:, t, :], st6[:, t, :])
                        elif kind == "N":
                            dve.wait_ge(pool_s.sem, pool_s.at(i, "RSTD"))
                            op = nc.vector.tensor_scalar(acc[:, t, :], xb[:, t, :], mv[:, t, 0:1], rstd[:, t, :], ALU.subtract, ALU.mult)
                        op.then_inc(dve_s.sem, 1)

            @block.scalar
            def _(act):
                act.sem_inc(act_s.sem, act_s.per)
                for c, (e, n) in enumerate(pieces):
                    raw, hi, lo = piece(e, n)
                    act.wait_ge(staged[c % 4], 16 * (c // 4) + 16)
                    nc.scalar.copy(hi, raw).then_inc(hi_split, 1)
                act.wait_ge(small_in, 32)
                with act.Fori(0, BATCH) as i:
                    for _, e, m in act_o:
                        act.wait_ge(pe_s.sem, pe_s.at(i, "H", e, m))
                        n = FT * e + m - 2
                        act.wait_ge(dve_s.sem, dve_s.at(i, "GL", n // FT, n % FT) if n >= 0 else dve_s.before(i, "GL", E_ - 1, FT + n))
                        nc.scalar.activation(g[:, m % 2, :], ps[:, bank["H", e, m], :], ACT.Gelu, bias=b1c[:, e, m:m + 1], scale=1.0).then_inc(act_s.sem, 1)

            @block.gpsimd
            def _(pool):
                pool.sem_inc(pool_s.sem, pool_s.per)
                with pool.Fori(0, BATCH) as i:
                    hold(pool, dve_s.sem, dve_s.at(i, "S", TT - 1))
                    nc.gpsimd.tensor_scalar(vare[:, :, :], mv[:, :, 1:2], EPS, None, ALU.add).then_inc(pool_s.sem, 1)
                    hold(pool, pool_s.sem, pool_s.at(i, "EPS"))
                    hold(pool, dve_s.sem, dve_s.before(i, "N", TT - 1))
                    nc.gpsimd.tensor_tensor(rstd[:, :, :], vare[:, :, :], const["minus_half"][:, :].unsqueeze(1).broadcast_to([P, TT, 1]), ALU.pow).then_inc(pool_s.sem, 1)


def constants(nc, ctx, ident_in):
    ident = ctx.enter_context(nc.sbuf_tensor("ident", [P, P], F32))
    minus_half = ctx.enter_context(nc.sbuf_tensor("minus_half", [P, 1], F32))
    ready = ctx.enter_context(nc.semaphore("constants_ready"))
    with nc.Block() as block:

        @block.gpsimd
        def _(pool):
            nc.gpsimd.memset(minus_half[:, :], -0.5)
            nc.gpsimd.memset(ident[:, :], 0.0).then_inc(ready, 1)
            pool.wait_ge(ready, 1)
            nc.gpsimd.affine_select(out=ident[:, :], in_=ident[:, :], compare_op=ALU.not_equal, fill=1.0,
                                    base=0, pattern=[[-1, P]], channel_multiplier=1).then_inc(ready, 1)
            pool.wait_ge(ready, 2)
    return {"ident": ident, "minus_half": minus_half, "ready": ready, "count": 2}


def build(nc, a, out):
    ctx = ExitStack()
    with ctx:
        const = constants(nc, ctx, None)
        x1, x2, x3 = (nc.dram_tensor(n, [BATCH, SEQ, D], F32, kind="Internal").ap() for n in ("x1", "x2", "x3"))
        mla = {k[7:]: v for k, v in a.items() if k.startswith("L1_ffn_")}
        m4 = nc.dram_tensor("m4", [BATCH, SEQ, D], F32, kind="Internal").ap()
        c4 = nc.dram_tensor("c4", [BATCH, SEQ, E_], F32, kind="Internal").ap()
        attention(nc, const, a["L0_attn_x"], x1, a["L0_attn_Wq"], a["L0_attn_Wkv"], a["L0_attn_Wo"], a["L0_attn_bo"], a["rope0"], None, True, "soft")
        quantized_ffn(nc, const, x1, x2, a["gamma_beta"], a["L0_ffn_fc1_q"], a["L0_ffn_fc1_scales"], a["L0_ffn_fc1_bias"], a["L0_ffn_fc2_q"], a["L0_ffn_fc2_scales"], a["L0_ffn_fc2_bias"], "ffn")
        attention(nc, const, x2, x3, a["L1_attn_Wq"], a["L1_attn_Wkv"], a["L1_attn_Wo"], None, a["rope1"], a["decay"], False, "decay")
        latent_attention(nc, const, x3, m4, c4, mla, "mla")
        dense_experts(nc, const, x3, m4, c4, mla["w1"], mla["b1"], mla["w2"], mla["b2"], out, "moe")


def tables():
    f = np.float32
    inv = (f(1.0) / np.power(f(10000.0), np.arange(0, HD, 2, dtype=f) / f(HD))).astype(f)
    ang = (np.arange(SEQ, dtype=f)[:, None] * inv[None, :]).astype(f).T
    inv64 = 1.0 / 10000.0 ** (np.arange(0, HD, 2, dtype=np.float64) / HD)
    ang64 = np.outer(np.arange(SEQ, dtype=np.float64), inv64).T
    def pack(c, s):
        t = np.stack([-s, c, s], axis=1).astype(f)
        return np.ascontiguousarray(np.tile(t, (P // HALF, 1, 1)))
    slopes = np.array([2.0 ** (-8.0 / HEADS * (i + 1)) for i in range(HEADS)], f).astype(np.float64)
    dist = np.arange(SEQ)[None, :] - np.arange(P)[:, None]
    decay = np.where(dist[:, None, :] >= 0, np.exp(-slopes[None, :, None] * np.maximum(dist, 0)[:, None, :]), 0.0).astype(f)
    return {"rope0": pack(np.cos(ang), np.sin(ang)), "rope1": pack(np.cos(ang64), np.sin(ang64)), "decay": np.ascontiguousarray(decay)}


def halves_first(w):
    d, n = w.shape
    return w.reshape(d, n // (GRP * HD), GRP, 2, HALF).transpose(0, 1, 3, 2, 4).reshape(d, n)


def kernel(**inputs):
    import concourse.bacc as _bacc
    from concourse.bass_utils import run_bass_kernel_spmd as _run

    nc = _bacc.Bacc("TRN2", target_bir_lowering=False, num_devices=1)
    host = {k: np.asarray(v) for k, v in inputs.items()}
    host["L0_attn_Wq"] = halves_first(host["L0_attn_Wq"])
    kv = host["L0_attn_Wkv"]
    host["L0_attn_Wkv"] = np.concatenate([halves_first(kv[:, :KVH * HD]), kv[:, KVH * HD:]], axis=1)
    host["L1_attn_Wq"] = halves_first(host["L1_attn_Wq"].T)
    host["L1_attn_Wkv"] = np.concatenate([halves_first(host.pop("L1_attn_Wk").T), host.pop("L1_attn_Wv").T], axis=1)
    host["L1_attn_Wo"] = host["L1_attn_Wo"].T
    host["gamma_beta"] = np.stack([host["L0_ffn_ln_gamma"], host["L0_ffn_ln_beta"]]).reshape(2, KD, P).transpose(2, 0, 1)
    host["L0_ffn_fc1_bias"] = host["L0_ffn_fc1_bias"].reshape(-1, P).T
    qw, kw = host.pop("L1_ffn_q_w"), host.pop("L1_ffn_k_w")
    qb, kb = host.pop("L1_ffn_q_b"), host.pop("L1_ffn_k_b")
    def stacked(m, width):
        m = m.reshape(m.shape[0], MH, 1, width)[:, :, :, :KPH]
        return np.broadcast_to(m, (m.shape[0], MH, VAR, KPH)).reshape(m.shape[0], MH * VAR * KPH)
    host["L1_ffn_stacks"] = np.concatenate([stacked(kw, KPH), stacked(qw, D // MH)], axis=1)
    host["L1_ffn_stack_b"] = np.concatenate([stacked(kb[None], KPH), stacked(qb[None], D // MH)], axis=1).reshape(2 * QUADS, P).T
    lo = np.array([[0, 0, -1, -1], [0, -1, 0, -1]], np.float32)
    host["L1_ffn_minus_lo"] = np.tile(np.repeat(lo, KPH, axis=1), (1, P // (VAR * KPH))).T
    host["L1_ffn_o_b_cols"] = host["L1_ffn_o_b"].reshape(KD, P).T
    host["L1_ffn_rev"] = (E_ - np.arange(E_)).astype(np.float32)
    host["L1_ffn_b1"] = host["L1_ffn_b1"].reshape(E_, -1, P).transpose(2, 0, 1)
    host.update(tables())
    arrays, aps = {}, {}
    for k, v in host.items():
        arrays["in_" + k] = np.ascontiguousarray(v)
        aps[k] = nc.dram_tensor("in_" + k, arrays["in_" + k].shape, mybir.dt.from_np(arrays["in_" + k].dtype), kind="ExternalInput").ap()
    out = nc.dram_tensor("out_x", (BATCH, SEQ, D), F32, kind="ExternalOutput").ap()
    build(nc, aps, out)
    r = _run(nc, [arrays], core_ids=[0])
    return r.results[0]["out_x"]
```

```python
from contextlib import ExitStack

import numpy as np

import concourse.bass as bass
from concourse import mybir

F32 = mybir.dt.float32
F32R = mybir.dt.float32r
I32 = mybir.dt.int32
ACT = mybir.ActivationFunctionType
ALU = mybir.AluOpType
AX = mybir.AxisListType

P = 128
BATCH, SEQ, D = 8, 512, 256
TT = SEQ // P
KD = D // P
HEADS, KVH, HD = 16, 4, 64
GRP = HEADS // KVH
PAIRS = HEADS // 2
INNER = HEADS * HD
HALF = HD // 2
EPS = 1e-5


def gated_hold(nc_sem):
    def hold(eng, semaphore, value):
        eng.wait_ge(semaphore, value)
        eng.sem_inc(nc_sem, 1)
    return hold


class Steps:

    def __init__(self, ahead_sem, main_sem, ahead, main):
        self.where = {}
        for sem, order in ((ahead_sem, ahead), (main_sem, main)):
            for n, k in enumerate(order):
                assert k not in self.where, k
                self.where[k] = (sem, n + 1, len(order))
        self.starts = [(s, len(o)) for s, o in ((ahead_sem, ahead), (main_sem, main)) if o]

    def start(self, eng):
        for sem, count in self.starts:
            eng.sem_inc(sem, count)

    def sem(self, key):
        return self.where[key][0]

    def at(self, seq, *key):
        sem, pos, per = self.where[key]
        i, offset = seq
        return sem, i * per + (per * (offset + 1) + pos)


FIRST = (0, -1)


def shift(seq, n):
    return seq[0], seq[1] + n


def last_use(i, run, key, place, ahead, order):
    mine = place[key]
    for k in reversed(run[:run.index(key)]):
        if place.get(k) == mine:
            return [(shift(i, 1 if k in ahead else 0), k)]
    found = []
    if i is FIRST:
        return found
    for part, offset in ((lambda k: k not in ahead, -1), (lambda k: k in ahead, 0)):
        users = [k for k in order if place.get(k) == mine and part(k)]
        if users:
            found.append((shift(i, offset), users[-1]))
    return found


def sum_of_parts(nc, out, a_hi, a_lo, b_hi, b_lo, tiles, before_last=None):
    for k in range(tiles):
        if before_last and k == tiles - 1:
            before_last()
        for n, (a, b) in enumerate(((a_hi, b_hi), (a_hi, b_lo), (a_lo, b_hi))):
            last = nc.tensor.matmul(out, a(k), b(k), start=(k == 0 and n == 0), stop=(k == tiles - 1 and n == 2))
    return last


def turns(eng, run_steps, ahead_order, order, ahead):
    run_steps(FIRST, ahead_order)
    with eng.Fori(0, BATCH - 1) as i:
        run_steps((i, 0), order)
    run_steps((BATCH - 1, 0), [k for k in order if k not in ahead])


def attention(nc, const, x_in, x_out, w_q, w_kv, w_o, out_bias, rope_tab, decay_tab, softmax, name):
    ctx = ExitStack()
    with ctx:
        sb = lambda n, s, dt=F32: ctx.enter_context(nc.sbuf_tensor(f"{name}_{n}", s, dt))
        sem = lambda n: ctx.enter_context(nc.semaphore(f"{name}_{n}"))
        ident = const["ident"]
        KVW = KVH * HD
        HH = HEADS // 2
        wqh, wql = (sb(n, [P, KD, INNER], F32R) for n in ("wqh", "wql"))
        wkh, wkl = (sb(n, [P, KD, 2 * KVW], F32R) for n in ("wkh", "wkl"))
        woh, wol = (sb(n, [P, PAIRS, D], F32R) for n in ("woh", "wol"))
        if out_bias is not None:
            bias = sb("bias", [P, D])
        rope = sb("rope", [P, TT, 2, HD])
        xc = sb("xc", [P, TT, D])
        xb = sb("xb", [P, TT, D])
        xth, xtl = (sb(n, [P, KD, SEQ], F32R) for n in ("xth", "xtl"))
        rt = sb("rt", [P, 2, HH * HD])
        st = sb("st", [P, 2, HH * 2 * HD])
        qs = sb("qs", [P, HEADS, SEQ], F32R)
        ks = sb("ks", [P, 2, KVH, SEQ], F32R)
        v = sb("v", [P, 2, TT, KVW])
        first_q = [0 if softmax else P * j for j in range(TT)]
        head_cols = sum(SEQ - c for c in first_q)
        RING = 3
        pt = sb("pt", [P, RING * head_cols])
        if softmax:
            probs = sb("probs", [P, 2, TT, SEQ])
            rs = sb("rs", [P, HEADS, TT])
            ri = sb("ri", [P, TT, HEADS])
            mx = sb("mx", [P, HEADS, TT])
            rrep = sb("rrep", [P, SEQ])
        else:
            dec = sb("dec", [P, HEADS, SEQ])
        if softmax:
            ot = sb("ot", [P, SEQ])
        ath, atl = (sb(n, [P, PAIRS, SEQ], F32R) for n in ("ath", "atl"))
        r = sb("r", [P, 2, D])
        st6, mv, vare, rstd = sb("st6", [P, 2, 6]), sb("mv", [P, 2, 2]), sb("vare", [P, 2, 1]), sb("rstd", [P, 2, 1])
        ps_s = ctx.enter_context(nc.psum_tensor(f"{name}_ps_s", [P, 4, SEQ], F32))
        ps_p = ctx.enter_context(nc.psum_tensor(f"{name}_ps_p", [P, 2, SEQ], F32))
        ps_m = ctx.enter_context(nc.psum_tensor(f"{name}_ps_m", [P, 2, SEQ], F32))

        def weights_of(h, j):
            at = (h % RING) * head_cols + sum(SEQ - c for c in first_q[:j])
            return pt[:, at:at + SEQ - first_q[j]]

        def pairs_before(h):
            if h >= RING:
                return 0, (h - RING) // 2
            return -1, max(x for x in range(HEADS) if x % RING == h % RING) // 2

        weights_in, hi_split, weights_split = sem("weights_in"), sem("hi_split"), sem("weights_split")
        keys_scaled, decay_in = sem("keys_scaled"), sem("decay_in")
        x_loaded = sem("x_loaded")
        stored = [sem(f"stored{s}") for s in range(2)]
        hold = gated_hold(sem("held"))

        units = [("Q", 1, t) for t in range(TT)] + [("Q", 0, t) for t in range(TT)] + [("KV", t) for t in range(TT)]
        turned = lambda u: [("QT",) + u[1:] + (b,) for b in range(2)] if u[0] == "Q" else [("KT", u[1], b) for b in range(2)]
        pe_o, dve_o, act_o, pool_o = [], [], [], []

        def project(u):
            pe_o.append(u)
            dve_o.append(("ROT",) + u)
            if u[0] == "KV":
                dve_o.append(("VC", u[1]))
            pool_o.extend((n,) + u for n in ("Y0", "Y1", "HI", "LO"))

        def turn_over(u):
            pe_o.extend(turned(u))
            act_o.extend(("C",) + k for k in turned(u))

        aside = {}
        for t in range(TT):
            aside.setdefault(t, []).append((project, ("Q", 1, t)))
            aside.setdefault(t + 2, []).append((turn_over, ("Q", 1, t)))
            aside.setdefault(9 + t, []).append((project, ("Q", 0, t)))
            aside.setdefault(11 + t, []).append((turn_over, ("Q", 0, t)))
        for n, t in ((14, 0), (15, 1)):
            aside.setdefault(n, []).append((project, ("KV", t)))
        aside[16] = [(turn_over, ("KV", 0)), (project, ("KV", 2))]
        aside[17] = [(turn_over, ("KV", 1)), (project, ("KV", 3))]
        for h in range(HEADS + 2):
            now, old = h < HEADS, 0 <= h - 1 < HEADS
            lag = 3 if softmax else 2
            p = (h - lag) // 2 if h >= lag and (h - lag) % 2 == 0 and (h - lag) // 2 < PAIRS else None
            for t in range(3):
                if now:
                    pe_o.append(("S", h, t)); dve_o.append(("M", h, t))
                    if softmax: act_o.append(("X", h, t))
            if h == 8:
                pe_o += [("T", k) for k in range(KD)]
                dve_o += [(n, k) for k in range(KD) for n in ("XH", "XL")]
            if softmax and old: dve_o.append(("I", h - 1))
            if p is not None:
                if softmax:
                    pe_o.append(("R", p)); act_o.append(("RC", p))
                pe_o.append(("A", p))
                if not softmax: act_o.append(("RC", p))
            if softmax and old:
                pe_o += [("P", h - 1, 0), ("P", h - 1, 1)]
                dve_o.append(("E", h - 1, 0)); act_o.append(("E", h - 1, 1))
            if now:
                pe_o.append(("S", h, 3)); dve_o.append(("M", h, 3))
                if softmax: act_o.append(("X", h, 3))
            if softmax and old:
                pe_o += [("P", h - 1, 2), ("P", h - 1, 3)]
                dve_o.append(("E", h - 1, 2)); act_o.append(("E", h - 1, 3))
            if p is not None:
                dve_o.append(("O", p))
                if softmax: pool_o += [("OH", p), ("OL", p)]
            for what, u in aside.get(h, []):
                what(u)
        dve_o.append(("VV",))
        for t in range(TT + 1):
            if t < TT:
                pe_o.append(("W", t))
                if t < 2:
                    turn_over(("KV", 2 + t))
                dve_o += [("F", t), ("B", t), ("G", t)]; pool_o += [("EPS", t), ("RSTD", t)]
            if t >= 1: dve_o.append(("N", t - 1))
        dve_o.append(("XB",))
        is_ahead = lambda k: (k[0] in ("T", "XH", "XL", "KV", "KT", "VC", "VV", "XB") or k[:2] in (("Q", 0), ("QT", 0))
                              or k[1:3] in (("Q", 0), ("QT", 0)) or k[1:2] in (("KV",), ("KT",)))
        S = {}
        ahead = {}
        for eng_name, o in (("tensor", pe_o), ("vector", dve_o), ("scalar", act_o), ("gpsimd", pool_o)):
            ahead[eng_name] = [k for k in o if is_ahead(k)]
            S[eng_name] = Steps(sem(f"{eng_name}_ahead"), sem(f"{eng_name}_main"), ahead[eng_name], [k for k in o if not is_ahead(k)])
        pe_s, dve_s, act_s, pool_s = (S[n] for n in ("tensor", "vector", "scalar", "gpsimd"))

        misc = [k for k in pe_o if k[0] not in ("S", "P")]
        bank = {k: n % 2 for n, k in enumerate(misc)}
        st_place = {k: n % 2 for n, k in enumerate(units)}
        hi_place = {("HI",) + k: n for k, n in st_place.items()}
        rt_place = {("ROT",) + k: 0 for k in units}
        emptied = {"T": lambda k: (dve_s, ("XL", k[1])), "KV": lambda k: (dve_s, ("VC", k[1])), "Q": lambda k: (dve_s, ("ROT",) + k),
                   "QT": lambda k: (act_s, ("C",) + k), "KT": lambda k: (act_s, ("C",) + k), "R": lambda k: (act_s, ("RC", k[1])),
                   "A": lambda k: (dve_s, ("O", k[1])), "W": lambda k: (dve_s, ("F", k[1]))}
        own = lambda i, key: (i[0], i[1] + 1) if is_ahead(key) else i

        n_in = 5 if softmax else 4

        def raw_and_parts():
            room = pt[:, :] if softmax else dec[:, :, :].rearrange("p h s -> p (h s)")
            q0, o0 = KD * 2 * KVW, KD * 2 * KVW + KD * INNER
            return ((room[:, 0:q0], wkh, wkl), (room[:, q0:o0], wqh, wql), (room[:, o0:o0 + PAIRS * D], woh, wol))

        flat = lambda x: x[:, :, :].rearrange("p k n -> p (k n)")

        with nc.Block() as block:

            @block.sync
            def _(sp):
                for s in range(2):
                    sp.sem_inc(stored[s], 32)

                def load(i, index):
                    hold(sp, *pe_s.at(shift(i, -1), "T", KD - 1))
                    hold(sp, *dve_s.at(shift(i, -1), "XB"))
                    sp.dma_start(xc[:, :, :], x_in[bass.ds(index, 1), :, :].rearrange("o (t p) d -> p (o t) d", p=P)).then_inc(x_loaded, 16)

                raw_kv, raw_q, raw_o = (raw for raw, _, _ in raw_and_parts())
                sp.dma_start(raw_kv.rearrange("p (k n) -> p k n", k=KD), w_kv.rearrange("(k p) n -> p k n", p=P)).then_inc(weights_in, 16)
                load((0, 0), 0)
                sp.dma_start(raw_q.rearrange("p (k n) -> p k n", k=KD), w_q.rearrange("(k p) n -> p k n", p=P)).then_inc(weights_in, 16)
                sp.dma_start(rope[:, :, :, :], rope_tab).then_inc(weights_in, 16)
                sp.dma_start(raw_o.rearrange("p (k n) -> p k n", k=PAIRS), w_o.rearrange("(k p) n -> p k n", p=P)).then_inc(weights_in, 16)
                if softmax:
                    sp.dma_start(bias[:, :], out_bias.partition_broadcast(P)).then_inc(weights_in, 16)
                else:
                    hold(sp, weights_split, 3)
                    sp.dma_start(dec[:, :, :], decay_tab).then_inc(decay_in, 16)

                def store(i, index):
                    for t in range(TT):
                        hold(sp, *dve_s.at(i, "N", t))
                        sp.dma_start(x_out[bass.ds(index, 1), P * t:P * t + P, :].rearrange("o p d -> p (o d)"), r[:, t % 2, :]).then_inc(stored[t % 2], 16)

                with sp.Fori(0, BATCH - 1) as i:
                    load((i, 1), i + 1)
                    store((i, 0), i)
                store((BATCH - 1, 0), BATCH - 1)
                for s in range(2):
                    hold(sp, stored[s], 32 * BATCH + 32)

            @block.tensor
            def _(pe):
                pe_s.start(pe)
                pe.wait_ge(weights_split, 3)

                def steps(i, run):
                    in_misc = [k for k in run if k in bank]
                    for key in run:
                        kind, j = key[0], own(i, key)
                        if key in bank:
                            m = ps_m[:, bank[key], :]
                            for seq, k in last_use(i, in_misc, key, bank, ahead["tensor"], misc):
                                who, step = emptied[k[0]](k)
                                pe.wait_ge(*who.at(seq, *step))
                        if kind == "T":
                            k = key[1]
                            if k == 0:
                                pe.wait_ge(x_loaded, 16 * j[0] + 16 * j[1] + 16)
                            for t in range(TT):
                                last = nc.tensor.transpose(m[:, P * t:P * t + P], xc[:, t, P * k:P * k + P], ident[:, :])
                        elif kind in ("Q", "KV"):
                            t = key[-1]
                            pe.wait_ge(*dve_s.at(j, "XL", KD - 1))
                            tok = slice(P * t, P * t + P)
                            c0 = HH * HD * key[1] if kind == "Q" else 0
                            hi, lo = (wqh, wql) if kind == "Q" else (wkh, wkl)
                            last = sum_of_parts(nc, m, lambda k: xth[:, k, tok], lambda k: xtl[:, k, tok],
                                                lambda k: hi[:, k, c0:c0 + SEQ], lambda k: lo[:, k, c0:c0 + SEQ], KD)
                        elif kind in ("QT", "KT"):
                            u, b = (key[0][0] + ("V" if kind == "KT" else ""),) + key[1:-1], key[-1]
                            pe.wait_ge(*pool_s.at(j, "LO", *u))
                            for a in range(4):
                                at = 2 * HD * (4 * b + a) if kind == "QT" else 3 * HD * a + HD * b
                                last = nc.tensor.transpose(m[:, P * a:P * a + P], st[:, st_place[u], at:at + 2 * HD], ident[:, :])
                        elif kind == "S":
                            h, t = key[1:]
                            g = h // GRP
                            if h % HH == 0 and t == 0:
                                pe.wait_ge(*act_s.at(j, "C", "QT", h // HH, TT - 1, 1))
                                if h == 0:
                                    pe.wait_ge(*act_s.at(j, "C", "KT", TT - 1, 1))
                            who, step = (act_s, "X") if softmax else (dve_s, "M")
                            pe.wait_ge(*(who.at(j, step, h - 1, t) if h else who.at(shift(j, -1), step, HEADS - 1, t)))
                            for n in range(2):
                                if softmax:
                                    last = nc.tensor.matmul(ps_s[:, t, :], qs[:, h, P * t:P * t + P], ks[:, n, g, :], start=(n == 0), stop=(n == 1))
                                else:
                                    last = nc.tensor.matmul(ps_s[:, t, P * t:SEQ], ks[:, n, g, P * t:P * t + P], qs[:, h, P * t:SEQ], start=(n == 0), stop=(n == 1))
                        elif kind == "P":
                            h, c = key[1:]
                            if c == 0:
                                pe.wait_ge(*act_s.at(j, "X", h, 3))
                            ph, pc, seq = (h, c - 2, j) if c >= 2 else (h - 1, c + 2, j) if h else (HEADS - 1, c + 2, shift(j, -1))
                            pe.wait_ge(*(dve_s if pc % 2 == 0 else act_s).at(seq, "E", ph, pc))
                            for t in range(TT):
                                last = nc.tensor.transpose(ps_p[:, c % 2, P * t:P * t + P], probs[:, h % 2, t, P * c:P * c + P], ident[:, :])
                        elif kind == "R":
                            p = key[1]
                            pe.wait_ge(*dve_s.at(j, "I", 2 * p + 1))
                            for t in range(TT):
                                for s in range(2):
                                    last = nc.tensor.matmul(m[HD * s:HD * s + HD, P * t:P * t + P], ri[:, t, 2 * p + s:2 * p + s + 1].broadcast_to([P, HD]),
                                                            ident[:, :], start=True, stop=True)
                        elif kind == "A":
                            p = key[1]
                            g = 2 * p // GRP
                            pe.wait_ge(*dve_s.at(j, "VV"))
                            if softmax:
                                pe.wait_ge(*dve_s.at(j, "E", 2 * p + 1, 2))
                                pe.wait_ge(*act_s.at(j, "E", 2 * p + 1, 3))
                            else:
                                pe.wait_ge(*dve_s.at(j, "M", 2 * p + 1, 3))
                            for c in range(TT):
                                for s in range(2):
                                    last = nc.tensor.matmul(m[HD * s:HD * s + HD, first_q[c]:SEQ], v[:, 1, c, HD * g:HD * g + HD],
                                                            weights_of(2 * p + s, c), start=(c == 0), stop=(c == TT - 1))
                        elif kind == "W":
                            tok = slice(P * key[1], P * key[1] + P)
                            split = (lambda p: pool_s.at(j, "OL", p)) if softmax else (lambda p: dve_s.at(j, "O", p))
                            pe.wait_ge(*split(PAIRS - 2))
                            last_pair = (lambda: pe.wait_ge(*split(PAIRS - 1))) if key[1] == 0 else None
                            last = sum_of_parts(nc, m[:, 0:D], lambda k: ath[:, k, tok], lambda k: atl[:, k, tok],
                                                lambda k: woh[:, k, :], lambda k: wol[:, k, :], PAIRS, last_pair)
                        last.then_inc(pe_s.sem(key), 1)

                turns(pe, steps, ahead["tensor"], pe_o, ahead["tensor"])

            @block.vector
            def _(dve):
                dve_s.start(dve)
                dve.wait_ge(weights_in, 16 * n_in)
                if softmax:
                    keys = raw_and_parts()[0][0].rearrange("p (k n) -> p k n", k=KD)[:, :, 0:KVW]
                    nc.vector.tensor_scalar(keys, keys, HD ** -0.5, None, ALU.mult).then_inc(keys_scaled, 1)
                for n, (raw, hi, lo) in enumerate(raw_and_parts()):
                    dve.wait_ge(hi_split, n + 1)
                    nc.vector.tensor_tensor(flat(lo), raw, flat(hi).bitcast(F32), ALU.subtract).then_inc(weights_split, 1)
                vv = nc.vector

                def steps(i, run):
                    rot = [k for k in run if k[0] == "ROT"]
                    for key in run:
                        kind, j = key[0], own(i, key)
                        if kind == "XH":
                            k = key[1]
                            dve.wait_ge(*pe_s.at(j, "T", k))
                            if k == 0:
                                dve.wait_ge(*pe_s.at(shift(j, -1), "Q", 1, TT - 1))
                                dve.wait_ge(*pe_s.at(shift(j, -1), "KV", TT - 1))
                            op = vv.tensor_copy(xth[:, k, :], ps_m[:, bank["T", k], :])
                        elif kind == "XL":
                            k = key[1]
                            dve.wait_ge(*dve_s.at(j, "XH", k))
                            op = vv.tensor_tensor(xtl[:, k, :], ps_m[:, bank["T", k], :], xth[:, k, :].bitcast(F32), ALU.subtract)
                        elif kind == "XB":
                            dve.wait_ge(x_loaded, 16 * j[0] + 16 * j[1] + 16)
                            dve.wait_ge(*dve_s.at(shift(j, -1), "F", TT - 1))
                            if softmax:
                                op = vv.tensor_tensor(xb[:, :, :], xc[:, :, :], bias[:, :].unsqueeze(1).broadcast_to([P, TT, D]), ALU.add)
                            else:
                                op = vv.tensor_copy(xb[:, :, :], xc[:, :, :])
                        elif kind == "ROT":
                            u, t = key[1:], key[-1]
                            heads = HH if u[0] == "Q" else KVH
                            dve.wait_ge(*pe_s.at(j, *u))
                            for seq, k in last_use(i, rot, key, rt_place, ahead["vector"], dve_o):
                                dve.wait_ge(*pool_s.at(seq, "LO", *k[1:]))
                            w = heads * HD
                            op = vv.tensor_tensor(rt[:, :, 0:w].rearrange("p u (h d) -> p u h d", d=HD),
                                                  ps_m[:, bank[u], 0:w].rearrange("p (h d) -> p h d", d=HD).unsqueeze(1).broadcast_to([P, 2, heads, HD]),
                                                  rope[:, t, :, :].unsqueeze(2).broadcast_to([P, 2, heads, HD]), ALU.mult)
                        elif kind == "VC":
                            t = key[1]
                            dve.wait_ge(*pe_s.at(j, "KV", t))
                            dve.wait_ge(*dve_s.at(shift(j, -1), "VV"))
                            op = vv.tensor_copy(v[:, 0, t, :], ps_m[:, bank["KV", t], KVW:2 * KVW])
                        elif kind == "VV":
                            dve.wait_ge(*pe_s.at(shift(j, -1), "A", PAIRS - 1))
                            dve.wait_ge(*dve_s.at(j, "VC", TT - 1))
                            op = vv.tensor_copy(v[:, 1, :, :], v[:, 0, :, :])
                        elif kind == "M":
                            h, t = key[1:]
                            dve.wait_ge(*pe_s.at(j, "S", h, t))
                            if softmax:
                                if t == 0:
                                    dve.wait_ge(*act_s.at(shift(j, -1), "X", h, TT - 1))
                                op = vv.tensor_reduce(out=mx[:, h, t:t + 1], in_=ps_s[:, t, :], axis=AX.X, op=ALU.max, negate=True)
                            else:
                                if h == 0 and t == 0:
                                    dve.wait_ge(decay_in, 16)
                                if t == 0:
                                    offset, p = pairs_before(h)
                                    dve.wait_ge(*pe_s.at(shift(j, offset), "A", p))
                                op = vv.tensor_tensor(weights_of(h, t), ps_s[:, t, P * t:SEQ], dec[:, h, 0:SEQ - P * t], ALU.mult)
                        elif kind == "I":
                            h = key[1]
                            dve.wait_ge(*act_s.at(j, "X", h, TT - 1))
                            if h == 0:
                                dve.wait_ge(*pe_s.at(shift(j, -1), "R", PAIRS - 1))
                            op = vv.reciprocal(ri[:, :, h], rs[:, h, :])
                        elif kind == "E":
                            h, c = key[1:]
                            dve.wait_ge(*pe_s.at(j, "P", h, c))
                            if c == 0:
                                offset, p = pairs_before(h)
                                dve.wait_ge(*pe_s.at(shift(j, offset), "A", p))
                            op = vv.tensor_copy(weights_of(h, c), ps_p[:, c % 2, :])
                        elif kind == "O":
                            p = key[1]
                            dve.wait_ge(*pe_s.at(j, "A", p))
                            dve.wait_ge(*act_s.at(j, "RC", p))
                            if not softmax:
                                op = vv.tensor_tensor(atl[:, p, :], ps_m[:, bank["A", p], :], ath[:, p, :].bitcast(F32), ALU.subtract)
                                op.then_inc(dve_s.sem(key), 1)
                                continue
                            dve.wait_ge(*(pool_s.at(j, "OL", p - 1) if p else pool_s.at(shift(j, -1), "OL", PAIRS - 1)))
                            op = vv.tensor_tensor(ot[:, :], ps_m[:, bank["A", p], :], rrep[:, :], ALU.mult)
                        elif kind == "F":
                            t = key[1]
                            dve.wait_ge(*pe_s.at(j, "W", t))
                            if t == 0:
                                dve.wait_ge(*dve_s.at(j, "XB"))
                            dve.wait_ge(stored[t % 2], 32 * j[0] + (32 * j[1] + 16 * (t // 2) + 32))
                            op = vv.tensor_tensor(r[:, t % 2, :], ps_m[:, bank["W", t], 0:D], xb[:, t, :], ALU.add)
                        elif kind == "B":
                            t = key[1]
                            dve.wait_ge(*dve_s.at(j, "F", t))
                            op = vv.bn_stats(st6[:, t % 2, :], r[:, t % 2, :])
                        elif kind == "G":
                            t = key[1]
                            hold(dve, *dve_s.at(j, "B", t))
                            op = vv.bn_aggr(mv[:, t % 2, :], st6[:, t % 2, :])
                        elif kind == "N":
                            t = key[1]
                            dve.wait_ge(*pool_s.at(j, "RSTD", t))
                            op = vv.tensor_scalar(r[:, t % 2, :], r[:, t % 2, :], mv[:, t % 2, 0:1], rstd[:, t % 2, :], ALU.subtract, ALU.mult)
                        op.then_inc(dve_s.sem(key), 1)

                turns(dve, steps, ahead["vector"], dve_o, ahead["vector"])

            @block.scalar
            def _(act):
                act_s.start(act)
                act.wait_ge(weights_in, 16 * n_in)
                if softmax:
                    act.wait_ge(keys_scaled, 1)
                for raw, hi, _ in raw_and_parts():
                    nc.scalar.copy(flat(hi), raw).then_inc(hi_split, 1)

                def steps(i, run):
                    for key in run:
                        kind, j = key[0], own(i, key)
                        if kind == "C":
                            k = key[1:]
                            t, b = k[-2:]
                            act.wait_ge(*pe_s.at(j, *k))
                            src = ps_m[:, bank[k], :].rearrange("p (a s) -> p a s", s=P)
                            if k[0] == "QT":
                                half = k[1]
                                if t == 0 and b == 0:
                                    act.wait_ge(*pe_s.at(shift(j, -1), "S", HH * half + HH - 1, 3))
                                op = nc.scalar.copy(qs[:, HH * half + 4 * b:HH * half + 4 * b + 4, P * t:P * t + P], src)
                            else:
                                if t == 0 and b == 0:
                                    act.wait_ge(*pe_s.at(shift(j, -1), "S", HEADS - 1, 3))
                                op = nc.scalar.copy(ks[:, b, :, P * t:P * t + P], src)
                        elif kind == "X":
                            h, t = key[1:]
                            act.wait_ge(*dve_s.at(j, "M", h, t))
                            if t == 0:
                                act.wait_ge(*(pe_s.at(j, "P", h - 2, TT - 1) if h >= 2 else pe_s.at(shift(j, -1), "P", h + HEADS - 2, TT - 1)))
                                act.wait_ge(*dve_s.at(shift(j, -1), "I", h))
                            op = nc.scalar.activation(probs[:, h % 2, t, :], ps_s[:, t, :], ACT.Exp, bias=mx[:, h, t:t + 1], scale=1.0,
                                                      accum_out=rs[:, h, t:t + 1])
                        elif kind == "E":
                            h, c = key[1:]
                            act.wait_ge(*pe_s.at(j, "P", h, c))
                            offset, p = pairs_before(h)
                            act.wait_ge(*pe_s.at(shift(j, offset), "A", p))
                            op = nc.scalar.copy(weights_of(h, c), ps_p[:, c % 2, :])
                        elif kind == "RC":
                            p = key[1]
                            if softmax:
                                act.wait_ge(*pe_s.at(j, "R", p))
                                act.wait_ge(*(dve_s.at(j, "O", p - 1) if p else dve_s.at(shift(j, -1), "O", PAIRS - 1)))
                                op = nc.scalar.copy(rrep[:, :], ps_m[:, bank["R", p], :])
                            else:
                                act.wait_ge(*pe_s.at(j, "A", p))
                                act.wait_ge(*pe_s.at(shift(j, -1), "W", TT - 1))
                                op = nc.scalar.copy(ath[:, p, :], ps_m[:, bank["A", p], :])
                        op.then_inc(act_s.sem(key), 1)

                turns(act, steps, ahead["scalar"], act_o, ahead["scalar"])

            @block.gpsimd
            def _(pool):
                pool_s.start(pool)

                def steps(i, run):
                    his = [k for k in run if k[0] == "HI"]
                    for key in run:
                        kind, j = key[0], own(i, key)
                        u = key[1:]
                        if kind in ("Y0", "Y1", "HI", "LO"):
                            heads = HH if u[0] == "Q" else KVH
                            half = lambda n, c: rt[:, n, 0:heads * HD].rearrange("p (h c d) -> p h c d", c=2, d=HALF)[:, :, c, :]
                            rows = rt[:, 0, 0:heads * HD].rearrange("p (h d) -> p h d", d=HD)
                            width = 2 * HD if u[0] == "Q" else 3 * HD
                            stack = st[:, st_place[u], 0:heads * width].rearrange("p (h d) -> p h d", d=width)
                        if kind in ("Y0", "Y1"):
                            c = int(kind[1])
                            hold(pool, *dve_s.at(j, "ROT", *u))
                            op = nc.gpsimd.tensor_tensor(half(0, c), half(0, c), half(1, 1 - c), ALU.add)
                        elif kind == "HI":
                            hold(pool, *pool_s.at(j, "Y1", *u))
                            for seq, k in last_use(i, his, key, hi_place, ahead["gpsimd"], pool_o):
                                hold(pool, *pe_s.at(seq, *turned(k[1:])[1]))
                            if u[0] == "Q":
                                op = nc.gpsimd.tensor_copy(stack[:, :, 0:HD].bitcast(F32R), rows)
                            else:
                                op = nc.gpsimd.tensor_copy(stack.rearrange("p h (c d) -> p h c d", d=HD)[:, :, 0:3:2, :].bitcast(F32R),
                                                           rows.unsqueeze(2).broadcast_to([P, heads, 2, HD]))
                        elif kind == "LO":
                            hold(pool, *pool_s.at(j, "HI", *u))
                            op = nc.gpsimd.tensor_tensor(stack[:, :, HD:2 * HD].bitcast(F32R), rows, stack[:, :, 0:HD], ALU.subtract)
                        elif kind == "OH":
                            p = key[1]
                            hold(pool, *(dve_s.at(j, "O", p) if softmax else act_s.at(j, "RC", p)))
                            if p == 0:
                                hold(pool, *pe_s.at(shift(j, -1), "W", TT - 1))
                            op = nc.gpsimd.tensor_copy(ath[:, p, :], ot[:, :])
                        elif kind == "OL":
                            p = key[1]
                            hold(pool, *pool_s.at(j, "OH", p))
                            op = nc.gpsimd.tensor_tensor(atl[:, p, :], ot[:, :], ath[:, p, :].bitcast(F32), ALU.subtract)
                        elif kind == "EPS":
                            t = key[1]
                            hold(pool, *dve_s.at(j, "G", t))
                            op = nc.gpsimd.tensor_scalar(vare[:, t % 2, :], mv[:, t % 2, 1:2], EPS, None, ALU.add)
                        elif kind == "RSTD":
                            t = key[1]
                            hold(pool, *pool_s.at(j, "EPS", t))
                            hold(pool, *(dve_s.at(j, "N", t - 2) if t >= 2 else dve_s.at(shift(j, -1), "N", t + 2)))
                            op = nc.gpsimd.tensor_tensor(rstd[:, t % 2, :], vare[:, t % 2, :], const["minus_half"][:, :], ALU.pow)
                        op.then_inc(pool_s.sem(key), 1)

                turns(pool, steps, ahead["gpsimd"], pool_o, ahead["gpsimd"])


class LoopSteps:

    def __init__(self, sem, order):
        self.sem, self.order, self.per = sem, order, len(order)
        self.pos = {k: n for n, k in enumerate(order)}
        assert len(self.pos) == self.per

    def at(self, i, *key):
        return i * self.per + (self.pos[key] + 1 + self.per)

    def before(self, i, *key):
        return i * self.per + (self.pos[key] + 1)


def quantized_ffn(nc, const, x_in, x_out, gamma_beta, q1, s1, b1, q2, s2, b2, name):
    F = q1.shape[1]
    FT = F // P
    ctx = ExitStack()
    with ctx:
        sb = lambda n, s, dt=F32: ctx.enter_context(nc.sbuf_tensor(f"{name}_{n}", s, dt))
        sem = lambda n: ctx.enter_context(nc.semaphore(f"{name}_{n}"))
        ident = const["ident"]
        qi1, qi2 = sb("qi1", [P, KD, F], I32), sb("qi2", [P, FT, D], I32)
        sc1, sc2 = sb("sc1", [P, KD, F]), sb("sc2", [P, FT, D])
        w1h, w1l = (sb(n, [P, KD, F], F32R) for n in ("w1h", "w1l"))
        w2h, w2l = (sb(n, [P, FT, D], F32R) for n in ("w2h", "w2l"))
        gb = sb("gb", [P, 2, KD])
        b1c = sb("b1c", [P, FT])
        b2r = sb("b2r", [P, D])
        xc = sb("xc", [P, TT, D])
        xb = sb("xb", [P, TT, D])
        xn = sb("xn", [P, TT, D])
        ht = sb("ht", [P, KD, SEQ])
        hth, htl = (sb(n, [P, KD, SEQ], F32R) for n in ("hth", "htl"))
        s = sb("s", [P, 2, SEQ])
        sh, sl = (sb(n, [P, FT, SEQ], F32R) for n in ("sh", "sl"))
        r = sb("r", [P, 2, D])
        st6, st6x = sb("st6", [P, 2, 6]), sb("st6x", [P, TT, 6])
        mv, mvx = sb("mv", [P, 2, 2]), sb("mvx", [P, TT, 2])
        vare, varex = sb("vare", [P, 2, 1]), sb("varex", [P, TT, 1])
        rstd, rstdx = sb("rstd", [P, 2, 1]), sb("rstdx", [P, TT, 1])
        outt = sb("outt", [P, 2, D])
        ps = ctx.enter_context(nc.psum_tensor(f"{name}_ps", [P, 8, SEQ], F32))
        weights_in, weight_steps, hi_split, weights_split = sem("weights_in"), sem("weight_steps"), sem("hi_split"), sem("weights_split")
        x_loaded = sem("x_loaded")
        stored = [sem(f"stored{k}") for k in range(2)]
        hold = gated_hold(sem("held"))

        pe_o = [("T", k) for k in range(KD)] + [("H", m) for m in range(FT)] + [("W", t) for t in range(TT)]
        dve_o = [(n, t) for t in range(TT) for n in ("BX", "GX")] + [("NX", t) for t in range(TT)] + [("XB",)]
        dve_o += [(n, k) for k in range(KD) for n in ("XH", "XL")]
        dve_o += [(n, m) for m in range(FT) for n in ("SH", "SL")]
        act_o = [("HT", k) for k in range(KD)] + [("S", m) for m in range(FT)]
        pool_o = [("EPSX",), ("RSTDX",)]
        for t in range(TT + 1):
            if t < TT:
                dve_o += [("F", t), ("B", t), ("G", t)]; pool_o += [("EPS", t), ("RSTD", t)]
            if t >= 1: dve_o.append(("N", t - 1))
        pe_s, dve_s = LoopSteps(sem("tensor_steps"), pe_o), LoopSteps(sem("vector_steps"), dve_o)
        act_s, pool_s = LoopSteps(sem("scalar_steps"), act_o), LoopSteps(sem("gpsimd_steps"), pool_o)
        BANKS = 7
        assert len(pe_o) % BANKS == 0
        bank = {k: n % BANKS for n, k in enumerate(pe_o)}

        with nc.Block() as block:

            @block.sync
            def _(sp):
                for k in range(2):
                    sp.sem_inc(stored[k], 32)
                sp.dma_start(qi1[:, :, :], q1.rearrange("(k p) n -> p k n", p=P)).then_inc(weights_in, 16)
                sp.dma_start(sc1[:, :, :].rearrange("p k n -> p (k n)"), s1.rearrange("k n -> (k n)").partition_broadcast(P)).then_inc(weights_in, 16)
                sp.dma_start(qi2[:, :, :], q2.rearrange("(k p) n -> p k n", p=P)).then_inc(weights_in, 16)
                sp.dma_start(sc2[:, :, :].rearrange("p k n -> p (k n)"), s2.rearrange("k n -> (k n)").partition_broadcast(P)).then_inc(weights_in, 16)
                sp.dma_start(gb[:, :, :], gamma_beta).then_inc(weights_in, 16)
                sp.dma_start(b1c[:, :], b1).then_inc(weights_in, 16)
                sp.dma_start(b2r[:, :], b2.partition_broadcast(P)).then_inc(weights_in, 16)
                with sp.Fori(0, BATCH) as i:
                    hold(sp, dve_s.sem, dve_s.before(i, "XB"))
                    sp.dma_start(xc[:, :, :], x_in[bass.ds(i, 1), :, :].rearrange("o (t p) d -> p (o t) d", p=P)).then_inc(x_loaded, 16)
                    for t in range(TT):
                        hold(sp, dve_s.sem, dve_s.at(i, "N", t))
                        sp.dma_start(x_out[bass.ds(i, 1), P * t:P * t + P, :].rearrange("o p d -> p (o d)"), outt[:, t % 2, :]).then_inc(stored[t % 2], 16)
                for k in range(2):
                    hold(sp, stored[k], 32 * BATCH + 32)

            @block.tensor
            def _(pe):
                pe.sem_inc(pe_s.sem, pe_s.per)
                pe.wait_ge(weights_split, 2)
                with pe.Fori(0, BATCH) as i:
                    for n, key in enumerate(pe_o):
                        kind = key[0]
                        m = ps[:, bank[key], :]
                        was = pe_o[n - BANKS]
                        reader, rk = {"T": (act_s, ("HT",)), "H": (act_s, ("S",)), "W": (dve_s, ("F",))}[was[0]]
                        value = reader.at if n >= BANKS else reader.before
                        pe.wait_ge(reader.sem, value(i, rk[0], was[1]))
                        if kind == "T":
                            k = key[1]
                            if k == 0:
                                pe.wait_ge(dve_s.sem, dve_s.at(i, "NX", TT - 1))
                            for t in range(TT):
                                last = nc.tensor.transpose(m[:, P * t:P * t + P], xn[:, t, P * k:P * k + P], ident[:, :])
                        elif kind == "H":
                            cols = slice(P * key[1], P * key[1] + P)
                            if key[1] == 0:
                                pe.wait_ge(dve_s.sem, dve_s.at(i, "XL", KD - 1))
                            last = sum_of_parts(nc, m, lambda k: w1h[:, k, cols], lambda k: w1l[:, k, cols],
                                                lambda k: hth[:, k, :], lambda k: htl[:, k, :], KD)
                        elif kind == "W":
                            t = key[1]
                            tok = slice(P * t, P * t + P)
                            if t == 0:
                                pe.wait_ge(dve_s.sem, dve_s.at(i, "SL", FT - 1))
                            last = sum_of_parts(nc, m[:, 0:D], lambda k: sh[:, k, tok], lambda k: sl[:, k, tok],
                                                lambda k: w2h[:, k, :], lambda k: w2l[:, k, :], FT)
                        last.then_inc(pe_s.sem, 1)

            flat = lambda x: x[:, :, :].rearrange("p k n -> p (k n)")

            @block.vector
            def _(dve):
                dve.sem_inc(dve_s.sem, dve_s.per)
                dve.wait_ge(weights_in, 16 * 7)
                nc.vector.tensor_scalar(b2r[:, :], b2r[:, :], 0.5, None, ALU.mult).then_inc(weight_steps, 1)
                for qi, sc in ((qi1, sc1), (qi2, sc2)):
                    nc.vector.scalar_tensor_tensor(out=flat(sc), in0=flat(qi), scalar=-128.0, in1=flat(sc), op0=ALU.add, op1=ALU.mult).then_inc(weight_steps, 1)
                for n, (raw, hi, lo) in enumerate(((sc1, w1h, w1l), (sc2, w2h, w2l))):
                    dve.wait_ge(hi_split, n + 1)
                    nc.vector.tensor_tensor(flat(lo), flat(raw), flat(hi).bitcast(F32), ALU.subtract).then_inc(weights_split, 1)
                with dve.Fori(0, BATCH) as i:
                    for key in dve_o:
                        kind = key[0]
                        t = k = m = key[1] if len(key) > 1 else 0
                        if kind == "BX":
                            if t == 0:
                                dve.wait_ge(x_loaded, 16 * i + 16)
                                dve.wait_ge(dve_s.sem, dve_s.before(i, "NX", TT - 1))
                            op = nc.vector.bn_stats(st6x[:, t, :], xc[:, t, :])
                        elif kind == "GX":
                            hold(dve, dve_s.sem, dve_s.at(i, "BX", t))
                            op = nc.vector.bn_aggr(mvx[:, t, :], st6x[:, t, :])
                        elif kind == "NX":
                            if t == 0:
                                dve.wait_ge(pool_s.sem, pool_s.at(i, "RSTDX"))
                                dve.wait_ge(pe_s.sem, pe_s.before(i, "T", KD - 1))
                            op = nc.vector.tensor_scalar(xn[:, t, :], xc[:, t, :], mvx[:, t, 0:1], rstdx[:, t, :], ALU.subtract, ALU.mult)
                        elif kind == "XB":
                            dve.wait_ge(dve_s.sem, dve_s.before(i, "F", TT - 1))
                            op = nc.vector.scalar_tensor_tensor(out=xb[:, :, :], in0=xc[:, :, :], scalar=2.0,
                                                                in1=b2r[:, :].unsqueeze(1).broadcast_to([P, TT, D]), op0=ALU.mult, op1=ALU.add)
                        elif kind == "XH":
                            dve.wait_ge(act_s.sem, act_s.at(i, "HT", k))
                            if k == 0:
                                dve.wait_ge(pe_s.sem, pe_s.before(i, "H", FT - 1))
                            op = nc.vector.tensor_copy(hth[:, k, :], ht[:, k, :])
                        elif kind == "XL":
                            dve.wait_ge(dve_s.sem, dve_s.at(i, "XH", k))
                            op = nc.vector.tensor_tensor(htl[:, k, :], ht[:, k, :], hth[:, k, :].bitcast(F32), ALU.subtract)
                        elif kind == "SH":
                            dve.wait_ge(act_s.sem, act_s.at(i, "S", m))
                            if m == 0:
                                dve.wait_ge(pe_s.sem, pe_s.before(i, "W", TT - 1))
                            op = nc.vector.tensor_copy(sh[:, m, :], s[:, m % 2, :])
                        elif kind == "SL":
                            dve.wait_ge(dve_s.sem, dve_s.at(i, "SH", m))
                            op = nc.vector.tensor_tensor(sl[:, m, :], s[:, m % 2, :], sh[:, m, :].bitcast(F32), ALU.subtract)
                        elif kind == "F":
                            dve.wait_ge(pe_s.sem, pe_s.at(i, "W", t))
                            dve.wait_ge(dve_s.sem, dve_s.at(i, "N", t - 2) if t >= 2 else dve_s.before(i, "N", t + 2))
                            op = nc.vector.scalar_tensor_tensor(out=r[:, t % 2, :], in0=ps[:, bank["W", t], 0:D], scalar=0.5, in1=xb[:, t, :], op0=ALU.mult, op1=ALU.add)
                        elif kind == "B":
                            dve.wait_ge(dve_s.sem, dve_s.at(i, "F", t))
                            op = nc.vector.bn_stats(st6[:, t % 2, :], r[:, t % 2, :])
                        elif kind == "G":
                            hold(dve, dve_s.sem, dve_s.at(i, "B", t))
                            op = nc.vector.bn_aggr(mv[:, t % 2, :], st6[:, t % 2, :])
                        elif kind == "N":
                            dve.wait_ge(pool_s.sem, pool_s.at(i, "RSTD", t))
                            dve.wait_ge(stored[t % 2], 32 * i + 16 * (t // 2) + 32)
                            op = nc.vector.tensor_scalar(outt[:, t % 2, :], r[:, t % 2, :], mv[:, t % 2, 0:1], rstd[:, t % 2, :], ALU.subtract, ALU.mult)
                        op.then_inc(dve_s.sem, 1)

            @block.scalar
            def _(act):
                act.sem_inc(act_s.sem, act_s.per)
                for n, (raw, hi) in enumerate(((sc1, w1h), (sc2, w2h))):
                    act.wait_ge(weight_steps, n + 2)
                    nc.scalar.copy(flat(hi), flat(raw)).then_inc(hi_split, 1)
                with act.Fori(0, BATCH) as i:
                    for key in act_o:
                        kind, k = key
                        if kind == "HT":
                            act.wait_ge(pe_s.sem, pe_s.at(i, "T", k))
                            act.wait_ge(dve_s.sem, dve_s.before(i, "XL", k))
                            op = nc.scalar.activation(ht[:, k, :], ps[:, bank["T", k], :], ACT.Identity, bias=gb[:, 1, k:k + 1], scale=gb[:, 0, k:k + 1])
                        else:
                            act.wait_ge(pe_s.sem, pe_s.at(i, "H", k))
                            act.wait_ge(dve_s.sem, dve_s.at(i, "SL", k - 2) if k >= 2 else dve_s.before(i, "SL", k + FT - 2))
                            op = nc.scalar.activation(s[:, k % 2, :], ps[:, bank["H", k], :], ACT.Silu, bias=b1c[:, k:k + 1], scale=1.0)
                        op.then_inc(act_s.sem, 1)

            @block.gpsimd
            def _(pool):
                pool.sem_inc(pool_s.sem, pool_s.per)
                with pool.Fori(0, BATCH) as i:
                    for key in pool_o:
                        kind = key[0]
                        if kind == "EPSX":
                            hold(pool, dve_s.sem, dve_s.at(i, "GX", TT - 1))
                            op = nc.gpsimd.tensor_scalar(varex[:, :, :], mvx[:, :, 1:2], EPS, None, ALU.add)
                        elif kind == "RSTDX":
                            hold(pool, pool_s.sem, pool_s.at(i, "EPSX"))
                            hold(pool, dve_s.sem, dve_s.before(i, "NX", TT - 1))
                            op = nc.gpsimd.tensor_tensor(rstdx[:, :, :], varex[:, :, :], const["minus_half"][:, :].unsqueeze(1).broadcast_to([P, TT, 1]), ALU.pow)
                        elif kind == "EPS":
                            t = key[1]
                            hold(pool, dve_s.sem, dve_s.at(i, "G", t))
                            op = nc.gpsimd.tensor_scalar(vare[:, t % 2, :], mv[:, t % 2, 1:2], EPS, None, ALU.add)
                        elif kind == "RSTD":
                            t = key[1]
                            hold(pool, pool_s.sem, pool_s.at(i, "EPS", t))
                            hold(pool, dve_s.sem, dve_s.at(i, "N", t - 2) if t >= 2 else dve_s.before(i, "N", t + 2))
                            op = nc.gpsimd.tensor_tensor(rstd[:, t % 2, :], vare[:, t % 2, :], const["minus_half"][:, :], ALU.pow)
                        op.then_inc(pool_s.sem, 1)


MH, KPH, VAR = 16, 8, 4
QUADS = MH // 4
E_ = 8


def latent_attention(nc, const, x_in, m_out, comb_out, w, name):
    ctx = ExitStack()
    with ctx:
        sb = lambda n, s, dt=F32: ctx.enter_context(nc.sbuf_tensor(f"{name}_{n}", s, dt))
        sem = lambda n: ctx.enter_context(nc.semaphore(f"{name}_{n}"))
        ident = const["ident"]
        LAT = MH * KPH
        raw_y = sb("raw_y", [P, KD, 2 * 4 * LAT])
        raw_v = sb("raw_v", [P, KD, LAT])
        raw_r = sb("raw_r", [P, KD, E_])
        raw_o = sb("raw_o", [P, 1, D])
        wyh, wyl = (sb(n, [P, KD, 2 * 4 * LAT], F32R) for n in ("wyh", "wyl"))
        wvh, wvl = (sb(n, [P, KD, LAT], F32R) for n in ("wvh", "wvl"))
        wrh, wrl = (sb(n, [P, KD, E_], F32R) for n in ("wrh", "wrl"))
        woh, wol = (sb(n, [P, 1, D], F32R) for n in ("woh", "wol"))
        yb = sb("yb", [P, 2 * QUADS])
        minus_lo = sb("minus_lo", [P, 2])
        vb, orow, rrow = sb("vb", [P, LAT]), sb("orow", [P, D]), sb("rrow", [P, E_])
        ocol = sb("ocol", [P, KD])
        rev = sb("rev", [P, E_])
        xc = sb("xc", [P, TT, D])
        xth, xtl = (sb(n, [P, KD, SEQ], F32R) for n in ("xth", "xtl"))
        y = sb("y", [P, 2, SEQ])
        yh = sb("yh", [P, 2, SEQ], F32R)
        stack = sb("stack", [P, 2 * QUADS, SEQ], F32R)
        v = sb("v", [P, TT, MH, 32])
        probs = sb("probs", [P, 2, TT, SEQ])
        rs = sb("rs", [P, MH, TT])
        ri = sb("ri", [P, TT, MH])
        mx = sb("mx", [P, MH, TT])
        pt = sb("pt", [P, 8, TT, SEQ])
        ot = sb("ot", [P, QUADS, SEQ])
        ao = sb("ao", [P, TT, LAT])
        ch, cl = (sb(n, [P, SEQ], F32R) for n in ("ch", "cl"))
        mt = sb("mt", [P, KD, SEQ])
        mth, mtl = (sb(n, [P, KD, SEQ], F32R) for n in ("mth", "mtl"))
        mo = sb("mo", [P, 2, D])
        small = lambda n: sb(n, [P, TT, E_])
        lg, ex, pr, eq, key_, oh1, p2, oh2, oh, wt, comb = (small(n) for n in ("lg", "ex", "pr", "eq", "key", "oh1", "p2", "oh2", "oh", "wt", "comb"))
        one = lambda n: sb(n, [P, TT, 1])
        lm, es, er, v1, k1, v2, k2, tw, tr = (one(n) for n in ("lm", "es", "er", "v1", "k1", "v2", "k2", "tw", "tr"))
        ps_s = ctx.enter_context(nc.psum_tensor(f"{name}_ps_s", [P, 4, SEQ], F32))
        ps_p = ctx.enter_context(nc.psum_tensor(f"{name}_ps_p", [P, 2, SEQ], F32))
        ps_m = ctx.enter_context(nc.psum_tensor(f"{name}_ps_m", [P, 2, SEQ], F32))
        weights_in, hi_split, weights_split, zeroed = sem("weights_in"), sem("hi_split"), sem("weights_split"), sem("zeroed")
        x_loaded, comb_stored = sem("x_loaded"), sem("comb_stored")
        stored = [sem(f"stored{k}") for k in range(2)]
        hold = gated_hold(sem("held"))

        pe_o = [("T", k) for k in range(KD)] + [("Y", n) for n in range(2 * QUADS)] + [("V", t) for t in range(TT)]
        dve_o = [(n, k) for k in range(KD) for n in ("XH", "XL")]
        for n in range(2 * QUADS + 1):
            if n < 2 * QUADS: dve_o.append(("YB", n))
            if n >= 1: dve_o.append(("YS", n - 1))
        pool_o = [("YH", n) for n in range(2 * QUADS)]
        dve_o += [("VB", t) for t in range(TT)]
        act_o = []
        for h in range(MH + 2):
            now, old = h < MH, 0 <= h - 1 < MH
            a = (h - 5) // 4 if h >= 5 and (h - 5) % 4 == 0 else None
            for t in range(3):
                if now:
                    pe_o.append(("S", h, t)); dve_o.append(("M", h, t)); act_o.append(("X", h, t))
            if old: dve_o.append(("I", h - 1))
            if a is not None:
                pe_o.append(("A", a)); act_o.append(("OT", a))
            if old:
                pe_o += [("P", h - 1, 0), ("P", h - 1, 1)]
                dve_o.append(("E", h - 1, 0)); act_o.append(("E", h - 1, 1))
            if now:
                pe_o.append(("S", h, 3)); dve_o.append(("M", h, 3)); act_o.append(("X", h, 3))
            if old:
                pe_o += [("P", h - 1, 2), ("P", h - 1, 3)]
                dve_o.append(("E", h - 1, 2)); act_o.append(("E", h - 1, 3))
        pe_o += [("BT", t) for t in range(TT)] + [("CT",)] + [("MT", c) for c in range(KD)] + [("MO", t) for t in range(TT)] + [("RL",)]
        dve_o += [("AO", t) for t in range(TT)] + [("CH",), ("CL",)] + [(n, c) for c in range(KD) for n in ("MB", "MH", "ML")]
        dve_o += [("MO", t) for t in range(TT)]
        ROUTE = ["LG", "LM", "LD"]
        ROUTE2 = ["ES", "ER", "PR", "V1", "EQ1", "KY1", "K1", "OH1", "P2", "V2", "EQ2", "KY2", "K2", "OH2", "OH", "TW", "TR", "WT", "COMB"]
        dve_o += [(n,) for n in ROUTE + ROUTE2]
        act_o += [("EX",)]
        pe_s, dve_s = LoopSteps(sem("tensor_steps"), pe_o), LoopSteps(sem("vector_steps"), dve_o)
        act_s, pool_s = LoopSteps(sem("scalar_steps"), act_o), LoopSteps(sem("gpsimd_steps"), pool_o)
        misc = [k for k in pe_o if k[0] not in ("S", "P")]
        assert len(misc) % 2 == 0, len(misc)
        bank = {k: n % 2 for n, k in enumerate(misc)}
        reader = {"T": (dve_s, "XL"), "Y": (dve_s, "YB"), "V": (dve_s, "VB"), "A": (act_s, "OT"), "BT": (dve_s, "AO"), "CT": (dve_s, "CL"),
                  "MT": (dve_s, "MB"), "MO": (dve_s, "MO"), "RL": (dve_s, "LG")}

        with nc.Block() as block:

            @block.sync
            def _(sp):
                for k in range(2):
                    sp.sem_inc(stored[k], 32)
                sp.sem_inc(comb_stored, 16)
                loads = [(raw_y[:, :, :], w["stacks"].rearrange("(k p) n -> p k n", p=P)), (raw_v[:, :, :], w["v_w"].rearrange("(k p) n -> p k n", p=P)),
                         (raw_r[:, :, :], w["router_w"].rearrange("(k p) n -> p k n", p=P)), (raw_o[:, 0, :], w["o_w"][0:P, :]),
                         (yb[:, :], w["stack_b"]), (minus_lo[:, :], w["minus_lo"]), (vb[:, :], w["v_b"].partition_broadcast(P)),
                         (orow[:, :], w["o_b"].partition_broadcast(P)), (rrow[:, :], w["router_b"].partition_broadcast(P)),
                         (ocol[:, :], w["o_b_cols"]), (rev[:, :], w["rev"].partition_broadcast(P))]
                for dst, src in loads:
                    sp.dma_start(dst, src).then_inc(weights_in, 16)
                with sp.Fori(0, BATCH) as i:
                    hold(sp, pe_s.sem, pe_s.before(i, "T", KD - 1))
                    sp.dma_start(xc[:, :, :], x_in[bass.ds(i, 1), :, :].rearrange("o (t p) d -> p (o t) d", p=P)).then_inc(x_loaded, 16)
                    for t in range(TT):
                        hold(sp, dve_s.sem, dve_s.at(i, "MO", t))
                        sp.dma_start(m_out[bass.ds(i, 1), P * t:P * t + P, :].rearrange("o p d -> p (o d)"), mo[:, t % 2, :]).then_inc(stored[t % 2], 16)
                    hold(sp, dve_s.sem, dve_s.at(i, "COMB"))
                    sp.dma_start(comb_out[bass.ds(i, 1), :, :].rearrange("o (t p) e -> p (o t) e", p=P), comb[:, :, :]).then_inc(comb_stored, 16)
                for k in range(2):
                    hold(sp, stored[k], 32 * BATCH + 32)
                hold(sp, comb_stored, 16 * BATCH + 16)

            @block.tensor
            def _(pe):
                pe.sem_inc(pe_s.sem, pe_s.per)
                pe.wait_ge(weights_split, 4)
                pe.wait_ge(zeroed, 1)
                with pe.Fori(0, BATCH) as i:
                    for key in pe_o:
                        kind = key[0]
                        if kind not in ("S", "P"):
                            n = misc.index(key)
                            was = misc[n - 2]
                            steps, rk = reader[was[0]]
                            pe.wait_ge(steps.sem, (steps.at if n >= 2 else steps.before)(i, rk, *was[1:]))
                            m = ps_m[:, bank[key], :]
                        if kind == "T":
                            k = key[1]
                            if k == 0:
                                pe.wait_ge(x_loaded, 16 * i + 16)
                            for t in range(TT):
                                last = nc.tensor.transpose(m[:, P * t:P * t + P], xc[:, t, P * k:P * k + P], ident[:, :])
                        elif kind == "Y":
                            n = key[1]
                            if n == 0:
                                pe.wait_ge(dve_s.sem, dve_s.at(i, "XL", KD - 1))
                            cols = slice(P * n, P * n + P)
                            last = sum_of_parts(nc, m, lambda k: wyh[:, k, cols], lambda k: wyl[:, k, cols], lambda k: xth[:, k, :], lambda k: xtl[:, k, :], KD)
                        elif kind == "V":
                            tok = slice(P * key[1], P * key[1] + P)
                            last = sum_of_parts(nc, m[:, 0:LAT], lambda k: xth[:, k, tok], lambda k: xtl[:, k, tok], lambda k: wvh[:, k, :], lambda k: wvl[:, k, :], KD)
                        elif kind == "S":
                            h, t = key[1:]
                            a, rows = h // 4, slice(32 * (h % 4), 32 * (h % 4) + 32)
                            if h == 0 and t == 0:
                                pe.wait_ge(dve_s.sem, dve_s.at(i, "YS", 2 * QUADS - 1))
                            pe.wait_ge(act_s.sem, act_s.at(i, "X", h - 1, t) if h else act_s.before(i, "X", MH - 1, t))
                            last = nc.tensor.matmul(ps_s[:, t, :], stack[rows, QUADS + a, P * t:P * t + P], stack[rows, a, :], start=True, stop=True)
                        elif kind == "P":
                            h, j = key[1:]
                            if j == 0:
                                pe.wait_ge(act_s.sem, act_s.at(i, "X", h, 3))
                            if (h, j) == (0, 0):
                                pe.wait_ge(dve_s.sem, dve_s.before(i, "E", MH - 1, 2))
                            elif (h, j) == (0, 1):
                                pe.wait_ge(act_s.sem, act_s.before(i, "E", MH - 1, 3))
                            else:
                                ph, pj = (h, j - 2) if j >= 2 else (h - 1, j + 2)
                                s_ = dve_s if pj % 2 == 0 else act_s
                                pe.wait_ge(s_.sem, s_.at(i, "E", ph, pj))
                            for t in range(TT):
                                last = nc.tensor.transpose(ps_p[:, j % 2, P * t:P * t + P], probs[:, h % 2, t, P * j:P * j + P], ident[:, :])
                        elif kind == "A":
                            a = key[1]
                            pe.wait_ge(dve_s.sem, dve_s.at(i, "VB", TT - 1))
                            pe.wait_ge(dve_s.sem, dve_s.at(i, "E", 4 * a + 3, 2))
                            pe.wait_ge(act_s.sem, act_s.at(i, "E", 4 * a + 3, 3))
                            for j in range(TT):
                                for s in range(4):
                                    last = nc.tensor.matmul(m[32 * s:32 * s + 32, :], v[:, j, 4 * a + s, :], pt[:, (4 * a + s) % 8, j, :], start=(j == 0), stop=(j == TT - 1), tile_position=(0, 32 * s))
                        elif kind == "BT":
                            t = key[1]
                            pe.wait_ge(act_s.sem, act_s.at(i, "OT", QUADS - 1))
                            for a in range(QUADS):
                                last = nc.tensor.transpose(m[:, P * a:P * a + P], ot[:, a, P * t:P * t + P], ident[:, :])
                        elif kind == "CT":
                            pe.wait_ge(dve_s.sem, dve_s.at(i, "AO", TT - 1))
                            for t in range(TT):
                                last = nc.tensor.transpose(m[:, P * t:P * t + P], ao[:, t, :], ident[:, :])
                        elif kind == "MT":
                            c = key[1]
                            pe.wait_ge(dve_s.sem, dve_s.at(i, "CL"))
                            cols = slice(P * c, P * c + P)
                            last = sum_of_parts(nc, m, lambda k: woh[:, k, cols], lambda k: wol[:, k, cols], lambda k: ch[:, :], lambda k: cl[:, :], 1)
                        elif kind == "MO":
                            tok = slice(P * key[1], P * key[1] + P)
                            last = sum_of_parts(nc, m[:, 0:D], lambda k: ch[:, tok], lambda k: cl[:, tok], lambda k: woh[:, k, :], lambda k: wol[:, k, :], 1)
                        elif kind == "RL":
                            pe.wait_ge(dve_s.sem, dve_s.at(i, "ML", KD - 1))
                            for t in range(TT):
                                tok = slice(P * t, P * t + P)
                                last = sum_of_parts(nc, m[:, E_ * t:E_ * t + E_], lambda k: mth[:, k, tok], lambda k: mtl[:, k, tok], lambda k: wrh[:, k, :], lambda k: wrl[:, k, :], KD)
                        last.then_inc(pe_s.sem, 1)

            flat = lambda x: x[:, :, :].rearrange("p k n -> p (k n)")
            splits = ((raw_y, wyh, wyl), (raw_v, wvh, wvl), (raw_r, wrh, wrl), (raw_o, woh, wol))

            @block.vector
            def _(dve):
                dve.sem_inc(dve_s.sem, dve_s.per)
                nc.vector.memset(v[:, :, :, :], 0.0).then_inc(zeroed, 1)
                dve.wait_ge(zeroed, 1)
                for n, (raw, hi, lo) in enumerate(splits):
                    dve.wait_ge(hi_split, n + 1)
                    nc.vector.tensor_tensor(flat(lo), flat(raw), flat(hi).bitcast(F32), ALU.subtract).then_inc(weights_split, 1)
                vv = nc.vector
                per_token = lambda s: s[:, :, :].broadcast_to([P, TT, E_])
                per_expert = lambda s: s[:, :].unsqueeze(1).broadcast_to([P, TT, E_])
                A3 = lambda s: s[:, :, :]
                route = {
                    "LM": lambda: vv.tensor_reduce(out=A3(lm), in_=A3(lg), axis=AX.X, op=ALU.max),
                    "LD": lambda: vv.tensor_tensor(A3(ex), A3(lg), per_token(lm), ALU.subtract),
                    "ES": lambda: vv.tensor_reduce(out=A3(es), in_=A3(pr), axis=AX.X, op=ALU.add),
                    "ER": lambda: vv.reciprocal(A3(er), A3(es)),
                    "PR": lambda: vv.tensor_tensor(A3(wt), A3(pr), per_token(er), ALU.mult),
                    "V1": lambda: vv.tensor_reduce(out=A3(v1), in_=A3(wt), axis=AX.X, op=ALU.max),
                    "EQ1": lambda: vv.tensor_tensor(A3(eq), A3(wt), per_token(v1), ALU.is_equal),
                    "KY1": lambda: vv.tensor_tensor(A3(key_), A3(eq), per_expert(rev), ALU.mult),
                    "K1": lambda: vv.tensor_reduce(out=A3(k1), in_=A3(key_), axis=AX.X, op=ALU.max),
                    "OH1": lambda: vv.tensor_tensor(A3(oh1), per_expert(rev), per_token(k1), ALU.is_equal),
                    "P2": lambda: vv.scalar_tensor_tensor(out=A3(p2), in0=A3(oh1), scalar=-2.0, in1=A3(wt), op0=ALU.mult, op1=ALU.add),
                    "V2": lambda: vv.tensor_reduce(out=A3(v2), in_=A3(p2), axis=AX.X, op=ALU.max),
                    "EQ2": lambda: vv.tensor_tensor(A3(eq), A3(p2), per_token(v2), ALU.is_equal),
                    "KY2": lambda: vv.tensor_tensor(A3(key_), A3(eq), per_expert(rev), ALU.mult),
                    "K2": lambda: vv.tensor_reduce(out=A3(k2), in_=A3(key_), axis=AX.X, op=ALU.max),
                    "OH2": lambda: vv.tensor_tensor(A3(oh2), per_expert(rev), per_token(k2), ALU.is_equal),
                    "OH": lambda: vv.tensor_tensor(A3(oh), A3(oh1), A3(oh2), ALU.add),
                    "TW": lambda: vv.scalar_tensor_tensor(out=A3(tw), in0=A3(v1), scalar=1e-8, in1=A3(v2), op0=ALU.add, op1=ALU.add),
                    "TR": lambda: vv.reciprocal(A3(tr), A3(tw)),
                    "WT": lambda: vv.tensor_tensor(A3(p2), A3(wt), A3(oh), ALU.mult),
                    "COMB": lambda: vv.tensor_tensor(A3(comb), A3(p2), per_token(tr), ALU.mult),
                }
                with dve.Fori(0, BATCH) as i:
                    for n_, key in enumerate(dve_o):
                        kind = key[0]
                        if kind == "XH":
                            k = key[1]
                            dve.wait_ge(pe_s.sem, pe_s.at(i, "T", k))
                            if k == 0:
                                dve.wait_ge(pe_s.sem, pe_s.before(i, "V", TT - 1))
                            op = vv.tensor_copy(xth[:, k, :], ps_m[:, bank["T", k], :])
                        elif kind == "XL":
                            k = key[1]
                            dve.wait_ge(dve_s.sem, dve_s.at(i, "XH", k))
                            op = vv.tensor_tensor(xtl[:, k, :], ps_m[:, bank["T", k], :], xth[:, k, :].bitcast(F32), ALU.subtract)
                        elif kind == "YB":
                            n = key[1]
                            dve.wait_ge(pe_s.sem, pe_s.at(i, "Y", n))
                            dve.wait_ge(dve_s.sem, dve_s.at(i, "YS", n - 2) if n >= 2 else dve_s.before(i, "YS", n + 2 * QUADS - 2))
                            op = vv.tensor_scalar(y[:, n % 2, :], ps_m[:, bank["Y", n], :], yb[:, n:n + 1], 1.0 if n < QUADS else KPH ** -0.5, ALU.add, ALU.mult)
                        elif kind == "YS":
                            n = key[1]
                            dve.wait_ge(pool_s.sem, pool_s.at(i, "YH", n))
                            if n == 0:
                                dve.wait_ge(pe_s.sem, pe_s.before(i, "S", MH - 1, 3))
                            op = vv.scalar_tensor_tensor(out=stack[:, n, :], in0=yh[:, n % 2, :].bitcast(F32), scalar=minus_lo[:, n // QUADS:n // QUADS + 1],
                                                         in1=y[:, n % 2, :], op0=ALU.mult, op1=ALU.add)
                        elif kind == "VB":
                            t = key[1]
                            dve.wait_ge(pe_s.sem, pe_s.at(i, "V", t))
                            if t == 0:
                                dve.wait_ge(pe_s.sem, pe_s.before(i, "A", QUADS - 1))
                            op = vv.tensor_tensor(v[:, t, :, 0:KPH], ps_m[:, bank["V", t], 0:LAT].rearrange("p (h e) -> p h e", e=KPH),
                                                  vb[:, :].rearrange("p (h e) -> p h e", e=KPH), ALU.add)
                        elif kind == "M":
                            h, t = key[1:]
                            dve.wait_ge(pe_s.sem, pe_s.at(i, "S", h, t))
                            if t == 0:
                                dve.wait_ge(act_s.sem, act_s.before(i, "X", h, TT - 1))
                            op = vv.tensor_reduce(out=mx[:, h, t:t + 1], in_=ps_s[:, t, :], axis=AX.X, op=ALU.max, negate=True)
                        elif kind == "I":
                            h = key[1]
                            dve.wait_ge(act_s.sem, act_s.at(i, "X", h, TT - 1))
                            if h == 0:
                                dve.wait_ge(dve_s.sem, dve_s.before(i, "AO", TT - 1))
                            op = vv.reciprocal(ri[:, :, h], rs[:, h, :])
                        elif kind == "E":
                            h, j = key[1:]
                            dve.wait_ge(pe_s.sem, pe_s.at(i, "P", h, j))
                            if j == 0 and h % 4 == 0:
                                a = h // 4
                                dve.wait_ge(pe_s.sem, pe_s.at(i, "A", a - 2) if a >= 2 else pe_s.before(i, "A", a + QUADS - 2))
                            op = vv.tensor_copy(pt[:, h % 8, j, :], ps_p[:, j % 2, :])
                        elif kind == "AO":
                            t = key[1]
                            dve.wait_ge(pe_s.sem, pe_s.at(i, "BT", t))
                            if t == 0:
                                dve.wait_ge(dve_s.sem, dve_s.at(i, "I", MH - 1))
                                dve.wait_ge(pe_s.sem, pe_s.before(i, "CT"))
                            op = vv.tensor_tensor(ao[:, t, :].rearrange("p (h e) -> p h e", e=KPH),
                                                  ps_m[:, bank["BT", t], :].rearrange("p (h e) -> p h e", e=32)[:, :, 0:KPH],
                                                  ri[:, t, :].unsqueeze(2).broadcast_to([P, MH, KPH]), ALU.mult)
                        elif kind == "CH":
                            dve.wait_ge(pe_s.sem, pe_s.at(i, "CT"))
                            dve.wait_ge(pe_s.sem, pe_s.before(i, "MO", TT - 1))
                            op = vv.tensor_copy(ch[:, :], ps_m[:, bank["CT",], :])
                        elif kind == "CL":
                            dve.wait_ge(dve_s.sem, dve_s.at(i, "CH"))
                            op = vv.tensor_tensor(cl[:, :], ps_m[:, bank["CT",], :], ch[:, :].bitcast(F32), ALU.subtract)
                        elif kind == "MB":
                            c = key[1]
                            dve.wait_ge(pe_s.sem, pe_s.at(i, "MT", c))
                            hold(dve, dve_s.sem, dve_s.before(i, "ML", c))
                            op = vv.tensor_scalar(mt[:, c, :], ps_m[:, bank["MT", c], :], ocol[:, c:c + 1], None, ALU.add)
                        elif kind == "MH":
                            c = key[1]
                            dve.wait_ge(dve_s.sem, dve_s.at(i, "MB", c))
                            if c == 0:
                                dve.wait_ge(pe_s.sem, pe_s.before(i, "RL"))
                            op = vv.tensor_copy(mth[:, c, :], mt[:, c, :])
                        elif kind == "ML":
                            c = key[1]
                            dve.wait_ge(dve_s.sem, dve_s.at(i, "MH", c))
                            op = vv.tensor_tensor(mtl[:, c, :], mt[:, c, :], mth[:, c, :].bitcast(F32), ALU.subtract)
                        elif kind == "MO":
                            t = key[1]
                            dve.wait_ge(pe_s.sem, pe_s.at(i, "MO", t))
                            dve.wait_ge(stored[t % 2], 32 * i + 16 * (t // 2) + 32)
                            op = vv.tensor_tensor(mo[:, t % 2, :], ps_m[:, bank["MO", t], 0:D], orow[:, :], ALU.add)
                        elif kind == "LG":
                            dve.wait_ge(pe_s.sem, pe_s.at(i, "RL"))
                            dve.wait_ge(dve_s.sem, dve_s.before(i, "COMB"))
                            op = vv.tensor_tensor(A3(lg), ps_m[:, bank["RL",], 0:TT * E_].rearrange("p (t e) -> p t e", e=E_), per_expert(rrow), ALU.add)
                        else:
                            if kind == "LD":
                                dve.wait_ge(act_s.sem, act_s.before(i, "EX"))
                            if kind == "ES":
                                dve.wait_ge(act_s.sem, act_s.at(i, "EX"))
                            if kind == "COMB":
                                dve.wait_ge(comb_stored, 16 * i + 16)
                            dve.wait_ge(dve_s.sem, dve_s.at(i, *dve_o[n_ - 1]))
                            op = route[kind]()
                        op.then_inc(dve_s.sem, 1)

            @block.scalar
            def _(act):
                act.sem_inc(act_s.sem, act_s.per)
                act.wait_ge(weights_in, 16 * 11)
                for raw, hi, _ in splits:
                    nc.scalar.copy(flat(hi), flat(raw)).then_inc(hi_split, 1)
                with act.Fori(0, BATCH) as i:
                    for key in act_o:
                        kind = key[0]
                        if kind == "X":
                            h, t = key[1:]
                            act.wait_ge(dve_s.sem, dve_s.at(i, "M", h, t))
                            if t == 0:
                                act.wait_ge(pe_s.sem, pe_s.at(i, "P", h - 2, TT - 1) if h >= 2 else pe_s.before(i, "P", h + MH - 2, TT - 1))
                                act.wait_ge(dve_s.sem, dve_s.before(i, "I", h))
                            op = nc.scalar.activation(probs[:, h % 2, t, :], ps_s[:, t, :], ACT.Exp, bias=mx[:, h, t:t + 1], scale=1.0, accum_out=rs[:, h, t:t + 1])
                        elif kind == "E":
                            h, j = key[1:]
                            act.wait_ge(pe_s.sem, pe_s.at(i, "P", h, j))
                            if j == 1 and h % 4 == 0:
                                a = h // 4
                                act.wait_ge(pe_s.sem, pe_s.at(i, "A", a - 2) if a >= 2 else pe_s.before(i, "A", a + QUADS - 2))
                            op = nc.scalar.copy(pt[:, h % 8, j, :], ps_p[:, j % 2, :])
                        elif kind == "OT":
                            a = key[1]
                            act.wait_ge(pe_s.sem, pe_s.at(i, "A", a))
                            act.wait_ge(pe_s.sem, pe_s.before(i, "BT", TT - 1))
                            op = nc.scalar.copy(ot[:, a, :], ps_m[:, bank["A", a], :])
                        elif kind == "EX":
                            act.wait_ge(dve_s.sem, dve_s.at(i, "LD"))
                            op = nc.scalar.activation(pr[:, :, :].rearrange("p t e -> p (t e)"), ex[:, :, :].rearrange("p t e -> p (t e)"), ACT.Exp)
                        op.then_inc(act_s.sem, 1)

            @block.gpsimd
            def _(pool):
                pool.sem_inc(pool_s.sem, pool_s.per)
                with pool.Fori(0, BATCH) as i:
                    for _, n in pool_o:
                        hold(pool, dve_s.sem, dve_s.at(i, "YB", n))
                        hold(pool, dve_s.sem, dve_s.at(i, "YS", n - 2) if n >= 2 else dve_s.before(i, "YS", n + 2 * QUADS - 2))
                        nc.gpsimd.tensor_copy(yh[:, n % 2, :], y[:, n % 2, :]).then_inc(pool_s.sem, 1)


def dense_experts(nc, const, x_in, m_in, comb_in, w1, b1, w2, b2, x_out, name):
    F = w1.shape[2]
    FT = F // P
    ctx = ExitStack()
    with ctx:
        sb = lambda n, s, dt=F32: ctx.enter_context(nc.sbuf_tensor(f"{name}_{n}", s, dt))
        sem = lambda n: ctx.enter_context(nc.semaphore(f"{name}_{n}"))
        ident = const["ident"]
        w1h, w1l = (sb(n, [P, E_, KD, F], F32R) for n in ("w1h", "w1l"))
        w2h, w2l = (sb(n, [P, E_, FT, D], F32R) for n in ("w2h", "w2l"))
        b1c = sb("b1c", [P, E_, FT])
        b2r = sb("b2r", [E_, D])
        work = sb("work", [P, 4, TT * D])
        xc, mc, xb, acc = (work[:, n, :].rearrange("p (t d) -> p t d", d=D) for n in range(4))
        comb = sb("comb", [P, TT, E_])
        combt = sb("combt", [E_, SEQ])
        xth, xtl = (sb(n, [P, KD, SEQ], F32R) for n in ("xth", "xtl"))
        g = sb("g", [P, 2, SEQ])
        gh, gl = (sb(n, [P, 2, FT, SEQ], F32R) for n in ("gh", "gl"))
        st6, mv, vare, rstd = sb("st6", [P, TT, 6]), sb("mv", [P, TT, 2]), sb("vare", [P, TT, 1]), sb("rstd", [P, TT, 1])
        ps = ctx.enter_context(nc.psum_tensor(f"{name}_ps", [P, 8, SEQ], F32))
        small_in, staged, hi_split, lo_split = sem("small_in"), [sem(f"staged{k}") for k in range(4)], sem("hi_split"), sem("lo_split")
        x_loaded, stored = sem("x_loaded"), sem("stored")
        hold = gated_hold(sem("held"))

        pe_o = [("T", k) for k in range(KD)] + [("C", n) for n in range(2)] + [("Z", t) for t in range(TT)]
        dve_o = [(n, k) for k in range(KD) for n in ("XH", "XL")] + [("CC", n) for n in range(2)] + [("XB",)] + [("ZA", t) for t in range(TT)]
        act_o, pool_o = [], []
        for e in range(E_ + 1):
            if e < E_:
                pe_o += [("H", e, m) for m in range(FT)]
                act_o += [("G", e, m) for m in range(FT)]
                dve_o += [(n, e, m) for m in range(FT) for n in ("GH", "GL")]
            if e >= 1:
                pe_o += [("Y", e - 1, t) for t in range(TT)]
                dve_o += [("AC", e - 1, t) for t in range(TT)]
        for t in range(TT):
            dve_o += [("F", t)]
        for t in range(TT):
            dve_o += [("B", t)]
        for t in range(TT):
            dve_o += [("S", t)]
        pool_o += [("EPS",), ("RSTD",)]
        dve_o += [("N", t) for t in range(TT)]
        pe_s, dve_s = LoopSteps(sem("tensor_steps"), pe_o), LoopSteps(sem("vector_steps"), dve_o)
        act_s, pool_s = LoopSteps(sem("scalar_steps"), act_o), LoopSteps(sem("gpsimd_steps"), pool_o)
        BANKS = 8
        assert len(pe_o) % BANKS == 0, len(pe_o)
        bank = {k: n % BANKS for n, k in enumerate(pe_o)}
        reader = {"T": (dve_s, "XL"), "C": (dve_s, "CC"), "Z": (dve_s, "ZA"), "H": (act_s, "G"), "Y": (dve_s, "AC")}
        pieces = [(e, n) for e in range(E_) for n in range(2)]

        def piece(e, n):
            raw = work[:, (2 * e + n) % 4, :]
            hi, lo = ((w1h, w1l), (w2h, w2l))[n]
            f = lambda x: x[:, e, :, :].rearrange("p k n -> p (k n)")
            return raw, f(hi), f(lo)

        with nc.Block() as block:

            @block.sync
            def _(sp):
                sp.sem_inc(stored, 64)
                sp.dma_start(b1c[:, :, :], b1).then_inc(small_in, 16)
                sp.dma_start(b2r[:, :], b2).then_inc(small_in, 16)
                for c, (e, n) in enumerate(pieces):
                    if c >= 4:
                        hold(sp, lo_split, c - 3)
                    src = (w1, w2)[n][e].rearrange("(k p) n -> p k n", p=P)
                    sp.dma_start(piece(e, n)[0].rearrange("p (k n) -> p k n", n=src.shape[2]), src).then_inc(staged[c % 4], 16)
                hold(sp, lo_split, len(pieces))
                with sp.Fori(0, BATCH) as i:
                    hold(sp, dve_s.sem, dve_s.before(i, "AC", E_ - 1, TT - 1))
                    tok = "o (t p) d -> p (o t) d"
                    sp.dma_start(mc, m_in[bass.ds(i, 1), :, :].rearrange(tok, p=P)).then_inc(x_loaded, 16)
                    sp.dma_start(xc, x_in[bass.ds(i, 1), :, :].rearrange(tok, p=P)).then_inc(x_loaded, 16)
                    sp.dma_start(comb[:, :, :], comb_in[bass.ds(i, 1), :, :].rearrange(tok, p=P)).then_inc(x_loaded, 16)
                    for t in range(TT):
                        hold(sp, dve_s.sem, dve_s.at(i, "N", t))
                        sp.dma_start(x_out[bass.ds(i, 1), P * t:P * t + P, :].rearrange("o p d -> p (o d)"), acc[:, t, :]).then_inc(stored, 16)
                hold(sp, stored, 64 * BATCH + 64)

            @block.tensor
            def _(pe):
                pe.sem_inc(pe_s.sem, pe_s.per)
                pe.wait_ge(lo_split, len(pieces))
                with pe.Fori(0, BATCH) as i:
                    for n, key in enumerate(pe_o):
                        kind = key[0]
                        m = ps[:, bank[key], :]
                        was = pe_o[n - BANKS]
                        steps, rk = reader[was[0]]
                        pe.wait_ge(steps.sem, (steps.at if n >= BANKS else steps.before)(i, rk, *was[1:]))
                        if kind == "T":
                            if key[1] == 0:
                                pe.wait_ge(x_loaded, 48 * i + 48)
                            for t in range(TT):
                                last = nc.tensor.transpose(m[:, P * t:P * t + P], mc[:, t, P * key[1]:P * key[1] + P], ident[:, :])
                        elif kind == "C":
                            for t in (2 * key[1], 2 * key[1] + 1):
                                last = nc.tensor.transpose(m[0:E_, P * (t % 2):P * (t % 2) + P], comb[:, t, :], ident[:, :])
                        elif kind == "Z":
                            t = key[1]
                            if t == 0:
                                pe.wait_ge(dve_s.sem, dve_s.at(i, "CC", 1))
                                pe.wait_ge(small_in, 32)
                            last = nc.tensor.matmul(m[:, 0:D], combt[:, P * t:P * t + P], b2r[:, :], start=True, stop=True)
                        elif kind == "H":
                            e, f = key[1:]
                            if (e, f) == (0, 0):
                                pe.wait_ge(dve_s.sem, dve_s.at(i, "XL", KD - 1))
                            cols = slice(P * f, P * f + P)
                            last = sum_of_parts(nc, m, lambda k: w1h[:, e, k, cols], lambda k: w1l[:, e, k, cols], lambda k: xth[:, k, :], lambda k: xtl[:, k, :], KD)
                        elif kind == "Y":
                            e, t = key[1:]
                            tok = slice(P * t, P * t + P)
                            if t == 0:
                                pe.wait_ge(dve_s.sem, dve_s.at(i, "GL", e, FT - 1))
                            last = sum_of_parts(nc, m[:, 0:D], lambda k: gh[:, e % 2, k, tok], lambda k: gl[:, e % 2, k, tok], lambda k: w2h[:, e, k, :], lambda k: w2l[:, e, k, :], FT)
                        last.then_inc(pe_s.sem, 1)

            @block.vector
            def _(dve):
                dve.sem_inc(dve_s.sem, dve_s.per)
                for c, (e, n) in enumerate(pieces):
                    raw, hi, lo = piece(e, n)
                    dve.wait_ge(hi_split, c + 1)
                    nc.vector.tensor_tensor(lo, raw, hi.bitcast(F32), ALU.subtract).then_inc(lo_split, 1)
                with dve.Fori(0, BATCH) as i:
                    for key in dve_o:
                        kind = key[0]
                        t = k = key[-1]
                        if kind == "XH":
                            dve.wait_ge(pe_s.sem, pe_s.at(i, "T", k))
                            if k == 0:
                                dve.wait_ge(pe_s.sem, pe_s.before(i, "H", E_ - 1, FT - 1))
                            op = nc.vector.tensor_copy(xth[:, k, :], ps[:, bank["T", k], :])
                        elif kind == "XL":
                            dve.wait_ge(dve_s.sem, dve_s.at(i, "XH", k))
                            op = nc.vector.tensor_tensor(xtl[:, k, :], ps[:, bank["T", k], :], xth[:, k, :].bitcast(F32), ALU.subtract)
                        elif kind == "CC":
                            dve.wait_ge(pe_s.sem, pe_s.at(i, "C", k))
                            dve.wait_ge(pe_s.sem, pe_s.before(i, "Z", TT - 1))
                            op = nc.vector.tensor_copy(combt[:, 2 * P * k:2 * P * k + 2 * P], ps[0:E_, bank["C", k], 0:2 * P])
                        elif kind == "XB":
                            dve.wait_ge(dve_s.sem, dve_s.before(i, "N", TT - 1))
                            op = nc.vector.tensor_scalar(xb, xc, 2.0, None, ALU.mult)
                        elif kind == "ZA":
                            dve.wait_ge(pe_s.sem, pe_s.at(i, "Z", t))
                            if t == 0:
                                dve.wait_ge(stored, 64 * i + 64)
                            op = nc.vector.tensor_copy(acc[:, t, :], ps[:, bank["Z", t], 0:D])
                        elif kind == "GH":
                            e, m = key[1:]
                            dve.wait_ge(act_s.sem, act_s.at(i, "G", e, m))
                            if m == 0:
                                dve.wait_ge(pe_s.sem, pe_s.at(i, "Y", e - 2, TT - 1) if e >= 2 else pe_s.before(i, "Y", e + E_ - 2, TT - 1))
                            op = nc.vector.tensor_copy(gh[:, e % 2, m, :], g[:, m % 2, :])
                        elif kind == "GL":
                            e, m = key[1:]
                            dve.wait_ge(dve_s.sem, dve_s.at(i, "GH", e, m))
                            op = nc.vector.tensor_tensor(gl[:, e % 2, m, :], g[:, m % 2, :], gh[:, e % 2, m, :].bitcast(F32), ALU.subtract)
                        elif kind == "AC":
                            e = key[1]
                            dve.wait_ge(pe_s.sem, pe_s.at(i, "Y", e, t))
                            dve.wait_ge(dve_s.sem, dve_s.at(i, "AC", e - 1, t) if e else dve_s.at(i, "ZA", t))
                            op = nc.vector.scalar_tensor_tensor(out=acc[:, t, :], in0=ps[:, bank[("Y", e, t)], 0:D], scalar=comb[:, t, e:e + 1], in1=acc[:, t, :], op0=ALU.mult, op1=ALU.add)
                        elif kind == "F":
                            dve.wait_ge(dve_s.sem, dve_s.at(i, "AC", E_ - 1, t))
                            op = nc.vector.scalar_tensor_tensor(out=xb[:, t, :], in0=acc[:, t, :], scalar=0.3, in1=xb[:, t, :], op0=ALU.mult, op1=ALU.add)
                        elif kind == "B":
                            dve.wait_ge(dve_s.sem, dve_s.at(i, "F", t))
                            op = nc.vector.bn_stats(st6[:, t, :], xb[:, t, :])
                        elif kind == "S":
                            hold(dve, dve_s.sem, dve_s.at(i, "B", t))
                            op = nc.vector.bn_aggr(mv[:, t, :], st6[:, t, :])
                        elif kind == "N":
                            dve.wait_ge(pool_s.sem, pool_s.at(i, "RSTD"))
                            op = nc.vector.tensor_scalar(acc[:, t, :], xb[:, t, :], mv[:, t, 0:1], rstd[:, t, :], ALU.subtract, ALU.mult)
                        op.then_inc(dve_s.sem, 1)

            @block.scalar
            def _(act):
                act.sem_inc(act_s.sem, act_s.per)
                for c, (e, n) in enumerate(pieces):
                    raw, hi, lo = piece(e, n)
                    act.wait_ge(staged[c % 4], 16 * (c // 4) + 16)
                    nc.scalar.copy(hi, raw).then_inc(hi_split, 1)
                act.wait_ge(small_in, 32)
                with act.Fori(0, BATCH) as i:
                    for _, e, m in act_o:
                        act.wait_ge(pe_s.sem, pe_s.at(i, "H", e, m))
                        n = FT * e + m - 2
                        act.wait_ge(dve_s.sem, dve_s.at(i, "GL", n // FT, n % FT) if n >= 0 else dve_s.before(i, "GL", E_ - 1, FT + n))
                        nc.scalar.activation(g[:, m % 2, :], ps[:, bank["H", e, m], :], ACT.Gelu, bias=b1c[:, e, m:m + 1], scale=1.0).then_inc(act_s.sem, 1)

            @block.gpsimd
            def _(pool):
                pool.sem_inc(pool_s.sem, pool_s.per)
                with pool.Fori(0, BATCH) as i:
                    hold(pool, dve_s.sem, dve_s.at(i, "S", TT - 1))
                    nc.gpsimd.tensor_scalar(vare[:, :, :], mv[:, :, 1:2], EPS, None, ALU.add).then_inc(pool_s.sem, 1)
                    hold(pool, pool_s.sem, pool_s.at(i, "EPS"))
                    hold(pool, dve_s.sem, dve_s.before(i, "N", TT - 1))
                    nc.gpsimd.tensor_tensor(rstd[:, :, :], vare[:, :, :], const["minus_half"][:, :].unsqueeze(1).broadcast_to([P, TT, 1]), ALU.pow).then_inc(pool_s.sem, 1)


def constants(nc, ctx, ident_in):
    ident = ctx.enter_context(nc.sbuf_tensor("ident", [P, P], F32))
    minus_half = ctx.enter_context(nc.sbuf_tensor("minus_half", [P, 1], F32))
    ready = ctx.enter_context(nc.semaphore("constants_ready"))
    with nc.Block() as block:

        @block.gpsimd
        def _(pool):
            nc.gpsimd.memset(minus_half[:, :], -0.5)
            nc.gpsimd.memset(ident[:, :], 0.0).then_inc(ready, 1)
            pool.wait_ge(ready, 1)
            nc.gpsimd.affine_select(out=ident[:, :], in_=ident[:, :], compare_op=ALU.not_equal, fill=1.0,
                                    base=0, pattern=[[-1, P]], channel_multiplier=1).then_inc(ready, 1)
            pool.wait_ge(ready, 2)
    return {"ident": ident, "minus_half": minus_half, "ready": ready, "count": 2}


def build(nc, a, out):
    ctx = ExitStack()
    with ctx:
        const = constants(nc, ctx, None)
        x1, x2, x3 = (nc.dram_tensor(n, [BATCH, SEQ, D], F32, kind="Internal").ap() for n in ("x1", "x2", "x3"))
        mla = {k[7:]: v for k, v in a.items() if k.startswith("L1_ffn_")}
        m4 = nc.dram_tensor("m4", [BATCH, SEQ, D], F32, kind="Internal").ap()
        c4 = nc.dram_tensor("c4", [BATCH, SEQ, E_], F32, kind="Internal").ap()
        attention(nc, const, a["L0_attn_x"], x1, a["L0_attn_Wq"], a["L0_attn_Wkv"], a["L0_attn_Wo"], a["L0_attn_bo"], a["rope0"], None, True, "soft")
        quantized_ffn(nc, const, x1, x2, a["gamma_beta"], a["L0_ffn_fc1_q"], a["L0_ffn_fc1_scales"], a["L0_ffn_fc1_bias"], a["L0_ffn_fc2_q"], a["L0_ffn_fc2_scales"], a["L0_ffn_fc2_bias"], "ffn")
        attention(nc, const, x2, x3, a["L1_attn_Wq"], a["L1_attn_Wkv"], a["L1_attn_Wo"], None, a["rope1"], a["decay"], False, "decay")
        latent_attention(nc, const, x3, m4, c4, mla, "mla")
        dense_experts(nc, const, x3, m4, c4, mla["w1"], mla["b1"], mla["w2"], mla["b2"], out, "moe")


def tables():
    f = np.float32
    inv = (f(1.0) / np.power(f(10000.0), np.arange(0, HD, 2, dtype=f) / f(HD))).astype(f)
    ang = (np.arange(SEQ, dtype=f)[:, None] * inv[None, :]).astype(f).T
    inv64 = 1.0 / 10000.0 ** (np.arange(0, HD, 2, dtype=np.float64) / HD)
    ang64 = np.outer(np.arange(SEQ, dtype=np.float64), inv64).T
    def pack(c, s):
        rows = np.stack([np.concatenate([c, c]), np.concatenate([s, -s])]).astype(f)
        return rows.reshape(2, HD, TT, P).transpose(3, 2, 0, 1)
    slopes = np.array([2.0 ** (-8.0 / HEADS * (i + 1)) for i in range(HEADS)], f).astype(np.float64)
    dist = np.arange(SEQ)[None, :] - np.arange(P)[:, None]
    decay = np.where(dist[:, None, :] >= 0, np.exp(-slopes[None, :, None] * np.maximum(dist, 0)[:, None, :]), 0.0).astype(f)
    return {"rope0": pack(np.cos(ang), np.sin(ang)), "rope1": pack(np.cos(ang64), np.sin(ang64)), "decay": np.ascontiguousarray(decay)}


def kernel(**inputs):
    import concourse.bacc as _bacc
    from concourse.bass_utils import run_bass_kernel_spmd as _run

    nc = _bacc.Bacc("TRN2", target_bir_lowering=False, num_devices=1)
    host = {k: np.asarray(v) for k, v in inputs.items()}
    host["L1_attn_Wq"] = host["L1_attn_Wq"].T
    host["L1_attn_Wkv"] = np.concatenate([host.pop("L1_attn_Wk").T, host.pop("L1_attn_Wv").T], axis=1)
    host["L1_attn_Wo"] = host["L1_attn_Wo"].T
    host["gamma_beta"] = np.stack([host["L0_ffn_ln_gamma"], host["L0_ffn_ln_beta"]]).reshape(2, KD, P).transpose(2, 0, 1)
    host["L0_ffn_fc1_bias"] = host["L0_ffn_fc1_bias"].reshape(-1, P).T
    qw, kw = host.pop("L1_ffn_q_w"), host.pop("L1_ffn_k_w")
    qb, kb = host.pop("L1_ffn_q_b"), host.pop("L1_ffn_k_b")
    def stacked(m, width):
        m = m.reshape(m.shape[0], MH, 1, width)[:, :, :, :KPH]
        return np.broadcast_to(m, (m.shape[0], MH, VAR, KPH)).reshape(m.shape[0], MH * VAR * KPH)
    host["L1_ffn_stacks"] = np.concatenate([stacked(kw, KPH), stacked(qw, D // MH)], axis=1)
    host["L1_ffn_stack_b"] = np.concatenate([stacked(kb[None], KPH), stacked(qb[None], D // MH)], axis=1).reshape(2 * QUADS, P).T
    lo = np.array([[0, 0, -1, -1], [0, -1, 0, -1]], np.float32)
    host["L1_ffn_minus_lo"] = np.tile(np.repeat(lo, KPH, axis=1), (1, P // (VAR * KPH))).T
    host["L1_ffn_o_b_cols"] = host["L1_ffn_o_b"].reshape(KD, P).T
    host["L1_ffn_rev"] = (E_ - np.arange(E_)).astype(np.float32)
    host["L1_ffn_b1"] = host["L1_ffn_b1"].reshape(E_, -1, P).transpose(2, 0, 1)
    host.update(tables())
    arrays, aps = {}, {}
    for k, v in host.items():
        arrays["in_" + k] = np.ascontiguousarray(v)
        aps[k] = nc.dram_tensor("in_" + k, arrays["in_" + k].shape, mybir.dt.from_np(arrays["in_" + k].dtype), kind="ExternalInput").ap()
    out = nc.dram_tensor("out_x", (BATCH, SEQ, D), F32, kind="ExternalOutput").ap()
    build(nc, aps, out)
    r = _run(nc, [arrays], core_ids=[0])
    return r.results[0]["out_x"]
```

```python
from contextlib import ExitStack

import numpy as np

import concourse.bass as bass
from concourse import mybir

F32 = mybir.dt.float32
F32R = mybir.dt.float32r
I32 = mybir.dt.int32
ACT = mybir.ActivationFunctionType
ALU = mybir.AluOpType
AX = mybir.AxisListType

P = 128
BATCH, SEQ, D = 8, 512, 256
TT = SEQ // P
KD = D // P
HEADS, KVH, HD = 16, 4, 64
GRP = HEADS // KVH
PAIRS = HEADS // 2
INNER = HEADS * HD
HALF = HD // 2
EPS = 1e-5


def gated_hold(nc_sem):
    def hold(eng, semaphore, value):
        eng.wait_ge(semaphore, value)
        eng.sem_inc(nc_sem, 1)
    return hold


class Steps:

    def __init__(self, ahead_sem, main_sem, ahead, main):
        self.where = {}
        for sem, order in ((ahead_sem, ahead), (main_sem, main)):
            for n, k in enumerate(order):
                assert k not in self.where, k
                self.where[k] = (sem, n + 1, len(order))
        self.starts = [(s, len(o)) for s, o in ((ahead_sem, ahead), (main_sem, main)) if o]

    def start(self, eng):
        for sem, count in self.starts:
            eng.sem_inc(sem, count)

    def sem(self, key):
        return self.where[key][0]

    def at(self, seq, *key):
        sem, pos, per = self.where[key]
        i, offset = seq
        return sem, i * per + (per * (offset + 1) + pos)


FIRST = (0, -1)


def shift(seq, n):
    return seq[0], seq[1] + n


def last_use(i, run, key, place, ahead, order):
    mine = place[key]
    for k in reversed(run[:run.index(key)]):
        if place.get(k) == mine:
            return [(shift(i, 1 if k in ahead else 0), k)]
    found = []
    if i is FIRST:
        return found
    for part, offset in ((lambda k: k not in ahead, -1), (lambda k: k in ahead, 0)):
        users = [k for k in order if place.get(k) == mine and part(k)]
        if users:
            found.append((shift(i, offset), users[-1]))
    return found


def sum_of_parts(nc, out, a_hi, a_lo, b_hi, b_lo, tiles, before_last=None):
    for k in range(tiles):
        if before_last and k == tiles - 1:
            before_last()
        for n, (a, b) in enumerate(((a_hi, b_hi), (a_hi, b_lo), (a_lo, b_hi))):
            last = nc.tensor.matmul(out, a(k), b(k), start=(k == 0 and n == 0), stop=(k == tiles - 1 and n == 2))
    return last


def turns(eng, run_steps, ahead, order, before_loop=None):
    run_steps(FIRST, ahead)
    if before_loop:
        before_loop()
    with eng.Fori(0, BATCH - 1) as i:
        run_steps((i, 0), order)
    run_steps((BATCH - 1, 0), [k for k in order if k not in ahead])


def attention(nc, const, x_in, x_out, w_q, w_kv, w_o, out_bias, rope_tab, decay_tab, softmax, name):
    ctx = ExitStack()
    with ctx:
        sb = lambda n, s, dt=F32: ctx.enter_context(nc.sbuf_tensor(f"{name}_{n}", s, dt))
        sem = lambda n: ctx.enter_context(nc.semaphore(f"{name}_{n}"))
        ident = const["ident"]
        KVW = KVH * HD
        HH = HEADS // 2
        wqh, wql = (sb(n, [P, KD, INNER], F32R) for n in ("wqh", "wql"))
        wkh, wkl = (sb(n, [P, KD, 2 * KVW], F32R) for n in ("wkh", "wkl"))
        woh, wol = (sb(n, [P, PAIRS, D], F32R) for n in ("woh", "wol"))
        if out_bias is not None:
            bias = sb("bias", [P, D])
        rope = sb("rope", [P, TT, 2, HD])
        xc = sb("xc", [P, TT, D])
        xb = sb("xb", [P, TT, D])
        xth, xtl = (sb(n, [P, KD, SEQ], F32R) for n in ("xth", "xtl"))
        rt = sb("rt", [P, 2, HH * HD])
        st = sb("st", [P, 2, HH * 2 * HD])
        qs = sb("qs", [P, HEADS, SEQ], F32R)
        ks = sb("ks", [P, 2, KVH, SEQ], F32R)
        v = sb("v", [P, 2, TT, KVW])
        first_q = [0 if softmax else P * j for j in range(TT)]
        head_cols = sum(SEQ - c for c in first_q)
        LATE = PAIRS * D // SEQ
        HI_ACT = not softmax
        RING = 3
        pt = sb("pt", [P, RING * head_cols])
        if softmax:
            probs = sb("probs", [P, 2, TT, SEQ])
            rs = sb("rs", [P, HEADS, TT])
            ri = sb("ri", [P, TT, HEADS])
            mx = sb("mx", [P, HEADS, TT])
            rrep = sb("rrep", [P, SEQ])
        else:
            dec = sb("dec", [P, HEADS, SEQ])
        if softmax:
            ot = sb("ot", [P, SEQ])
        ath, atl = (sb(n, [P, PAIRS, SEQ], F32R) for n in ("ath", "atl"))
        r = sb("r", [P, 2, D])
        st6, mv, vare, rstd = sb("st6", [P, 2, 6]), sb("mv", [P, 2, 2]), sb("vare", [P, 2, 1]), sb("rstd", [P, 2, 1])
        ps_s = ctx.enter_context(nc.psum_tensor(f"{name}_ps_s", [P, 4, SEQ], F32))
        if softmax:
            ps_p = ctx.enter_context(nc.psum_tensor(f"{name}_ps_p", [P, 2, SEQ], F32))
        MISC = 2 if softmax else 4
        ps_m = ctx.enter_context(nc.psum_tensor(f"{name}_ps_m", [P, MISC, SEQ], F32))

        def weights_of(h, j):
            at = (h % RING) * head_cols + sum(SEQ - c for c in first_q[:j])
            return pt[:, at:at + SEQ - first_q[j]]

        def pairs_before(h):
            if h >= RING:
                return 0, (h - RING) // 2
            return -1, max(x for x in range(HEADS) if x % RING == h % RING) // 2

        weights_in, hi_split, weights_split = [sem(f"weights_in{n}") for n in range(3)], sem("hi_split"), sem("weights_split")
        rope_in, bias_in = sem("rope_in"), sem("bias_in")
        keys_scaled, decay_in, late_decay_in = sem("keys_scaled"), sem("decay_in"), sem("late_decay_in")
        x_loaded = sem("x_loaded")
        stored = [sem(f"stored{s}") for s in range(2)]
        hold = gated_hold(sem("held"))

        units = [("Q", 1, t) for t in range(TT)] + [("Q", 0, t) for t in range(TT)] + [("KV", t) for t in range(TT)]
        turned = lambda u: [("QT",) + u[1:] + (b,) for b in range(2)] if u[0] == "Q" else [("KT", u[1], b) for b in range(2)]
        pe_o, dve_o, act_o, pool_o = [], [], [], []

        def project(u):
            pe_o.append(u)
            dve_o.append(("ROT",) + u)
            if u[0] == "KV":
                dve_o.append(("VC", u[1]))
            pool_o.extend((n,) + u for n in (("Y0", "Y1", "HI", "LO") if not HI_ACT else ("Y0", "Y1", "LO")))
            if HI_ACT:
                act_o.append(("HI",) + u)

        def turn_over(u):
            pe_o.extend(turned(u))
            act_o.extend(("C",) + k for k in turned(u))

        rows = {("Q", 1): ((0, 2), (1, 3), (2, 4), (3, 5)), ("Q", 0): ((9, 11), (10, 12), (11, 13), (12, 14)), ("KV",): ((14, 16), (15, 17), (16, 18), (17, 19))}
        LOOK = 8
        plan = {u + (t,): rows[u][t] for u in rows for t in range(TT)}
        aside = {}
        for unit, (at, back) in plan.items():
            aside.setdefault(at, []).append((1, project, unit))
            aside.setdefault(back, []).append((0, turn_over, unit))
        step_order = "S0 S1 R I A0 P0 A1 P1 S2 S3 T A2 P2 A3 P3 O" if softmax else "S0 S1 S2 T S3 A0 A1 A2 A3 O"
        for h in range(HEADS + 2):
            now, old = h < HEADS, 0 <= h - 1 < HEADS
            lag = 3 if softmax else 2
            p = (h - lag) // 2 if h >= lag and (h - lag) % 2 == 0 and (h - lag) // 2 < PAIRS else None
            for token in step_order.split():
                kind, c = token[0], int(token[1:] or 0)
                if kind == "S" and now:
                    pe_o.append(("S", h, c)); dve_o.append(("M", h, c))
                    if softmax: act_o.append(("X", h, c))
                elif kind == "T" and h == LOOK:
                    pe_o += [("T", k) for k in range(KD)]
                    dve_o += [(n, k) for k in range(KD) for n in ("XH", "XL")]
                elif kind == "I" and softmax and old:
                    dve_o.append(("I", h - 1))
                elif kind == "R" and softmax and p is not None:
                    pe_o.append(("R", p)); act_o.append(("RC", p))
                elif kind == "A" and p is not None:
                    pe_o.append(("A", p, c))
                    if not softmax and c == TT - 1: act_o.append(("RC", p))
                elif kind == "O" and p is not None:
                    dve_o.append(("O", p))
                    if softmax: pool_o += [("OH", p), ("OL", p)]
                elif kind == "P" and softmax and old:
                    pe_o.append(("P", h - 1, c))
                    if c % 2: act_o.append(("E", h - 1, c))
                    else: dve_o.append(("E", h - 1, c))
            for _, what, u in sorted(aside.get(h, []), key=lambda x: x[0]):
                what(u)
        dve_o.append(("VV",))
        for t in range(TT + 1):
            if t < TT:
                pe_o.append(("W", t))
                for _, what, u in sorted(aside.get(HEADS + 2 + t, []), key=lambda x: x[0]):
                    what(u)
                dve_o += [("F", t), ("B", t), ("G", t)]; pool_o += [("EPS", t), ("RSTD", t)]
            if t >= 1: dve_o.append(("N", t - 1))
        dve_o.append(("XB",))
        is_ahead = lambda k: (k[0] in ("T", "XH", "XL", "KV", "KT", "VC", "VV", "XB") or k[:2] in (("Q", 0), ("QT", 0))
                              or k[1:3] in (("Q", 0), ("QT", 0)) or k[1:2] in (("KV",), ("KT",)))
        S = {}
        ahead = {}
        for eng_name, o in (("tensor", pe_o), ("vector", dve_o), ("scalar", act_o), ("gpsimd", pool_o)):
            ahead[eng_name] = [k for k in o if is_ahead(k)]
            S[eng_name] = Steps(sem(f"{eng_name}_ahead"), sem(f"{eng_name}_main"), ahead[eng_name], [k for k in o if not is_ahead(k)])
        pe_s, dve_s, act_s, pool_s = (S[n] for n in ("tensor", "vector", "scalar", "gpsimd"))

        misc = [k for k in pe_o if k[0] not in ("S", "P")]
        misc = [k[:2] if k[0] == "A" else k for k in misc if k[0] != "A" or k[2] == 0]
        bank = {k: n % MISC for n, k in enumerate(misc)}
        st_place = {k: n % 2 for n, k in enumerate(units)}
        hi_s, hi_o = (act_s, act_o) if HI_ACT else (pool_s, pool_o)
        hi_place = {("HI",) + k: n for k, n in st_place.items()}
        rt_place = {("ROT",) + k: 0 for k in units}
        emptied = {"T": lambda k: (dve_s, ("XL", k[1])), "KV": lambda k: (dve_s, ("VC", k[1])), "Q": lambda k: (dve_s, ("ROT",) + k),
                   "QT": lambda k: (act_s, ("C",) + k), "KT": lambda k: (act_s, ("C",) + k), "R": lambda k: (act_s, ("RC", k[1])),
                   "A": lambda k: (dve_s, ("O", k[1])), "W": lambda k: (dve_s, ("F", k[1]))}
        own = lambda i, key: (i[0], i[1] + 1) if is_ahead(key) else i

        def raw_and_parts():
            nq, nkv, no = KD * INNER, KD * 2 * KVW, PAIRS * D
            late = pt[:, nq + nkv:nq + nkv + no] if softmax else dec[:, HEADS - LATE:HEADS, :].rearrange("p h s -> p (h s)")
            return ((pt[:, 0:nq], wqh, wql), (pt[:, nq:nq + nkv], wkh, wkl), (late, woh, wol))

        flat = lambda x: x[:, :, :].rearrange("p k n -> p (k n)")

        def rows_of(u):
            heads = HH if u[0] == "Q" else KVH
            width = 2 * HD if u[0] == "Q" else 3 * HD
            return (heads, rt[:, 0, 0:heads * HD].rearrange("p (h d) -> p h d", d=HD),
                    st[:, st_place[u], 0:heads * width].rearrange("p (h d) -> p h d", d=width))

        def make_hi(eng, copy, i, run, key):
            u, j = key[1:], own(i, key)
            hold(eng, *pool_s.at(j, "Y1", *u))
            for seq, k in last_use(i, [k for k in run if k[0] == "HI"], key, hi_place, ahead["scalar" if HI_ACT else "gpsimd"], hi_o):
                hold(eng, *pe_s.at(seq, *turned(k[1:])[1]))
            heads, rows, stack = rows_of(u)
            if u[0] == "Q":
                return copy(stack[:, :, 0:HD].bitcast(F32R), rows)
            return copy(stack.rearrange("p h (c d) -> p h c d", d=HD)[:, :, 0:3:2, :].bitcast(F32R), rows.unsqueeze(2).broadcast_to([P, heads, 2, HD]))

        with nc.Block() as block:

            @block.sync
            def _(sp):
                for s in range(2):
                    sp.sem_inc(stored[s], 32)

                def load(i, index):
                    hold(sp, *pe_s.at(shift(i, -1), "T", KD - 1))
                    hold(sp, *dve_s.at(shift(i, -1), "XB"))
                    sp.dma_start(xc[:, :, :], x_in[bass.ds(index, 1), :, :].rearrange("o (t p) d -> p (o t) d", p=P)).then_inc(x_loaded, 16)

                raw_q, raw_kv, raw_o = (raw for raw, _, _ in raw_and_parts())
                load((0, 0), 0)
                sp.dma_start(raw_q.rearrange("p (k n) -> p k n", k=KD), w_q.rearrange("(k p) n -> p k n", p=P)).then_inc(weights_in[0], 16)
                sp.dma_start(raw_kv.rearrange("p (k n) -> p k n", k=KD), w_kv.rearrange("(k p) n -> p k n", p=P)).then_inc(weights_in[1], 16)
                sp.dma_start(rope[:, :, :, :], rope_tab).then_inc(rope_in, 16)
                sp.dma_start(raw_o.rearrange("p (k n) -> p k n", k=PAIRS), w_o.rearrange("(k p) n -> p k n", p=P)).then_inc(weights_in[2], 16)
                if softmax:
                    sp.dma_start(bias[:, :], out_bias.partition_broadcast(P)).then_inc(bias_in, 16)
                else:
                    sp.dma_start(dec[:, 0:HEADS - LATE, :], decay_tab[:, 0:HEADS - LATE, :]).then_inc(decay_in, 16)
                    hold(sp, weights_split, 3)
                    sp.dma_start(dec[:, HEADS - LATE:HEADS, :], decay_tab[:, HEADS - LATE:HEADS, :]).then_inc(late_decay_in, 16)

                def store(i, index):
                    for t in range(TT):
                        hold(sp, *dve_s.at(i, "N", t))
                        sp.dma_start(x_out[bass.ds(index, 1), P * t:P * t + P, :].rearrange("o p d -> p (o d)"), r[:, t % 2, :]).then_inc(stored[t % 2], 16)

                with sp.Fori(0, BATCH - 1) as i:
                    load((i, 1), i + 1)
                    store((i, 0), i)
                store((BATCH - 1, 0), BATCH - 1)
                for s in range(2):
                    hold(sp, stored[s], 32 * BATCH + 32)

            @block.tensor
            def _(pe):
                pe_s.start(pe)

                def steps(i, run):
                    in_misc = [x for x in misc if x in run or x + (0,) in run]
                    for key in run:
                        kind, j = key[0], own(i, key)
                        product = key[:2] if kind == "A" else key
                        if product in bank:
                            m = ps_m[:, bank[product], :]
                        if product in bank and (kind != "A" or key[2] == 0):
                            for seq, k in last_use(i, in_misc, product, bank, ahead["tensor"], misc):
                                who, step = emptied[k[0]](k)
                                pe.wait_ge(*who.at(seq, *step))
                        if kind == "T":
                            k = key[1]
                            if k == 0:
                                pe.wait_ge(x_loaded, 16 * j[0] + 16 * j[1] + 16)
                            for t in range(TT):
                                last = nc.tensor.transpose(m[:, P * t:P * t + P], xc[:, t, P * k:P * k + P], ident[:, :])
                        elif kind in ("Q", "KV"):
                            t = key[-1]
                            pe.wait_ge(weights_split, 1 if kind == "Q" else 2)
                            pe.wait_ge(*dve_s.at(j, "XL", KD - 1))
                            tok = slice(P * t, P * t + P)
                            c0 = HH * HD * key[1] if kind == "Q" else 0
                            hi, lo = (wqh, wql) if kind == "Q" else (wkh, wkl)
                            last = sum_of_parts(nc, m, lambda k: xth[:, k, tok], lambda k: xtl[:, k, tok],
                                                lambda k: hi[:, k, c0:c0 + SEQ], lambda k: lo[:, k, c0:c0 + SEQ], KD)
                        elif kind in ("QT", "KT"):
                            u, b = (key[0][0] + ("V" if kind == "KT" else ""),) + key[1:-1], key[-1]
                            pe.wait_ge(*pool_s.at(j, "LO", *u))
                            for a in range(4):
                                at = 2 * HD * (4 * b + a) if kind == "QT" else 3 * HD * a + HD * b
                                last = nc.tensor.transpose(m[:, P * a:P * a + P], st[:, st_place[u], at:at + 2 * HD], ident[:, :])
                        elif kind == "S":
                            h, t = key[1:]
                            g = h // GRP
                            if h % HH == 0 and t == 0:
                                pe.wait_ge(*act_s.at(j, "C", "QT", h // HH, TT - 1, 1))
                                if h == 0:
                                    pe.wait_ge(*act_s.at(j, "C", "KT", TT - 1, 1))
                            who, step = (act_s, "X") if softmax else (dve_s, "M")
                            pe.wait_ge(*(who.at(j, step, h - 1, t) if h else who.at(shift(j, -1), step, HEADS - 1, t)))
                            for n in range(2):
                                if softmax:
                                    last = nc.tensor.matmul(ps_s[:, t, :], qs[:, h, P * t:P * t + P], ks[:, n, g, :], start=(n == 0), stop=(n == 1))
                                else:
                                    last = nc.tensor.matmul(ps_s[:, t, P * t:SEQ], ks[:, n, g, P * t:P * t + P], qs[:, h, P * t:SEQ], start=(n == 0), stop=(n == 1))
                        elif kind == "P":
                            h, c = key[1:]
                            if c == 0:
                                pe.wait_ge(*act_s.at(j, "X", h, 3))
                            ph, pc, seq = (h, c - 2, j) if c >= 2 else (h - 1, c + 2, j) if h else (HEADS - 1, c + 2, shift(j, -1))
                            pe.wait_ge(*(dve_s if pc % 2 == 0 else act_s).at(seq, "E", ph, pc))
                            for t in range(TT):
                                last = nc.tensor.transpose(ps_p[:, c % 2, P * t:P * t + P], probs[:, h % 2, t, P * c:P * c + P], ident[:, :])
                        elif kind == "R":
                            p = key[1]
                            pe.wait_ge(*dve_s.at(j, "I", 2 * p + 1))
                            for t in range(TT):
                                for s in range(2):
                                    last = nc.tensor.matmul(m[HD * s:HD * s + HD, P * t:P * t + P], ri[:, t, 2 * p + s:2 * p + s + 1].broadcast_to([P, HD]),
                                                            ident[:, :], start=True, stop=True)
                        elif kind == "A":
                            p, c = key[1:]
                            g = 2 * p // GRP
                            if c == 0:
                                pe.wait_ge(*dve_s.at(j, "VV"))
                            if softmax:
                                pe.wait_ge(*(act_s if c % 2 else dve_s).at(j, "E", 2 * p + 1, c))
                            else:
                                pe.wait_ge(*dve_s.at(j, "M", 2 * p + 1, c))
                            for s in range(2):
                                last = nc.tensor.matmul(m[HD * s:HD * s + HD, first_q[c]:SEQ], v[:, 1, c, HD * g:HD * g + HD],
                                                        weights_of(2 * p + s, c), start=(c == 0), stop=(c == TT - 1))
                        elif kind == "W":
                            tok = slice(P * key[1], P * key[1] + P)
                            split = (lambda p: pool_s.at(j, "OL", p)) if softmax else (lambda p: dve_s.at(j, "O", p))
                            pe.wait_ge(weights_split, 3)
                            pe.wait_ge(*split(PAIRS - 2))
                            last_pair = (lambda: pe.wait_ge(*split(PAIRS - 1))) if key[1] == 0 else None
                            last = sum_of_parts(nc, m[:, 0:D], lambda k: ath[:, k, tok], lambda k: atl[:, k, tok],
                                                lambda k: woh[:, k, :], lambda k: wol[:, k, :], PAIRS, last_pair)
                        last.then_inc(pe_s.sem(key), 1)

                turns(pe, steps, ahead["tensor"], pe_o)

            @block.vector
            def _(dve):
                dve_s.start(dve)

                def split_weights(n):
                    raw, hi, lo = raw_and_parts()[n]
                    if n == 1 and softmax:
                        dve.wait_ge(weights_in[1], 16)
                        keys = raw.rearrange("p (k n) -> p k n", k=KD)[:, :, 0:KVW]
                        nc.vector.tensor_scalar(keys, keys, HD ** -0.5, None, ALU.mult).then_inc(keys_scaled, 1)
                    dve.wait_ge(hi_split, n + 1)
                    nc.vector.tensor_tensor(flat(lo), raw, flat(hi).bitcast(F32), ALU.subtract).then_inc(weights_split, 1)

                split_weights(0)
                split_weights(1)
                vv = nc.vector

                def steps(i, run):
                    rot = [k for k in run if k[0] == "ROT"]
                    for key in run:
                        kind, j = key[0], own(i, key)
                        if kind == "XH":
                            k = key[1]
                            dve.wait_ge(*pe_s.at(j, "T", k))
                            if k == 0:
                                dve.wait_ge(*pe_s.at(shift(j, -1), "Q", 1, TT - 1))
                                dve.wait_ge(*pe_s.at(shift(j, -1), "KV", TT - 1))
                            op = vv.tensor_copy(xth[:, k, :], ps_m[:, bank["T", k], :])
                        elif kind == "XL":
                            k = key[1]
                            dve.wait_ge(*dve_s.at(j, "XH", k))
                            op = vv.tensor_tensor(xtl[:, k, :], ps_m[:, bank["T", k], :], xth[:, k, :].bitcast(F32), ALU.subtract)
                        elif kind == "XB":
                            dve.wait_ge(x_loaded, 16 * j[0] + 16 * j[1] + 16)
                            dve.wait_ge(*dve_s.at(shift(j, -1), "F", TT - 1))
                            if softmax:
                                dve.wait_ge(bias_in, 16)
                                op = vv.tensor_tensor(xb[:, :, :], xc[:, :, :], bias[:, :].unsqueeze(1).broadcast_to([P, TT, D]), ALU.add)
                            else:
                                op = vv.tensor_copy(xb[:, :, :], xc[:, :, :])
                        elif kind == "ROT":
                            u, t = key[1:], key[-1]
                            heads = HH if u[0] == "Q" else KVH
                            dve.wait_ge(*pe_s.at(j, *u))
                            dve.wait_ge(rope_in, 16)
                            for seq, k in last_use(i, rot, key, rt_place, ahead["vector"], dve_o):
                                dve.wait_ge(*pool_s.at(seq, "LO", *k[1:]))
                            w = heads * HD
                            op = vv.tensor_tensor(rt[:, :, 0:w].rearrange("p u (h d) -> p u h d", d=HD),
                                                  ps_m[:, bank[u], 0:w].rearrange("p (h d) -> p h d", d=HD).unsqueeze(1).broadcast_to([P, 2, heads, HD]),
                                                  rope[:, t, :, :].unsqueeze(2).broadcast_to([P, 2, heads, HD]), ALU.mult)
                        elif kind == "VC":
                            t = key[1]
                            dve.wait_ge(*pe_s.at(j, "KV", t))
                            dve.wait_ge(*dve_s.at(shift(j, -1), "VV"))
                            op = vv.tensor_copy(v[:, 0, t, :], ps_m[:, bank["KV", t], KVW:2 * KVW])
                        elif kind == "VV":
                            dve.wait_ge(*pe_s.at(shift(j, -1), "A", PAIRS - 1, TT - 1))
                            dve.wait_ge(*dve_s.at(j, "VC", TT - 1))
                            op = vv.tensor_copy(v[:, 1, :, :], v[:, 0, :, :])
                        elif kind == "M":
                            h, t = key[1:]
                            dve.wait_ge(*pe_s.at(j, "S", h, t))
                            if softmax:
                                if t == 0:
                                    dve.wait_ge(*act_s.at(shift(j, -1), "X", h, TT - 1))
                                op = vv.tensor_reduce(out=mx[:, h, t:t + 1], in_=ps_s[:, t, :], axis=AX.X, op=ALU.max, negate=True)
                            else:
                                if h in (0, HEADS - LATE) and t == 0:
                                    dve.wait_ge(late_decay_in if h else decay_in, 16)
                                if t == 0:
                                    offset, p = pairs_before(h)
                                    dve.wait_ge(*pe_s.at(shift(j, offset), "A", p, TT - 1))
                                op = vv.tensor_tensor(weights_of(h, t), ps_s[:, t, P * t:SEQ], dec[:, h, 0:SEQ - P * t], ALU.mult)
                        elif kind == "I":
                            h = key[1]
                            dve.wait_ge(*act_s.at(j, "X", h, TT - 1))
                            if h == 0:
                                dve.wait_ge(*pe_s.at(shift(j, -1), "R", PAIRS - 1))
                            op = vv.reciprocal(ri[:, :, h], rs[:, h, :])
                        elif kind == "E":
                            h, c = key[1:]
                            dve.wait_ge(*pe_s.at(j, "P", h, c))
                            if c == 0:
                                offset, p = pairs_before(h)
                                dve.wait_ge(*pe_s.at(shift(j, offset), "A", p, TT - 1))
                            op = vv.tensor_copy(weights_of(h, c), ps_p[:, c % 2, :])
                        elif kind == "O":
                            p = key[1]
                            dve.wait_ge(*pe_s.at(j, "A", p, TT - 1))
                            dve.wait_ge(*act_s.at(j, "RC", p))
                            if not softmax:
                                op = vv.tensor_tensor(atl[:, p, :], ps_m[:, bank["A", p], :], ath[:, p, :].bitcast(F32), ALU.subtract)
                                op.then_inc(dve_s.sem(key), 1)
                                continue
                            dve.wait_ge(*(pool_s.at(j, "OL", p - 1) if p else pool_s.at(shift(j, -1), "OL", PAIRS - 1)))
                            op = vv.tensor_tensor(ot[:, :], ps_m[:, bank["A", p], :], rrep[:, :], ALU.mult)
                        elif kind == "F":
                            t = key[1]
                            dve.wait_ge(*pe_s.at(j, "W", t))
                            if t == 0:
                                dve.wait_ge(*dve_s.at(j, "XB"))
                            dve.wait_ge(stored[t % 2], 32 * j[0] + (32 * j[1] + 16 * (t // 2) + 32))
                            op = vv.tensor_tensor(r[:, t % 2, :], ps_m[:, bank["W", t], 0:D], xb[:, t, :], ALU.add)
                        elif kind == "B":
                            t = key[1]
                            dve.wait_ge(*dve_s.at(j, "F", t))
                            op = vv.bn_stats(st6[:, t % 2, :], r[:, t % 2, :])
                        elif kind == "G":
                            t = key[1]
                            hold(dve, *dve_s.at(j, "B", t))
                            op = vv.bn_aggr(mv[:, t % 2, :], st6[:, t % 2, :])
                        elif kind == "N":
                            t = key[1]
                            dve.wait_ge(*pool_s.at(j, "RSTD", t))
                            op = vv.tensor_scalar(r[:, t % 2, :], r[:, t % 2, :], mv[:, t % 2, 0:1], rstd[:, t % 2, :], ALU.subtract, ALU.mult)
                        op.then_inc(dve_s.sem(key), 1)

                turns(dve, steps, ahead["vector"], dve_o, lambda: split_weights(2))

            @block.scalar
            def _(act):
                act_s.start(act)

                def hi_weights(n):
                    act.wait_ge(weights_in[n], 16)
                    if n == 1 and softmax:
                        act.wait_ge(keys_scaled, 1)
                    raw, hi, _ = raw_and_parts()[n]
                    nc.scalar.copy(flat(hi), raw).then_inc(hi_split, 1)

                hi_weights(0)
                hi_weights(1)

                def steps(i, run):
                    for key in run:
                        kind, j = key[0], own(i, key)
                        if kind == "C":
                            k = key[1:]
                            t, b = k[-2:]
                            act.wait_ge(*pe_s.at(j, *k))
                            src = ps_m[:, bank[k], :].rearrange("p (a s) -> p a s", s=P)
                            if k[0] == "QT":
                                half = k[1]
                                if t == 0 and b == 0:
                                    act.wait_ge(*pe_s.at(shift(j, -1), "S", HH * half + HH - 1, 3))
                                op = nc.scalar.copy(qs[:, HH * half + 4 * b:HH * half + 4 * b + 4, P * t:P * t + P], src)
                            else:
                                if t == 0 and b == 0:
                                    act.wait_ge(*pe_s.at(shift(j, -1), "S", HEADS - 1, 3))
                                op = nc.scalar.copy(ks[:, b, :, P * t:P * t + P], src)
                        elif kind == "HI":
                            op = make_hi(act, nc.scalar.copy, i, run, key)
                        elif kind == "X":
                            h, t = key[1:]
                            act.wait_ge(*dve_s.at(j, "M", h, t))
                            if t == 0:
                                act.wait_ge(*(pe_s.at(j, "P", h - 2, TT - 1) if h >= 2 else pe_s.at(shift(j, -1), "P", h + HEADS - 2, TT - 1)))
                                act.wait_ge(*dve_s.at(shift(j, -1), "I", h))
                            op = nc.scalar.activation(probs[:, h % 2, t, :], ps_s[:, t, :], ACT.Exp, bias=mx[:, h, t:t + 1], scale=1.0,
                                                      accum_out=rs[:, h, t:t + 1])
                        elif kind == "E":
                            h, c = key[1:]
                            act.wait_ge(*pe_s.at(j, "P", h, c))
                            offset, p = pairs_before(h)
                            act.wait_ge(*pe_s.at(shift(j, offset), "A", p, TT - 1))
                            op = nc.scalar.copy(weights_of(h, c), ps_p[:, c % 2, :])
                        elif kind == "RC":
                            p = key[1]
                            if softmax:
                                act.wait_ge(*pe_s.at(j, "R", p))
                                act.wait_ge(*(dve_s.at(j, "O", p - 1) if p else dve_s.at(shift(j, -1), "O", PAIRS - 1)))
                                op = nc.scalar.copy(rrep[:, :], ps_m[:, bank["R", p], :])
                            else:
                                act.wait_ge(*pe_s.at(j, "A", p, TT - 1))
                                act.wait_ge(*pe_s.at(shift(j, -1), "W", TT - 1))
                                op = nc.scalar.copy(ath[:, p, :], ps_m[:, bank["A", p], :])
                        op.then_inc(act_s.sem(key), 1)

                turns(act, steps, ahead["scalar"], act_o, lambda: hi_weights(2))

            @block.gpsimd
            def _(pool):
                pool_s.start(pool)

                def steps(i, run):
                    for key in run:
                        kind, j = key[0], own(i, key)
                        u = key[1:]
                        if kind in ("Y0", "Y1", "HI", "LO"):
                            heads, rows, stack = rows_of(u)
                            half = lambda n, c: rt[:, n, 0:heads * HD].rearrange("p (h c d) -> p h c d", c=2, d=HALF)[:, :, c, :]
                        if kind in ("Y0", "Y1"):
                            c = int(kind[1])
                            hold(pool, *dve_s.at(j, "ROT", *u))
                            op = nc.gpsimd.tensor_tensor(half(0, c), half(0, c), half(1, 1 - c), ALU.add)
                        elif kind == "HI":
                            op = make_hi(pool, nc.gpsimd.tensor_copy, i, run, key)
                        elif kind == "LO":
                            hold(pool, *hi_s.at(j, "HI", *u))
                            op = nc.gpsimd.tensor_tensor(stack[:, :, HD:2 * HD].bitcast(F32R), rows, stack[:, :, 0:HD], ALU.subtract)
                        elif kind == "OH":
                            p = key[1]
                            hold(pool, *(dve_s.at(j, "O", p) if softmax else act_s.at(j, "RC", p)))
                            if p == 0:
                                hold(pool, *pe_s.at(shift(j, -1), "W", TT - 1))
                            op = nc.gpsimd.tensor_copy(ath[:, p, :], ot[:, :])
                        elif kind == "OL":
                            p = key[1]
                            hold(pool, *pool_s.at(j, "OH", p))
                            op = nc.gpsimd.tensor_tensor(atl[:, p, :], ot[:, :], ath[:, p, :].bitcast(F32), ALU.subtract)
                        elif kind == "EPS":
                            t = key[1]
                            hold(pool, *dve_s.at(j, "G", t))
                            op = nc.gpsimd.tensor_scalar(vare[:, t % 2, :], mv[:, t % 2, 1:2], EPS, None, ALU.add)
                        elif kind == "RSTD":
                            t = key[1]
                            hold(pool, *pool_s.at(j, "EPS", t))
                            hold(pool, *(dve_s.at(j, "N", t - 2) if t >= 2 else dve_s.at(shift(j, -1), "N", t + 2)))
                            op = nc.gpsimd.tensor_tensor(rstd[:, t % 2, :], vare[:, t % 2, :], const["minus_half"][:, :], ALU.pow)
                        op.then_inc(pool_s.sem(key), 1)

                turns(pool, steps, ahead["gpsimd"], pool_o)


def quantized_ffn(nc, const, x_in, x_out, gamma_beta, q1, s1, b1, q2, s2, b2, name):
    F = q1.shape[1]
    FT = F // P
    ctx = ExitStack()
    with ctx:
        sb = lambda n, s, dt=F32: ctx.enter_context(nc.sbuf_tensor(f"{name}_{n}", s, dt))
        sem = lambda n: ctx.enter_context(nc.semaphore(f"{name}_{n}"))
        ident = const["ident"]
        qi1, qi2 = sb("qi1", [P, KD, F], I32), sb("qi2", [P, FT, D], I32)
        sc1, sc2 = sb("sc1", [P, KD, F]), sb("sc2", [P, FT, D])
        w1h, w1l = (sb(n, [P, KD, F], F32R) for n in ("w1h", "w1l"))
        w2h, w2l = (sb(n, [P, FT, D], F32R) for n in ("w2h", "w2l"))
        gb = sb("gb", [P, 2, KD])
        b1c = sb("b1c", [P, FT])
        b2r = sb("b2r", [P, D])
        xc = sb("xc", [P, TT, D])
        xb = sb("xb", [P, TT, D])
        xn = sb("xn", [P, TT, D])
        ht = sb("ht", [P, KD, SEQ])
        hth, htl = (sb(n, [P, KD, SEQ], F32R) for n in ("hth", "htl"))
        s = sb("s", [P, 2, SEQ])
        sh, sl = (sb(n, [P, FT, SEQ], F32R) for n in ("sh", "sl"))
        r = sb("r", [P, 2, D])
        st6, st6x = sb("st6", [P, 2, 6]), sb("st6x", [P, TT, 6])
        mv, mvx = sb("mv", [P, 2, 2]), sb("mvx", [P, TT, 2])
        vare, varex = sb("vare", [P, 2, 1]), sb("varex", [P, TT, 1])
        rstd, rstdx = sb("rstd", [P, 2, 1]), sb("rstdx", [P, TT, 1])
        outt = sb("outt", [P, 2, D])
        ps = ctx.enter_context(nc.psum_tensor(f"{name}_ps", [P, 8, SEQ], F32))
        first_in, second_in, bias_in = sem("first_in"), sem("second_in"), sem("bias_in")
        scaled, hi_split, first_split, second_split, bias_halved = (sem(n) for n in ("scaled", "hi_split", "first_split", "second_split", "bias_halved"))
        x_loaded = sem("x_loaded")
        stored = [sem(f"stored{k}") for k in range(2)]
        hold = gated_hold(sem("held"))

        pe_o = [("H", m) for m in range(FT)] + [("W", 0), ("W", 1)] + [("T", k) for k in range(KD)] + [("W", t) for t in range(2, TT)]
        dve_o, act_o = [], [("S", m) for m in range(FT)]
        pool_o = [("EPSX",), ("RSTDX",)] + [(n, t) for t in range(TT) for n in ("EPS", "RSTD")]
        for m in range(FT):
            dve_o += [("SH", m), ("SL", m)]
            if 3 <= m < 3 + TT:
                dve_o += [("BX", m - 3), ("GX", m - 3)]
            if m == 7:
                dve_o += [("NX", t) for t in range(TT)]
        for t in range(TT + 1):
            if t < TT:
                dve_o += [("F", t), ("B", t), ("G", t)]
            if t == TT - 1:
                dve_o.append(("XB",))
            if 1 <= t < 1 + KD:
                dve_o += [("HT", t - 1), ("XH", t - 1), ("XL", t - 1)]
            if t >= 1: dve_o.append(("N", t - 1))
        is_ahead = lambda k: k[0] in ("T", "XB", "BX", "GX", "NX", "HT", "XH", "XL", "EPSX", "RSTDX")
        S, ahead = {}, {}
        for eng_name, o in (("tensor", pe_o), ("vector", dve_o), ("scalar", act_o), ("gpsimd", pool_o)):
            ahead[eng_name] = [k for k in o if is_ahead(k)]
            S[eng_name] = Steps(sem(f"{eng_name}_ahead"), sem(f"{eng_name}_main"), ahead[eng_name], [k for k in o if not is_ahead(k)])
        pe_s, dve_s, act_s, pool_s = (S[n] for n in ("tensor", "vector", "scalar", "gpsimd"))
        own = lambda i, key: (i[0], i[1] + 1) if is_ahead(key) else i
        BANKS = 7
        bank = {k: n % BANKS for n, k in enumerate(pe_o)}
        emptied = {"T": (dve_s, "HT"), "H": (act_s, "S"), "W": (dve_s, "F")}

        with nc.Block() as block:

            @block.sync
            def _(sp):
                for k in range(2):
                    sp.sem_inc(stored[k], 32)

                def load(i, index):
                    hold(sp, *dve_s.at(shift(i, -1), "XB"))
                    sp.dma_start(xc[:, :, :], x_in[bass.ds(index, 1), :, :].rearrange("o (t p) d -> p (o t) d", p=P)).then_inc(x_loaded, 16)

                def store(i, index):
                    for t in range(TT):
                        hold(sp, *dve_s.at(i, "N", t))
                        sp.dma_start(x_out[bass.ds(index, 1), P * t:P * t + P, :].rearrange("o p d -> p (o d)"), outt[:, t % 2, :]).then_inc(stored[t % 2], 16)

                sp.dma_start(qi1[:, :, :], q1.rearrange("(k p) n -> p k n", p=P)).then_inc(first_in, 16)
                sp.dma_start(sc1[:, :, :].rearrange("p k n -> p (k n)"), s1.rearrange("k n -> (k n)").partition_broadcast(P)).then_inc(first_in, 16)
                load((0, 0), 0)
                sp.dma_start(gb[:, :, :], gamma_beta).then_inc(bias_in, 16)
                sp.dma_start(b1c[:, :], b1).then_inc(bias_in, 16)
                sp.dma_start(b2r[:, :], b2.partition_broadcast(P)).then_inc(bias_in, 16)
                sp.dma_start(qi2[:, :, :], q2.rearrange("(k p) n -> p k n", p=P)).then_inc(second_in, 16)
                sp.dma_start(sc2[:, :, :].rearrange("p k n -> p (k n)"), s2.rearrange("k n -> (k n)").partition_broadcast(P)).then_inc(second_in, 16)
                with sp.Fori(0, BATCH - 1) as i:
                    load((i, 1), i + 1)
                    store((i, 0), i)
                store((BATCH - 1, 0), BATCH - 1)
                for k in range(2):
                    hold(sp, stored[k], 32 * BATCH + 32)

            @block.tensor
            def _(pe):
                pe_s.start(pe)

                def steps(i, run):
                    for key in run:
                        kind, j = key[0], own(i, key)
                        m = ps[:, bank[key], :]
                        for seq, k in last_use(i, run, key, bank, ahead["tensor"], pe_o):
                            who, step = emptied[k[0]]
                            pe.wait_ge(*who.at(seq, step, *k[1:]))
                        if kind == "T":
                            k = key[1]
                            pe.wait_ge(*dve_s.at(j, "NX", TT - 1))
                            for t in range(TT):
                                last = nc.tensor.transpose(m[:, P * t:P * t + P], xn[:, t, P * k:P * k + P], ident[:, :])
                        elif kind == "H":
                            cols = slice(P * key[1], P * key[1] + P)
                            if key[1] == 0:
                                pe.wait_ge(first_split, 1)
                                pe.wait_ge(*dve_s.at(j, "XL", KD - 1))
                            last = sum_of_parts(nc, m, lambda k: w1h[:, k, cols], lambda k: w1l[:, k, cols],
                                                lambda k: hth[:, k, :], lambda k: htl[:, k, :], KD)
                        elif kind == "W":
                            t = key[1]
                            tok = slice(P * t, P * t + P)
                            if t == 0:
                                pe.wait_ge(second_split, 1)
                                pe.wait_ge(*dve_s.at(j, "SL", FT - 2))
                            last_part = (lambda: pe.wait_ge(*dve_s.at(j, "SL", FT - 1))) if t == 0 else None
                            last = sum_of_parts(nc, m[:, 0:D], lambda k: sh[:, k, tok], lambda k: sl[:, k, tok],
                                                lambda k: w2h[:, k, :], lambda k: w2l[:, k, :], FT, last_part)
                        last.then_inc(pe_s.sem(key), 1)

                turns(pe, steps, ahead["tensor"], pe_o)

            flat = lambda x: x[:, :, :].rearrange("p k n -> p (k n)")

            @block.vector
            def _(dve):
                dve_s.start(dve)
                dve.wait_ge(first_in, 32)
                nc.vector.scalar_tensor_tensor(out=flat(sc1), in0=flat(qi1), scalar=-128.0, in1=flat(sc1), op0=ALU.add, op1=ALU.mult).then_inc(scaled, 1)
                dve.wait_ge(bias_in, 48)
                nc.vector.tensor_scalar(b2r[:, :], b2r[:, :], 0.5, None, ALU.mult).then_inc(bias_halved, 1)
                dve.wait_ge(hi_split, 1)
                nc.vector.tensor_tensor(flat(w1l), flat(sc1), flat(w1h).bitcast(F32), ALU.subtract).then_inc(first_split, 1)
                dve.wait_ge(second_in, 32)
                nc.vector.scalar_tensor_tensor(out=flat(sc2), in0=flat(qi2), scalar=-128.0, in1=flat(sc2), op0=ALU.add, op1=ALU.mult).then_inc(scaled, 1)

                def steps(i, run):
                    for key in run:
                        kind, j = key[0], own(i, key)
                        t = k = m = key[1] if len(key) > 1 else 0
                        if kind == "BX":
                            dve.wait_ge(x_loaded, 16 * j[0] + (16 * j[1] + 16))
                            op = nc.vector.bn_stats(st6x[:, t, :], xc[:, t, :])
                        elif kind == "GX":
                            hold(dve, *dve_s.at(j, "BX", t))
                            op = nc.vector.bn_aggr(mvx[:, t, :], st6x[:, t, :])
                        elif kind == "NX":
                            if t == 0:
                                dve.wait_ge(*pool_s.at(j, "RSTDX"))
                                dve.wait_ge(*pe_s.at(shift(j, -1), "T", KD - 1))
                            op = nc.vector.tensor_scalar(xn[:, t, :], xc[:, t, :], mvx[:, t, 0:1], rstdx[:, t, :], ALU.subtract, ALU.mult)
                        elif kind == "XB":
                            dve.wait_ge(bias_halved, 1)
                            dve.wait_ge(*dve_s.at(shift(j, -1), "F", TT - 1))
                            op = nc.vector.scalar_tensor_tensor(out=xb[:, :, :], in0=xc[:, :, :], scalar=2.0,
                                                                in1=b2r[:, :].unsqueeze(1).broadcast_to([P, TT, D]), op0=ALU.mult, op1=ALU.add)
                        elif kind == "HT":
                            dve.wait_ge(*pe_s.at(j, "T", k))
                            dve.wait_ge(*dve_s.at(shift(j, -1), "XL", k))
                            op = nc.vector.tensor_scalar(ht[:, k, :], ps[:, bank["T", k], :], gb[:, 0, k:k + 1], gb[:, 1, k:k + 1], ALU.mult, ALU.add)
                        elif kind == "XH":
                            dve.wait_ge(*dve_s.at(j, "HT", k))
                            if k == 0:
                                dve.wait_ge(*pe_s.at(shift(j, -1), "H", FT - 1))
                            op = nc.vector.tensor_copy(hth[:, k, :], ht[:, k, :])
                        elif kind == "XL":
                            dve.wait_ge(*dve_s.at(j, "XH", k))
                            op = nc.vector.tensor_tensor(htl[:, k, :], ht[:, k, :], hth[:, k, :].bitcast(F32), ALU.subtract)
                        elif kind == "SH":
                            dve.wait_ge(*act_s.at(j, "S", m))
                            if m == 0:
                                dve.wait_ge(*pe_s.at(shift(j, -1), "W", TT - 1))
                            op = nc.vector.tensor_copy(sh[:, m, :], s[:, m % 2, :])
                        elif kind == "SL":
                            dve.wait_ge(*dve_s.at(j, "SH", m))
                            op = nc.vector.tensor_tensor(sl[:, m, :], s[:, m % 2, :], sh[:, m, :].bitcast(F32), ALU.subtract)
                        elif kind == "F":
                            dve.wait_ge(*pe_s.at(j, "W", t))
                            if t == 0:
                                dve.wait_ge(*dve_s.at(j, "XB"))
                            dve.wait_ge(*(dve_s.at(j, "N", t - 2) if t >= 2 else dve_s.at(shift(j, -1), "N", t + 2)))
                            op = nc.vector.scalar_tensor_tensor(out=r[:, t % 2, :], in0=ps[:, bank["W", t], 0:D], scalar=0.5, in1=xb[:, t, :], op0=ALU.mult, op1=ALU.add)
                        elif kind == "B":
                            dve.wait_ge(*dve_s.at(j, "F", t))
                            op = nc.vector.bn_stats(st6[:, t % 2, :], r[:, t % 2, :])
                        elif kind == "G":
                            hold(dve, *dve_s.at(j, "B", t))
                            op = nc.vector.bn_aggr(mv[:, t % 2, :], st6[:, t % 2, :])
                        elif kind == "N":
                            dve.wait_ge(*pool_s.at(j, "RSTD", t))
                            dve.wait_ge(stored[t % 2], 32 * j[0] + (32 * j[1] + 16 * (t // 2) + 32))
                            op = nc.vector.tensor_scalar(outt[:, t % 2, :], r[:, t % 2, :], mv[:, t % 2, 0:1], rstd[:, t % 2, :], ALU.subtract, ALU.mult)
                        op.then_inc(dve_s.sem(key), 1)

                turns(dve, steps, ahead["vector"], dve_o)

            @block.scalar
            def _(act):
                act_s.start(act)
                for n, (raw, hi) in enumerate(((sc1, w1h), (sc2, w2h))):
                    act.wait_ge(scaled, n + 1)
                    nc.scalar.copy(flat(hi), flat(raw)).then_inc(hi_split, 1)
                act.wait_ge(bias_in, 48)

                def steps(i, run):
                    for key in run:
                        j, m = own(i, key), key[1]
                        act.wait_ge(*pe_s.at(j, "H", m))
                        act.wait_ge(*(dve_s.at(j, "SL", m - 2) if m >= 2 else dve_s.at(shift(j, -1), "SL", m + FT - 2)))
                        op = nc.scalar.activation(s[:, m % 2, :], ps[:, bank["H", m], :], ACT.Silu, bias=b1c[:, m:m + 1], scale=1.0)
                        op.then_inc(act_s.sem(key), 1)

                turns(act, steps, ahead["scalar"], act_o)

            @block.gpsimd
            def _(pool):
                pool_s.start(pool)

                def steps(i, run):
                    for key in run:
                        kind, j = key[0], own(i, key)
                        if kind == "EPSX":
                            hold(pool, *dve_s.at(j, "GX", TT - 1))
                            op = nc.gpsimd.tensor_scalar(varex[:, :, :], mvx[:, :, 1:2], EPS, None, ALU.add)
                        elif kind == "RSTDX":
                            hold(pool, *pool_s.at(j, "EPSX"))
                            hold(pool, *dve_s.at(shift(j, -1), "NX", TT - 1))
                            op = nc.gpsimd.tensor_tensor(rstdx[:, :, :], varex[:, :, :], const["minus_half"][:, :].unsqueeze(1).broadcast_to([P, TT, 1]), ALU.pow)
                        elif kind == "EPS":
                            t = key[1]
                            hold(pool, *dve_s.at(j, "G", t))
                            op = nc.gpsimd.tensor_scalar(vare[:, t % 2, :], mv[:, t % 2, 1:2], EPS, None, ALU.add)
                        elif kind == "RSTD":
                            t = key[1]
                            hold(pool, *pool_s.at(j, "EPS", t))
                            hold(pool, *(dve_s.at(j, "N", t - 2) if t >= 2 else dve_s.at(shift(j, -1), "N", t + 2)))
                            op = nc.gpsimd.tensor_tensor(rstd[:, t % 2, :], vare[:, t % 2, :], const["minus_half"][:, :], ALU.pow)
                        op.then_inc(pool_s.sem(key), 1)

                steps(FIRST, ahead["gpsimd"])
                hold(pool, hi_split, 2)
                nc.gpsimd.tensor_tensor(flat(w2l), flat(sc2), flat(w2h).bitcast(F32), ALU.subtract).then_inc(second_split, 1)
                with pool.Fori(0, BATCH - 1) as i:
                    steps((i, 0), pool_o)
                steps((BATCH - 1, 0), [k for k in pool_o if not is_ahead(k)])



MH, KPH, VAR = 16, 8, 4
MAX_ROW = (VAR - 1) * KPH
QUADS = MH // 4
E_ = 8


def latent_attention(nc, const, x_in, m_out, comb_out, w, name):
    ctx = ExitStack()
    with ctx:
        sb = lambda n, s, dt=F32: ctx.enter_context(nc.sbuf_tensor(f"{name}_{n}", s, dt))
        sem = lambda n: ctx.enter_context(nc.semaphore(f"{name}_{n}"))
        ident = const["ident"]
        LAT = MH * KPH
        raw_y = sb("raw_y", [P, KD, 2 * 4 * LAT])
        raw_v = sb("raw_v", [P, KD, LAT])
        raw_r = sb("raw_r", [P, KD, E_])
        raw_o = sb("raw_o", [P, 1, D])
        wyh, wyl = (sb(n, [P, KD, 2 * 4 * LAT], F32R) for n in ("wyh", "wyl"))
        wvh, wvl = (sb(n, [P, KD, LAT], F32R) for n in ("wvh", "wvl"))
        wrh, wrl = (sb(n, [P, KD, E_], F32R) for n in ("wrh", "wrl"))
        woh, wol = (sb(n, [P, 1, D], F32R) for n in ("woh", "wol"))
        yb = sb("yb", [P, 2 * QUADS])
        minus_lo = sb("minus_lo", [P, 2])
        vb, orow, rrow = sb("vb", [P, LAT]), sb("orow", [P, D]), sb("rrow", [P, E_])
        ocol = sb("ocol", [P, KD])
        rev = sb("rev", [P, E_])
        xc = sb("xc", [P, TT, D])
        xth, xtl = (sb(n, [P, KD, SEQ], F32R) for n in ("xth", "xtl"))
        y = sb("y", [P, 2, SEQ])
        yh = sb("yh", [P, 2, SEQ], F32R)
        stack = sb("stack", [P, 2 * QUADS, SEQ], F32R)
        vn = sb("vn", [P, TT, LAT])
        v = sb("v", [P, TT, MH, 32])
        ri = sb("ri", [P, TT, MH])
        mx = sb("mx", [P, QUADS, TT, 4])
        mrow = sb("mrow", [P, QUADS, TT, P])
        pt = sb("pt", [P, 2, TT, 4, SEQ])
        ot = sb("ot", [P, QUADS, SEQ])
        ao = sb("ao", [P, TT, LAT])
        ch, cl = (sb(n, [P, SEQ], F32R) for n in ("ch", "cl"))
        mt = sb("mt", [P, KD, SEQ])
        mth, mtl = (sb(n, [P, KD, SEQ], F32R) for n in ("mth", "mtl"))
        mo = sb("mo", [P, 2, D])
        small = lambda n: sb(n, [P, TT, E_])
        lg, ex, pr, eq, key_, oh1, p2, oh2, oh, wt, comb = (small(n) for n in ("lg", "ex", "pr", "eq", "key", "oh1", "p2", "oh2", "oh", "wt", "comb"))
        one = lambda n: sb(n, [P, TT, 1])
        lm, es, er, v1, k1, v2, k2, tw, tr = (one(n) for n in ("lm", "es", "er", "v1", "k1", "v2", "k2", "tw", "tr"))
        ps_s, ps_t, ps_a = (ctx.enter_context(nc.psum_tensor(f"{name}_{n}", [P, 2, SEQ], F32)) for n in ("ps_s", "ps_t", "ps_a"))
        ps_m = ctx.enter_context(nc.psum_tensor(f"{name}_ps_m", [P, 2, SEQ], F32))
        weights_in, small_in, hi_split, weights_split, zeroed = [sem(f"weights_in{n}") for n in range(4)], sem("small_in"), sem("hi_split"), sem("weights_split"), sem("zeroed")
        x_loaded, comb_stored = sem("x_loaded"), sem("comb_stored")
        stored = [sem(f"stored{k}") for k in range(2)]
        hold = gated_hold(sem("held"))

        pe_o, dve_o, act_o, pool_o = [], [], [], []
        units = [n for a in range(QUADS) for n in (a, QUADS + a)]

        ROT, LEAD = 2, 5
        ROUTE = ["LG", "LM", "LD"]
        ROUTE2 = ["ES", "ER", "PR", "V1", "EQ1", "KY1", "K1", "OH1", "P2", "V2", "EQ2", "KY2", "K2", "OH2", "OH", "TW", "TR", "WT", "COMB"]
        gaps = {}

        def put(gap, order, *keys):
            gaps.setdefault(gap, []).extend((order, k) for k in keys)

        for k in range(KD):
            put(k, pe_o, ("T", k)); put(k + 1, dve_o, ("XH", k), ("XL", k))
        for a, gap in enumerate((4, 17, 24, 32)):
            for n, g in ((a, gap), (QUADS + a, gap + 2)):
                put(g, pe_o, ("Y", n)); put(g + 2, act_o, ("YB", n)); put(g + 2, pool_o, ("YH", n)); put(g + 5, dve_o, ("YS", n))
        for t in range(TT):
            put(9 + t, pe_o, ("V", t)); put(10 + t, dve_o, ("VB", t))
            put(36 + 2 * t, pe_o, ("BT", t)); put(37 + 2 * t, dve_o, ("RI", t), ("AO", t))
            put(50 + t, pe_o, ("MO", t)); put(51 + t, dve_o, ("MO", t))
        put(35, dve_o, ("VV",))
        put(44, pe_o, ("CT",)); put(45, dve_o, ("CH",)); put(46, dve_o, ("CL",))
        for c in range(KD):
            put(47 + c, pe_o, ("MT", c)); put(48 + c, dve_o, ("MB", c)); put(50 + c, dve_o, ("MH", c), ("ML", c))
        put(54, pe_o, ("RL",))
        for n, k in enumerate(ROUTE + ROUTE2):
            put(55 + n * 3 // 8, dve_o, (k,))
        put(56, act_o, ("EX",))
        for u in range(4 * QUADS):
            a, j = (u // 4 + ROT) % QUADS, u % 4
            ma, mt_ = ((u + LEAD) // 4 + ROT) % QUADS, (u + LEAD) % 4
            for s in range(4):
                gap = 4 * u + s
                pe_o += [("S", ma, mt_, s), ("ST", a, j, s)]
                dve_o.append(("M", ma, mt_, s)); act_o.append(("X", a, j, s))
                if s == 1:
                    pa, pj = (a, j - 1) if j else ((a - 1) % QUADS, TT - 1)
                    pe_o.append(("A", pa, pj))
                    if pj == TT - 1: put(gap, act_o, ("OT", pa))
                if mt_ == TT - 1 and s == 3:
                    put(gap, dve_o, ("NH", ma), ("NL", ma)); put(gap + 1, pe_o, ("TM", ma)); put(gap + 2, dve_o, ("QM", ma))
                for order, k in gaps.get(gap, []):
                    order.append(k)
        is_ahead = lambda k: (k[0] in ("T", "XH", "XL", "Y", "YB", "YH", "YS", "V", "VB", "VV") or (k[0] in ("ST", "X") and k[1] < ROT)
                              or (k[0] == "A" and 4 * k[1] + k[2] < 4 * ROT - 1) or (k[0] == "OT" and k[1] < ROT - 1)
                              or (k[0] in ("S", "M") and 4 * k[1] + k[2] < LEAD + 4 * ROT)
                              or (k[0] in ("NH", "NL", "TM", "QM") and 4 * k[1] + 3 < LEAD + 4 * ROT))
        S, ahead = {}, {}
        for eng_name, o in (("tensor", pe_o), ("vector", dve_o), ("scalar", act_o), ("gpsimd", pool_o)):
            ahead[eng_name] = [k for k in o if is_ahead(k)]
            S[eng_name] = Steps(sem(f"{eng_name}_ahead"), sem(f"{eng_name}_main"), ahead[eng_name], [k for k in o if not is_ahead(k)])
        pe_s, dve_s, act_s, pool_s = (S[n] for n in ("tensor", "vector", "scalar", "gpsimd"))
        misc = [k for k in pe_o if k[0] not in ("S", "ST", "A")]
        bank = {k: n % 2 for n, k in enumerate(misc)}
        emptied = {"T": (dve_s, "XL"), "Y": (act_s, "YB"), "V": (dve_s, "VB"), "BT": (dve_s, "AO"), "CT": (dve_s, "CL"),
                   "MT": (dve_s, "MB"), "MO": (dve_s, "MO"), "RL": (dve_s, "LG"), "TM": (dve_s, "QM")}
        own = lambda i, key: (i[0], i[1] + 1) if is_ahead(key) else i

        def two_before(j, kind, a, t, s):
            n = (4 * a + t) * 4 + s - 2
            return (j if n >= 0 else shift(j, -1),) + (kind,) + (n % 64 // 16, n % 16 // 4, n % 4)

        with nc.Block() as block:

            @block.sync
            def _(sp):
                for k in range(2):
                    sp.sem_inc(stored[k], 32)
                sp.sem_inc(comb_stored, 16)
                weights = [(raw_y[:, :, :], w["stacks"].rearrange("(k p) n -> p k n", p=P)), (raw_v[:, :, :], w["v_w"].rearrange("(k p) n -> p k n", p=P)),
                           (raw_r[:, :, :], w["router_w"].rearrange("(k p) n -> p k n", p=P)), (raw_o[:, 0, :], w["o_w"][0:P, :])]
                small = [(yb[:, :], w["stack_b"]), (minus_lo[:, :], w["minus_lo"]), (vb[:, :], w["v_b"].partition_broadcast(P)),
                         (orow[:, :], w["o_b"].partition_broadcast(P)), (rrow[:, :], w["router_b"].partition_broadcast(P)),
                         (ocol[:, :], w["o_b_cols"]), (rev[:, :], w["rev"].partition_broadcast(P))]

                def load(i, index):
                    hold(sp, *pe_s.at(shift(i, -1), "T", KD - 1))
                    sp.dma_start(xc[:, :, :], x_in[bass.ds(index, 1), :, :].rearrange("o (t p) d -> p (o t) d", p=P)).then_inc(x_loaded, 16)

                def store(i, index):
                    for t in range(TT):
                        hold(sp, *dve_s.at(i, "MO", t))
                        sp.dma_start(m_out[bass.ds(index, 1), P * t:P * t + P, :].rearrange("o p d -> p (o d)"), mo[:, t % 2, :]).then_inc(stored[t % 2], 16)
                    hold(sp, *dve_s.at(i, "COMB"))
                    sp.dma_start(comb_out[bass.ds(index, 1), :, :].rearrange("o (t p) e -> p (o t) e", p=P), comb[:, :, :]).then_inc(comb_stored, 16)

                sp.dma_start(*weights[0]).then_inc(weights_in[0], 16)
                load((0, 0), 0)
                sp.dma_start(*weights[1]).then_inc(weights_in[1], 16)
                for dst, src in small:
                    sp.dma_start(dst, src).then_inc(small_in, 16)
                for n in (2, 3):
                    sp.dma_start(*weights[n]).then_inc(weights_in[n], 16)
                with sp.Fori(0, BATCH - 1) as i:
                    load((i, 1), i + 1)
                    store((i, 0), i)
                store((BATCH - 1, 0), BATCH - 1)
                for k in range(2):
                    hold(sp, stored[k], 32 * BATCH + 32)
                hold(sp, comb_stored, 16 * BATCH + 16)

            @block.tensor
            def _(pe):
                pe_s.start(pe)
                pe.wait_ge(zeroed, 3)

                def steps(i, run):
                    in_misc = [k for k in run if k in bank]
                    for key in run:
                        kind, j = key[0], own(i, key)
                        if key in bank:
                            m = ps_m[:, bank[key], :]
                            for seq, k in last_use(i, in_misc, key, bank, ahead["tensor"], misc):
                                who, step = emptied[k[0]]
                                pe.wait_ge(*who.at(seq, step, *k[1:]))
                        if kind == "T":
                            k = key[1]
                            if k == 0:
                                pe.wait_ge(x_loaded, 16 * j[0] + 16 * j[1] + 16)
                            for t in range(TT):
                                last = nc.tensor.transpose(m[:, P * t:P * t + P], xc[:, t, P * k:P * k + P], ident[:, :])
                        elif kind == "Y":
                            n = key[1]
                            pe.wait_ge(weights_split, 1)
                            pe.wait_ge(*dve_s.at(j, "XL", KD - 1))
                            cols = slice(P * n, P * n + P)
                            last = sum_of_parts(nc, m, lambda k: wyh[:, k, cols], lambda k: wyl[:, k, cols], lambda k: xth[:, k, :], lambda k: xtl[:, k, :], KD)
                        elif kind == "V":
                            tok = slice(P * key[1], P * key[1] + P)
                            pe.wait_ge(weights_split, 2)
                            last = sum_of_parts(nc, m[:, 0:LAT], lambda k: xth[:, k, tok], lambda k: xtl[:, k, tok], lambda k: wvh[:, k, :], lambda k: wvl[:, k, :], KD)
                        elif kind == "S":
                            a, t, s = key[1:]
                            rows = slice(32 * s, 32 * s + 32)
                            if t == 0 and s == 0:
                                pe.wait_ge(*dve_s.at(j, "YS", QUADS + a))
                            pe.wait_ge(*dve_s.at(*two_before(j, "M", a, t, s)))
                            last = nc.tensor.matmul(ps_s[:, s % 2, :], stack[rows, QUADS + a, P * t:P * t + P], stack[rows, a, :], start=True, stop=True, tile_position=(32 * s, 0))
                        elif kind == "TM":
                            a = key[1]
                            pe.wait_ge(*dve_s.at(j, "NL", a))
                            for t in range(TT):
                                last = nc.tensor.transpose(m[:, P * t:P * t + P], mrow[:, a, t, :], ident[:, :])
                        elif kind == "ST":
                            a, t, s = key[1:]
                            rows = slice(32 * s, 32 * s + 32)
                            if t == 0 and s == 0:
                                pe.wait_ge(*dve_s.at(j, "QM", a))
                            pe.wait_ge(*act_s.at(*two_before(j, "X", a, t, s)))
                            last = nc.tensor.matmul(ps_t[:, s % 2, :], stack[rows, a, P * t:P * t + P], stack[rows, QUADS + a, :], start=True, stop=True, tile_position=(32 * s, 0))
                        elif kind == "A":
                            a, t = key[1:]
                            pe.wait_ge(*act_s.at(j, "X", a, t, 3))
                            if t == 0:
                                pe.wait_ge(*(act_s.at(j, "OT", a - 2) if a >= 2 else act_s.at(shift(j, -1), "OT", a + 2)))
                                if a == 0:
                                    pe.wait_ge(*dve_s.at(j, "VV"))
                            for s in range(4):
                                last = nc.tensor.matmul(ps_a[32 * s:32 * s + 32, a % 2, :], v[:, t, 4 * a + s, :], pt[:, a % 2, t, s, :], start=(t == 0), stop=(t == TT - 1), tile_position=(0, 32 * s))
                        elif kind == "BT":
                            t = key[1]
                            pe.wait_ge(*act_s.at(j, "OT", QUADS - 1))
                            for a in range(QUADS):
                                last = nc.tensor.transpose(m[:, P * a:P * a + P], ot[:, a, P * t:P * t + P], ident[:, :])
                        elif kind == "CT":
                            pe.wait_ge(*dve_s.at(j, "AO", TT - 1))
                            for t in range(TT):
                                last = nc.tensor.transpose(m[:, P * t:P * t + P], ao[:, t, :], ident[:, :])
                        elif kind == "MT":
                            c = key[1]
                            pe.wait_ge(weights_split, 4)
                            pe.wait_ge(*dve_s.at(j, "CL"))
                            cols = slice(P * c, P * c + P)
                            last = sum_of_parts(nc, m, lambda k: woh[:, k, cols], lambda k: wol[:, k, cols], lambda k: ch[:, :], lambda k: cl[:, :], 1)
                        elif kind == "MO":
                            tok = slice(P * key[1], P * key[1] + P)
                            last = sum_of_parts(nc, m[:, 0:D], lambda k: ch[:, tok], lambda k: cl[:, tok], lambda k: woh[:, k, :], lambda k: wol[:, k, :], 1)
                        elif kind == "RL":
                            pe.wait_ge(*dve_s.at(j, "ML", KD - 1))
                            for t in range(TT):
                                tok = slice(P * t, P * t + P)
                                last = sum_of_parts(nc, m[:, E_ * t:E_ * t + E_], lambda k: mth[:, k, tok], lambda k: mtl[:, k, tok], lambda k: wrh[:, k, :], lambda k: wrl[:, k, :], KD)
                        last.then_inc(pe_s.sem(key), 1)

                turns(pe, steps, ahead["tensor"], pe_o)

            flat = lambda x: x[:, :, :].rearrange("p k n -> p (k n)")
            splits = ((raw_y, wyh, wyl), (raw_v, wvh, wvl), (raw_r, wrh, wrl), (raw_o, woh, wol))

            @block.vector
            def _(dve):
                dve_s.start(dve)
                nc.vector.memset(v[:, :, :, :], 0.0).then_inc(zeroed, 1)
                nc.vector.memset(mrow[:, :, :, :], 0.0).then_inc(zeroed, 1)
                dve.wait_ge(zeroed, 2)
                nc.vector.memset(v[:, :, :, KPH:KPH + 1], 1.0).then_inc(zeroed, 1)
                dve.wait_ge(zeroed, 3)

                def split_weights(*which):
                    for n in which:
                        raw, hi, lo = splits[n]
                        dve.wait_ge(hi_split, n + 1)
                        nc.vector.tensor_tensor(flat(lo), flat(raw), flat(hi).bitcast(F32), ALU.subtract).then_inc(weights_split, 1)

                split_weights(0, 1)
                dve.wait_ge(small_in, 16 * 7)
                vv = nc.vector
                per_token = lambda s: s[:, :, :].broadcast_to([P, TT, E_])
                per_expert = lambda s: s[:, :].unsqueeze(1).broadcast_to([P, TT, E_])
                A3 = lambda s: s[:, :, :]
                route = {
                    "LM": lambda: vv.tensor_reduce(out=A3(lm), in_=A3(lg), axis=AX.X, op=ALU.max),
                    "LD": lambda: vv.tensor_tensor(A3(ex), A3(lg), per_token(lm), ALU.subtract),
                    "ES": lambda: vv.tensor_reduce(out=A3(es), in_=A3(pr), axis=AX.X, op=ALU.add),
                    "ER": lambda: vv.reciprocal(A3(er), A3(es)),
                    "PR": lambda: vv.tensor_tensor(A3(wt), A3(pr), per_token(er), ALU.mult),
                    "V1": lambda: vv.tensor_reduce(out=A3(v1), in_=A3(wt), axis=AX.X, op=ALU.max),
                    "EQ1": lambda: vv.tensor_tensor(A3(eq), A3(wt), per_token(v1), ALU.is_equal),
                    "KY1": lambda: vv.tensor_tensor(A3(key_), A3(eq), per_expert(rev), ALU.mult),
                    "K1": lambda: vv.tensor_reduce(out=A3(k1), in_=A3(key_), axis=AX.X, op=ALU.max),
                    "OH1": lambda: vv.tensor_tensor(A3(oh1), per_expert(rev), per_token(k1), ALU.is_equal),
                    "P2": lambda: vv.scalar_tensor_tensor(out=A3(p2), in0=A3(oh1), scalar=-2.0, in1=A3(wt), op0=ALU.mult, op1=ALU.add),
                    "V2": lambda: vv.tensor_reduce(out=A3(v2), in_=A3(p2), axis=AX.X, op=ALU.max),
                    "EQ2": lambda: vv.tensor_tensor(A3(eq), A3(p2), per_token(v2), ALU.is_equal),
                    "KY2": lambda: vv.tensor_tensor(A3(key_), A3(eq), per_expert(rev), ALU.mult),
                    "K2": lambda: vv.tensor_reduce(out=A3(k2), in_=A3(key_), axis=AX.X, op=ALU.max),
                    "OH2": lambda: vv.tensor_tensor(A3(oh2), per_expert(rev), per_token(k2), ALU.is_equal),
                    "OH": lambda: vv.tensor_tensor(A3(oh), A3(oh1), A3(oh2), ALU.add),
                    "TW": lambda: vv.scalar_tensor_tensor(out=A3(tw), in0=A3(v1), scalar=1e-8, in1=A3(v2), op0=ALU.add, op1=ALU.add),
                    "TR": lambda: vv.reciprocal(A3(tr), A3(tw)),
                    "WT": lambda: vv.tensor_tensor(A3(p2), A3(wt), A3(oh), ALU.mult),
                    "COMB": lambda: vv.tensor_tensor(A3(comb), A3(p2), per_token(tr), ALU.mult),
                }

                def steps(i, run):
                    for key in run:
                        kind, j = key[0], own(i, key)
                        if kind == "XH":
                            k = key[1]
                            dve.wait_ge(*pe_s.at(j, "T", k))
                            if k == 0:
                                dve.wait_ge(*pe_s.at(shift(j, -1), "V", TT - 1))
                                dve.wait_ge(*pe_s.at(shift(j, -1), "Y", 2 * QUADS - 1))
                            op = vv.tensor_copy(xth[:, k, :], ps_m[:, bank["T", k], :])
                        elif kind == "XL":
                            k = key[1]
                            dve.wait_ge(*dve_s.at(j, "XH", k))
                            op = vv.tensor_tensor(xtl[:, k, :], ps_m[:, bank["T", k], :], xth[:, k, :].bitcast(F32), ALU.subtract)
                        elif kind == "YS":
                            n = key[1]
                            p = units.index(n) % 2
                            dve.wait_ge(*pool_s.at(j, "YH", n))
                            dve.wait_ge(*pe_s.at(shift(j, -1), "ST", n % QUADS, TT - 1, 3))
                            op = vv.scalar_tensor_tensor(out=stack[:, n, :], in0=yh[:, p, :].bitcast(F32), scalar=minus_lo[:, n // QUADS:n // QUADS + 1],
                                                         in1=y[:, p, :], op0=ALU.mult, op1=ALU.add)
                        elif kind == "VB":
                            t = key[1]
                            dve.wait_ge(*pe_s.at(j, "V", t))
                            dve.wait_ge(*dve_s.at(shift(j, -1), "VV"))
                            op = vv.tensor_tensor(vn[:, t, :], ps_m[:, bank["V", t], 0:LAT], vb[:, :], ALU.add)
                        elif kind == "VV":
                            dve.wait_ge(*pe_s.at(shift(j, -1), "A", QUADS - 1, TT - 1))
                            dve.wait_ge(*dve_s.at(j, "VB", TT - 1))
                            op = vv.tensor_copy(v[:, :, :, 0:KPH], vn[:, :, :].rearrange("p t (h e) -> p t h e", e=KPH))
                        elif kind == "M":
                            a, t, s = key[1:]
                            dve.wait_ge(*pe_s.at(j, "S", a, t, s))
                            op = vv.tensor_reduce(out=mx[:, a, t, s:s + 1], in_=ps_s[:, s % 2, :], axis=AX.X, op=ALU.max, negate=True)
                        elif kind == "NH":
                            a = key[1]
                            dve.wait_ge(*dve_s.at(j, "M", a, TT - 1, 3))
                            dve.wait_ge(*pe_s.at(shift(j, -1), "TM", a))
                            op = vv.tensor_copy(mrow[:, a, :, MAX_ROW::32].bitcast(F32R), mx[:, a, :, :])
                        elif kind == "NL":
                            a = key[1]
                            dve.wait_ge(*dve_s.at(j, "NH", a))
                            op = vv.tensor_tensor(mrow[:, a, :, MAX_ROW + 1::32].bitcast(F32R), mx[:, a, :, :], mrow[:, a, :, MAX_ROW::32], ALU.subtract)
                        elif kind == "QM":
                            a = key[1]
                            dve.wait_ge(*pe_s.at(j, "TM", a))
                            op = vv.tensor_tensor(stack[:, QUADS + a, :], stack[:, QUADS + a, :].bitcast(F32), ps_m[:, bank["TM", a], :], ALU.add)
                        elif kind == "RI":
                            t = key[1]
                            dve.wait_ge(*pe_s.at(j, "BT", t))
                            op = vv.reciprocal(ri[:, t, :], ps_m[:, bank["BT", t], :].rearrange("p (h e) -> p h e", e=32)[:, :, KPH])
                        elif kind == "AO":
                            t = key[1]
                            dve.wait_ge(*dve_s.at(j, "RI", t))
                            if t == 0:
                                dve.wait_ge(*pe_s.at(shift(j, -1), "CT"))
                            op = vv.tensor_tensor(ao[:, t, :].rearrange("p (h e) -> p h e", e=KPH),
                                                  ps_m[:, bank["BT", t], :].rearrange("p (h e) -> p h e", e=32)[:, :, 0:KPH],
                                                  ri[:, t, :].unsqueeze(2).broadcast_to([P, MH, KPH]), ALU.mult)
                        elif kind == "CH":
                            dve.wait_ge(*pe_s.at(j, "CT"))
                            dve.wait_ge(*pe_s.at(shift(j, -1), "MO", TT - 1))
                            op = vv.tensor_copy(ch[:, :], ps_m[:, bank["CT",], :])
                        elif kind == "CL":
                            dve.wait_ge(*dve_s.at(j, "CH"))
                            op = vv.tensor_tensor(cl[:, :], ps_m[:, bank["CT",], :], ch[:, :].bitcast(F32), ALU.subtract)
                        elif kind == "MB":
                            c = key[1]
                            dve.wait_ge(*pe_s.at(j, "MT", c))
                            op = vv.tensor_scalar(mt[:, c, :], ps_m[:, bank["MT", c], :], ocol[:, c:c + 1], None, ALU.add)
                        elif kind == "MH":
                            c = key[1]
                            dve.wait_ge(*dve_s.at(j, "MB", c))
                            if c == 0:
                                dve.wait_ge(*pe_s.at(shift(j, -1), "RL"))
                            op = vv.tensor_copy(mth[:, c, :], mt[:, c, :])
                        elif kind == "ML":
                            c = key[1]
                            dve.wait_ge(*dve_s.at(j, "MH", c))
                            op = vv.tensor_tensor(mtl[:, c, :], mt[:, c, :], mth[:, c, :].bitcast(F32), ALU.subtract)
                        elif kind == "MO":
                            t = key[1]
                            dve.wait_ge(*pe_s.at(j, "MO", t))
                            dve.wait_ge(stored[t % 2], 32 * j[0] + (32 * j[1] + 16 * (t // 2) + 32))
                            op = vv.tensor_tensor(mo[:, t % 2, :], ps_m[:, bank["MO", t], 0:D], orow[:, :], ALU.add)
                        elif kind == "LG":
                            dve.wait_ge(*pe_s.at(j, "RL"))
                            op = vv.tensor_tensor(A3(lg), ps_m[:, bank["RL",], 0:TT * E_].rearrange("p (t e) -> p t e", e=E_), per_expert(rrow), ALU.add)
                        else:
                            if kind == "LD":
                                dve.wait_ge(*act_s.at(shift(j, -1), "EX"))
                            if kind == "ES":
                                dve.wait_ge(*act_s.at(j, "EX"))
                            if kind == "COMB":
                                dve.wait_ge(comb_stored, 16 * j[0] + (16 * j[1] + 16))
                            order = ROUTE + ROUTE2
                            dve.wait_ge(*dve_s.at(j, order[order.index(kind) - 1]))
                            op = route[kind]()
                        op.then_inc(dve_s.sem(key), 1)

                turns(dve, steps, ahead["vector"], dve_o, lambda: split_weights(2, 3))

            @block.scalar
            def _(act):
                act_s.start(act)

                def hi_weights(*which):
                    for n in which:
                        act.wait_ge(weights_in[n], 16)
                        nc.scalar.copy(flat(splits[n][1]), flat(splits[n][0])).then_inc(hi_split, 1)

                hi_weights(0, 1)
                act.wait_ge(small_in, 16 * 7)

                def steps(i, run):
                    for key in run:
                        kind, j = key[0], own(i, key)
                        if kind == "YB":
                            n = key[1]
                            p = units.index(n)
                            act.wait_ge(*pe_s.at(j, "Y", n))
                            act.wait_ge(*(dve_s.at(j, "YS", units[p - 2]) if p >= 2 else dve_s.at(shift(j, -1), "YS", units[p - 2])))
                            op = nc.scalar.activation(y[:, p % 2, :], ps_m[:, bank["Y", n], :], ACT.Identity, bias=yb[:, n:n + 1], scale=1.0)
                        elif kind == "X":
                            a, t, s = key[1:]
                            act.wait_ge(*pe_s.at(j, "ST", a, t, s))
                            if s == 0:
                                act.wait_ge(*(pe_s.at(j, "A", a - 2, t) if a >= 2 else pe_s.at(shift(j, -1), "A", a + 2, t)))
                            op = nc.scalar.activation(pt[:, a % 2, t, s, :], ps_t[:, s % 2, :], ACT.Exp, scale=KPH ** -0.5)
                        elif kind == "OT":
                            a = key[1]
                            act.wait_ge(*pe_s.at(j, "A", a, TT - 1))
                            act.wait_ge(*pe_s.at(shift(j, -1), "BT", TT - 1))
                            op = nc.scalar.copy(ot[:, a, :], ps_a[:, a % 2, :])
                        elif kind == "EX":
                            act.wait_ge(*dve_s.at(j, "LD"))
                            op = nc.scalar.activation(pr[:, :, :].rearrange("p t e -> p (t e)"), ex[:, :, :].rearrange("p t e -> p (t e)"), ACT.Exp)
                        op.then_inc(act_s.sem(key), 1)

                turns(act, steps, ahead["scalar"], act_o, lambda: hi_weights(2, 3))

            @block.gpsimd
            def _(pool):
                pool_s.start(pool)

                def steps(i, run):
                    for key in run:
                        kind, n = key
                        j, p = own(i, key), units.index(n) % 2
                        hold(pool, *act_s.at(j, "YB", n))
                        x = units[units.index(n) - 2]
                        hold(pool, *dve_s.at(j if units.index(n) >= 2 else shift(j, -1), "YS", x))
                        op = nc.gpsimd.tensor_copy(yh[:, p, :], y[:, p, :])
                        op.then_inc(pool_s.sem(key), 1)

                turns(pool, steps, ahead["gpsimd"], pool_o)


def dense_experts(nc, const, x_in, m_in, comb_in, w1, b1, w2, b2, x_out, name):
    F = w1.shape[2]
    FT = F // P
    ctx = ExitStack()
    with ctx:
        sb = lambda n, s, dt=F32: ctx.enter_context(nc.sbuf_tensor(f"{name}_{n}", s, dt))
        sem = lambda n: ctx.enter_context(nc.semaphore(f"{name}_{n}"))
        ident = const["ident"]
        w1h, w1l = (sb(n, [P, E_, KD, F], F32R) for n in ("w1h", "w1l"))
        w2h, w2l = (sb(n, [P, E_, FT, D], F32R) for n in ("w2h", "w2l"))
        RAW = 2
        b1c = sb("b1c", [P, E_, FT])
        b2r = sb("b2r", [E_, D])
        raw = sb("raw", [P, RAW, KD * F])
        xc, mc, xb, acc = (sb(n, [P, TT, D]) for n in ("xc", "mc", "xb", "acc"))
        zn = sb("zn", [P, TT, D])
        next_comb = sb("next_comb", [P, TT, E_])
        comb = sb("comb", [P, TT, E_])
        combt = sb("combt", [E_, SEQ])
        xth, xtl = (sb(n, [P, KD, SEQ], F32R) for n in ("xth", "xtl"))
        g = sb("g", [P, 2, SEQ])
        gh, gl = (sb(n, [P, 2, FT, SEQ], F32R) for n in ("gh", "gl"))
        st6, mv, vare, rstd = sb("st6", [P, TT, 6]), sb("mv", [P, TT, 2]), sb("vare", [P, TT, 1]), sb("rstd", [P, TT, 1])
        ps = ctx.enter_context(nc.psum_tensor(f"{name}_ps", [P, 8, SEQ], F32))
        small_in, staged, hi_split, lo_split = sem("small_in"), [sem(f"staged{k}") for k in range(RAW)], sem("hi_split"), sem("lo_split")
        m_loaded, x_loaded, stored = sem("m_loaded"), sem("x_loaded"), sem("stored")
        hold = gated_hold(sem("held"))

        pe_o, dve_o, act_o = [], [("COMB",), ("XB",)], []
        for e in [*range(1, E_), 0]:
            if e == 0:
                pe_o += [("C", n) for n in range(2)] + [("Z", t) for t in range(TT)]
                dve_o += [("CC", n) for n in range(2)] + [("ZA", t) for t in range(TT)]
            pe_o += [("H", e, m) for m in range(FT)]
            act_o += [("G", e, m) for m in range(FT)]
            dve_o += [(n, e, m) for m in range(FT) for n in ("GH", "GL")]
            if e == E_ - 1:
                pe_o += [("T", k) for k in range(KD)]
                dve_o += [(n, k) for k in range(KD) for n in ("XH", "XL")]
            pe_o += [("Y", (e - 1) % E_, t) for t in range(TT)]
            dve_o += [("AC", (e - 1) % E_, t) for t in range(TT)]
        dve_o += [(n, t) for n in ("F", "B", "S", "N") for t in range(TT)]
        pool_o = [("EPS",), ("RSTD",)]
        is_ahead = lambda k: k[0] in ("T", "XH", "XL", "C", "CC", "Z", "ZA") or (k[0] in ("H", "G", "GH", "GL") and k[1] == 0)
        S, ahead = {}, {}
        for eng_name, o in (("tensor", pe_o), ("vector", dve_o), ("scalar", act_o), ("gpsimd", pool_o)):
            ahead[eng_name] = [k for k in o if is_ahead(k)]
            S[eng_name] = Steps(sem(f"{eng_name}_ahead"), sem(f"{eng_name}_main"), ahead[eng_name], [k for k in o if not is_ahead(k)])
        pe_s, dve_s, act_s, pool_s = (S[n] for n in ("tensor", "vector", "scalar", "gpsimd"))
        own = lambda i, key: (i[0], i[1] + 1) if is_ahead(key) else i
        BANKS = 8
        bank = {k: n % BANKS for n, k in enumerate(pe_o)}
        emptied = {"T": (dve_s, "XL"), "C": (dve_s, "CC"), "Z": (dve_s, "ZA"), "H": (act_s, "G"), "Y": (dve_s, "AC")}
        pieces = [(e, n) for e in range(E_) for n in range(2)]

        def piece(e, n):
            hi, lo = ((w1h, w1l), (w2h, w2l))[n]
            f = lambda x: x[:, e, :, :].rearrange("p k n -> p (k n)")
            return raw[:, (2 * e + n) % RAW, :], f(hi), f(lo)

        with nc.Block() as block:

            @block.sync
            def _(sp):
                sp.sem_inc(stored, 64)
                tok = "o (t p) d -> p (o t) d"

                def load(i, index):
                    hold(sp, *pe_s.at(shift(i, -1), "T", KD - 1))
                    sp.dma_start(mc[:, :, :], m_in[bass.ds(index, 1), :, :].rearrange(tok, p=P)).then_inc(m_loaded, 16)
                    hold(sp, *dve_s.at(shift(i, -1), "COMB"))
                    hold(sp, *dve_s.at(shift(i, -1), "XB"))
                    hold(sp, *pe_s.at(shift(i, -1), "C", 1))
                    sp.dma_start(next_comb[:, :, :], comb_in[bass.ds(index, 1), :, :].rearrange(tok, p=P)).then_inc(x_loaded, 16)
                    sp.dma_start(xc[:, :, :], x_in[bass.ds(index, 1), :, :].rearrange(tok, p=P)).then_inc(x_loaded, 16)

                def store(i, index):
                    for t in range(TT):
                        hold(sp, *dve_s.at(i, "N", t))
                        sp.dma_start(x_out[bass.ds(index, 1), P * t:P * t + P, :].rearrange("o p d -> p (o d)"), acc[:, t, :]).then_inc(stored, 16)

                load((0, 0), 0)
                sp.dma_start(b1c[:, :, :], b1).then_inc(small_in, 16)
                sp.dma_start(b2r[:, :], b2).then_inc(small_in, 16)
                for c, (e, n) in enumerate(pieces):
                    if c >= RAW:
                        hold(sp, lo_split, c - RAW + 1)
                    src = (w1, w2)[n][e].rearrange("(k p) n -> p k n", p=P)
                    sp.dma_start(piece(e, n)[0].rearrange("p (k n) -> p k n", n=src.shape[2]), src).then_inc(staged[c % RAW], 16)
                with sp.Fori(0, BATCH - 1) as i:
                    load((i, 1), i + 1)
                    store((i, 0), i)
                store((BATCH - 1, 0), BATCH - 1)
                hold(sp, stored, 64 * BATCH + 64)

            @block.tensor
            def _(pe):
                pe_s.start(pe)

                def steps(i, run):
                    for key in run:
                        kind, j = key[0], own(i, key)
                        m = ps[:, bank[key], :]
                        for seq, k in last_use(i, run, key, bank, ahead["tensor"], pe_o):
                            who, step = emptied[k[0]]
                            pe.wait_ge(*who.at(seq, step, *k[1:]))
                        if kind == "T":
                            if key[1] == 0:
                                pe.wait_ge(m_loaded, 16 * j[0] + (16 * j[1] + 16))
                            for t in range(TT):
                                last = nc.tensor.transpose(m[:, P * t:P * t + P], mc[:, t, P * key[1]:P * key[1] + P], ident[:, :])
                        elif kind == "C":
                            pe.wait_ge(x_loaded, 32 * j[0] + (32 * j[1] + 32))
                            for t in (2 * key[1], 2 * key[1] + 1):
                                last = nc.tensor.transpose(m[0:E_, P * (t % 2):P * (t % 2) + P], next_comb[:, t, :], ident[:, :])
                        elif kind == "Z":
                            t = key[1]
                            if t == 0:
                                pe.wait_ge(*dve_s.at(j, "CC", 1))
                                pe.wait_ge(small_in, 32)
                            last = nc.tensor.matmul(m[:, 0:D], combt[:, P * t:P * t + P], b2r[:, :], start=True, stop=True)
                        elif kind == "H":
                            e, f = key[1:]
                            if f == 0:
                                pe.wait_ge(lo_split, 2 * e + 1)
                                if e == 0:
                                    pe.wait_ge(*dve_s.at(j, "XL", KD - 1))
                            cols = slice(P * f, P * f + P)
                            last = sum_of_parts(nc, m, lambda k: w1h[:, e, k, cols], lambda k: w1l[:, e, k, cols], lambda k: xth[:, k, :], lambda k: xtl[:, k, :], KD)
                        elif kind == "Y":
                            e, t = key[1:]
                            tok = slice(P * t, P * t + P)
                            if t == 0:
                                pe.wait_ge(lo_split, 2 * e + 2)
                                pe.wait_ge(*dve_s.at(j, "GL", e, FT - 1))
                            last = sum_of_parts(nc, m[:, 0:D], lambda k: gh[:, e % 2, k, tok], lambda k: gl[:, e % 2, k, tok], lambda k: w2h[:, e, k, :], lambda k: w2l[:, e, k, :], FT)
                        last.then_inc(pe_s.sem(key), 1)

                turns(pe, steps, ahead["tensor"], pe_o)

            @block.vector
            def _(dve):
                dve_s.start(dve)

                def steps(i, run):
                    for key in run:
                        kind, j = key[0], own(i, key)
                        t = k = key[-1]
                        if kind == "XH":
                            dve.wait_ge(*pe_s.at(j, "T", k))
                            if k == 0:
                                dve.wait_ge(*pe_s.at(shift(j, -1), "H", E_ - 1, FT - 1))
                            op = nc.vector.tensor_copy(xth[:, k, :], ps[:, bank["T", k], :])
                        elif kind == "XL":
                            dve.wait_ge(*dve_s.at(j, "XH", k))
                            op = nc.vector.tensor_tensor(xtl[:, k, :], ps[:, bank["T", k], :], xth[:, k, :].bitcast(F32), ALU.subtract)
                        elif kind == "CC":
                            dve.wait_ge(*pe_s.at(j, "C", k))
                            dve.wait_ge(*pe_s.at(shift(j, -1), "Z", TT - 1))
                            op = nc.vector.tensor_copy(combt[:, 2 * P * k:2 * P * k + 2 * P], ps[0:E_, bank["C", k], 0:2 * P])
                        elif kind == "ZA":
                            dve.wait_ge(*pe_s.at(j, "Z", t))
                            dve.wait_ge(*dve_s.at(shift(j, -1), "AC", 0, t))
                            op = nc.vector.tensor_copy(zn[:, t, :], ps[:, bank["Z", t], 0:D])
                        elif kind == "COMB":
                            dve.wait_ge(x_loaded, 32 * j[0] + (32 * j[1] + 32))
                            dve.wait_ge(*dve_s.at(shift(j, -1), "AC", E_ - 1, TT - 1))
                            op = nc.vector.tensor_copy(comb[:, :, :], next_comb[:, :, :])
                        elif kind == "XB":
                            dve.wait_ge(*dve_s.at(shift(j, -1), "N", TT - 1))
                            op = nc.vector.tensor_scalar(xb[:, :, :], xc[:, :, :], 2.0, None, ALU.mult)
                        elif kind == "GH":
                            e, m = key[1:]
                            dve.wait_ge(*act_s.at(j, "G", e, m))
                            if m == 0:
                                dve.wait_ge(*(pe_s.at(j, "Y", e - 2, TT - 1) if e >= 2 else pe_s.at(shift(j, -1), "Y", e + E_ - 2, TT - 1)))
                            op = nc.vector.tensor_copy(gh[:, e % 2, m, :], g[:, m % 2, :])
                        elif kind == "GL":
                            e, m = key[1:]
                            dve.wait_ge(*dve_s.at(j, "GH", e, m))
                            op = nc.vector.tensor_tensor(gl[:, e % 2, m, :], g[:, m % 2, :], gh[:, e % 2, m, :].bitcast(F32), ALU.subtract)
                        elif kind == "AC":
                            e = key[1]
                            dve.wait_ge(*pe_s.at(j, "Y", e, t))
                            if e == 0:
                                dve.wait_ge(*dve_s.at(j, "ZA", t))
                                dve.wait_ge(*dve_s.at(j, "COMB"))
                                if t == 0:
                                    dve.wait_ge(stored, 64 * j[0] + (64 * j[1] + 64))
                            else:
                                dve.wait_ge(*dve_s.at(j, "AC", e - 1, t))
                            op = nc.vector.scalar_tensor_tensor(out=acc[:, t, :], in0=ps[:, bank[("Y", e, t)], 0:D], scalar=comb[:, t, e:e + 1],
                                                                in1=(acc if e else zn)[:, t, :], op0=ALU.mult, op1=ALU.add)
                        elif kind == "F":
                            dve.wait_ge(*dve_s.at(j, "AC", E_ - 1, t))
                            dve.wait_ge(*dve_s.at(j, "XB"))
                            op = nc.vector.scalar_tensor_tensor(out=xb[:, t, :], in0=acc[:, t, :], scalar=0.3, in1=xb[:, t, :], op0=ALU.mult, op1=ALU.add)
                        elif kind == "B":
                            dve.wait_ge(*dve_s.at(j, "F", t))
                            op = nc.vector.bn_stats(st6[:, t, :], xb[:, t, :])
                        elif kind == "S":
                            hold(dve, *dve_s.at(j, "B", t))
                            op = nc.vector.bn_aggr(mv[:, t, :], st6[:, t, :])
                        elif kind == "N":
                            dve.wait_ge(*pool_s.at(j, "RSTD"))
                            op = nc.vector.tensor_scalar(acc[:, t, :], xb[:, t, :], mv[:, t, 0:1], rstd[:, t, :], ALU.subtract, ALU.mult)
                        op.then_inc(dve_s.sem(key), 1)

                turns(dve, steps, ahead["vector"], dve_o)

            @block.scalar
            def _(act):
                act_s.start(act)
                act.wait_ge(small_in, 32)

                def steps(i, run):
                    for key in run:
                        j = own(i, key)
                        _, e, m = key
                        act.wait_ge(*pe_s.at(j, "H", e, m))
                        n = FT * e + m - 2
                        act.wait_ge(*dve_s.at(j if n >= 0 else shift(j, -1), "GL", n // FT % E_, n % FT))
                        nc.scalar.activation(g[:, m % 2, :], ps[:, bank["H", e, m], :], ACT.Gelu, bias=b1c[:, e, m:m + 1], scale=1.0).then_inc(act_s.sem(key), 1)

                turns(act, steps, ahead["scalar"], act_o)

            @block.gpsimd
            def _(pool):
                pool_s.start(pool)
                for c, (e, n) in enumerate(pieces):
                    src, hi, lo = piece(e, n)
                    hold(pool, staged[c % RAW], 16 * (c // RAW) + 16)
                    nc.gpsimd.tensor_copy(hi, src).then_inc(hi_split, 1)
                    hold(pool, hi_split, c + 1)
                    nc.gpsimd.tensor_tensor(lo, src, hi.bitcast(F32), ALU.subtract).then_inc(lo_split, 1)

                def steps(i, run):
                    for key in run:
                        j = own(i, key)
                        if key == ("EPS",):
                            hold(pool, *dve_s.at(j, "S", TT - 1))
                            op = nc.gpsimd.tensor_scalar(vare[:, :, :], mv[:, :, 1:2], EPS, None, ALU.add)
                        else:
                            hold(pool, *pool_s.at(j, "EPS"))
                            hold(pool, *dve_s.at(shift(j, -1), "N", TT - 1))
                            op = nc.gpsimd.tensor_tensor(rstd[:, :, :], vare[:, :, :], const["minus_half"][:, :].unsqueeze(1).broadcast_to([P, TT, 1]), ALU.pow)
                        op.then_inc(pool_s.sem(key), 1)

                turns(pool, steps, ahead["gpsimd"], pool_o)



def constants(nc, ctx):
    ident = ctx.enter_context(nc.sbuf_tensor("ident", [P, P], F32))
    minus_half = ctx.enter_context(nc.sbuf_tensor("minus_half", [P, 1], F32))
    ready = ctx.enter_context(nc.semaphore("constants_ready"))
    with nc.Block() as block:

        @block.gpsimd
        def _(pool):
            nc.gpsimd.memset(minus_half[:, :], -0.5)
            nc.gpsimd.memset(ident[:, :], 0.0).then_inc(ready, 1)
            pool.wait_ge(ready, 1)
            nc.gpsimd.affine_select(out=ident[:, :], in_=ident[:, :], compare_op=ALU.not_equal, fill=1.0,
                                    base=0, pattern=[[-1, P]], channel_multiplier=1).then_inc(ready, 1)
            pool.wait_ge(ready, 2)
    return {"ident": ident, "minus_half": minus_half}


def build(nc, a, out):
    ctx = ExitStack()
    with ctx:
        const = constants(nc, ctx)
        x1, x2, x3 = (nc.dram_tensor(n, [BATCH, SEQ, D], F32, kind="Internal").ap() for n in ("x1", "x2", "x3"))
        mla = {k[7:]: v for k, v in a.items() if k.startswith("L1_ffn_")}
        m4 = nc.dram_tensor("m4", [BATCH, SEQ, D], F32, kind="Internal").ap()
        c4 = nc.dram_tensor("c4", [BATCH, SEQ, E_], F32, kind="Internal").ap()
        attention(nc, const, a["L0_attn_x"], x1, a["L0_attn_Wq"], a["L0_attn_Wkv"], a["L0_attn_Wo"], a["L0_attn_bo"], a["rope0"], None, True, "soft")
        quantized_ffn(nc, const, x1, x2, a["gamma_beta"], a["L0_ffn_fc1_q"], a["L0_ffn_fc1_scales"], a["L0_ffn_fc1_bias"], a["L0_ffn_fc2_q"], a["L0_ffn_fc2_scales"], a["L0_ffn_fc2_bias"], "ffn")
        attention(nc, const, x2, x3, a["L1_attn_Wq"], a["L1_attn_Wkv"], a["L1_attn_Wo"], None, a["rope1"], a["decay"], False, "decay")
        latent_attention(nc, const, x3, m4, c4, mla, "mla")
        dense_experts(nc, const, x3, m4, c4, mla["w1"], mla["b1"], mla["w2"], mla["b2"], out, "moe")


def tables():
    f = np.float32
    inv = (f(1.0) / np.power(f(10000.0), np.arange(0, HD, 2, dtype=f) / f(HD))).astype(f)
    ang = (np.arange(SEQ, dtype=f)[:, None] * inv[None, :]).astype(f).T
    inv64 = 1.0 / 10000.0 ** (np.arange(0, HD, 2, dtype=np.float64) / HD)
    ang64 = np.outer(np.arange(SEQ, dtype=np.float64), inv64).T
    def pack(c, s):
        rows = np.stack([np.concatenate([c, c]), np.concatenate([s, -s])]).astype(f)
        return rows.reshape(2, HD, TT, P).transpose(3, 2, 0, 1)
    slopes = np.array([2.0 ** (-8.0 / HEADS * (i + 1)) for i in range(HEADS)], f).astype(np.float64)
    dist = np.arange(SEQ)[None, :] - np.arange(P)[:, None]
    decay = np.where(dist[:, None, :] >= 0, np.exp(-slopes[None, :, None] * np.maximum(dist, 0)[:, None, :]), 0.0).astype(f)
    return {"rope0": pack(np.cos(ang), np.sin(ang)), "rope1": pack(np.cos(ang64), np.sin(ang64)), "decay": np.ascontiguousarray(decay)}


def kernel(**inputs):
    import concourse.bacc as _bacc
    from concourse.bass_utils import run_bass_kernel_spmd as _run

    nc = _bacc.Bacc("TRN2", target_bir_lowering=False, num_devices=1)
    host = {k: np.asarray(v) for k, v in inputs.items()}
    host["L1_attn_Wq"] = host["L1_attn_Wq"].T
    host["L1_attn_Wkv"] = np.concatenate([host.pop("L1_attn_Wk").T, host.pop("L1_attn_Wv").T], axis=1)
    host["L1_attn_Wo"] = host["L1_attn_Wo"].T
    host["gamma_beta"] = np.stack([host["L0_ffn_ln_gamma"], host["L0_ffn_ln_beta"]]).reshape(2, KD, P).transpose(2, 0, 1)
    host["L0_ffn_fc1_bias"] = host["L0_ffn_fc1_bias"].reshape(-1, P).T
    qw, kw = host.pop("L1_ffn_q_w"), host.pop("L1_ffn_k_w")
    qb, kb = host.pop("L1_ffn_q_b"), host.pop("L1_ffn_k_b")
    def stacked(m, width, ones=False):
        m = m.reshape(m.shape[0], MH, 1, width)[:, :, :, :KPH]
        out = np.zeros((m.shape[0], MH, VAR, KPH), m.dtype)
        out[:, :, 0:VAR - 1] = m
        if ones:
            out[:, :, VAR - 1, 0:2] = 1
        return out.reshape(m.shape[0], MH * VAR * KPH)
    host["L1_ffn_stacks"] = np.concatenate([stacked(kw, KPH), stacked(qw, D // MH)], axis=1)
    host["L1_ffn_stack_b"] = np.concatenate([stacked(kb[None], KPH, True), stacked(qb[None], D // MH)], axis=1).reshape(2 * QUADS, P).T
    lo = np.array([[0, 0, -1, 0], [0, -1, 0, 0]], np.float32)
    host["L1_ffn_minus_lo"] = np.tile(np.repeat(lo, KPH, axis=1), (1, P // (VAR * KPH))).T
    host["L1_ffn_o_b_cols"] = host["L1_ffn_o_b"].reshape(KD, P).T
    host["L1_ffn_rev"] = (E_ - np.arange(E_)).astype(np.float32)
    host["L1_ffn_b1"] = host["L1_ffn_b1"].reshape(E_, -1, P).transpose(2, 0, 1)
    host.update(tables())
    arrays, aps = {}, {}
    for k, v in host.items():
        arrays["in_" + k] = np.ascontiguousarray(v)
        aps[k] = nc.dram_tensor("in_" + k, arrays["in_" + k].shape, mybir.dt.from_np(arrays["in_" + k].dtype), kind="ExternalInput").ap()
    out = nc.dram_tensor("out_x", (BATCH, SEQ, D), F32, kind="ExternalOutput").ap()
    build(nc, aps, out)
    r = _run(nc, [arrays], core_ids=[0])
    return r.results[0]["out_x"]
```
